# Optimizing a Trainium2 kernel written in Bass

```python
import numpy as np
import jax
import jax.numpy as jnp

def _softmax(x, axis=-1):
    return jax.nn.softmax(x, axis=axis)

def _gelu(x):
    return jax.nn.gelu(x, approximate=True)

def _silu(x):
    return jax.nn.silu(x)

def _sigmoid(x):
    return jax.nn.sigmoid(x)

def _layernorm(x, axis=-1, eps=1e-05):
    m = jnp.mean(x, axis=axis, keepdims=True)
    v = jnp.var(x, axis=axis, keepdims=True)
    return (x - m) / jnp.sqrt(v + eps)

def _scatter_add(tgt, idx, src, axis=0):
    return tgt.at[idx].add(src)

def _segment_sum(src, seg, n):
    return jax.ops.segment_sum(src, seg, n)
kernel_name = 'mk_early_fusion_d1_tok_img2048_r4_7557e0'

def setup_inputs(seed: int=0):
    np.random.seed(seed)
    _w = jnp.asarray

    def _rec_inputs():
        import jax
        import jax.numpy as jnp
        _rk = jax.random.key(seed)
        x = -0.0043416 + 0.998921 * jax.random.normal(jax.random.fold_in(_rk, 1), (64, 64, 64, 2), jnp.float32)
        txt = 0.000243251 + 0.0342838 * jax.random.normal(jax.random.fold_in(_rk, 2), (64, 77, 512), jnp.float32)
        return (x, txt)
    x, txt = _rec_inputs()

    def _L0_tok_setup():
        import jax, jax.numpy as jnp
        import numpy as np
        H, N, CH = (64, 64, 1)

        def _r2c(x):
            return x[..., 0] + 1j * x[..., 1]

        def _bilinear(dt, Ac, Bc):
            n = Ac.shape[-1]
            I = jnp.eye(n, dtype=Ac.dtype)
            half = (dt.astype(Ac.real.dtype) / 2)[:, None]
            A_back = I - half * Ac
            A_fwd = I + half * Ac
            dB = dt.astype(Ac.dtype) * jnp.linalg.solve(A_back, Bc[..., None])[..., 0]
            dA = jnp.linalg.solve(A_back, A_fwd)
            return (dA, dB)

        def _krylov(L, dA, dB):
            x = dB[..., None]
            A_ = dA
            while x.shape[-1] < L:
                x = jnp.concatenate([x, jnp.einsum('hnm,hml->hnl', A_, x)], axis=-1)
                A_ = A_ @ A_
            return x[..., :L]
        key = jax.random.key(seed)
        kA, kB, kC, kdt = jax.random.split(key, 4)
        M = jax.random.normal(kA, (H, N, N, 2), dtype=jnp.float32) / np.float32(np.sqrt(N))
        Mc = _r2c(M)
        Ac = 0.5 * (Mc - jnp.conjugate(jnp.swapaxes(Mc, -1, -2))) - 0.5 * jnp.eye(N, dtype=Mc.dtype)
        A = jnp.stack([Ac.real, Ac.imag], axis=-1)
        B = jax.random.normal(kB, (H, N, 2), dtype=jnp.float32)
        C = jax.random.normal(kC, (CH, H, N, 2), dtype=jnp.float32)
        log_dt = jax.random.uniform(kdt, (H, 1), dtype=jnp.float32, minval=np.float32(np.log(0.001)), maxval=np.float32(np.log(0.1)))
        return {'A': A, 'B': B, 'C': C, 'log_dt': log_dt, 'L': 512}
    _L0_tok_all = _L0_tok_setup()
    _L0_tok_in = {k: v for k, v in _L0_tok_all.items() if k in ('A', 'B', 'log_dt')}
    del _L0_tok_all

    def _L0_attn_setup():
        import math
        import jax, jax.numpy as jnp
        import numpy as np
        MODEL_DIM = 512
        N_HEADS = 32
        N_GROUPS = 8
        R = N_HEADS // N_GROUPS
        HEAD_DIM = MODEL_DIM // N_HEADS
        KV_DIM = MODEL_DIM // R
        B, S = (1, 512)
        key = jax.random.key(seed)
        k1, k2, k3 = jax.random.split(key, 3)
        scale = 0.02
        return {'x': jax.random.normal(k1, (B, S, MODEL_DIM), dtype=jnp.float32), 'w_qkv': jax.random.normal(k2, (MODEL_DIM + 2 * KV_DIM, MODEL_DIM), dtype=jnp.float32) * scale, 'b_qkv': jnp.zeros((MODEL_DIM + 2 * KV_DIM,), dtype=jnp.float32), 'w_out': jax.random.normal(k3, (MODEL_DIM, MODEL_DIM), dtype=jnp.float32) * scale, 'b_out': jnp.zeros((MODEL_DIM,), dtype=jnp.float32)}
    _L0_attn_all = _L0_attn_setup()
    _L0_attn_in = {k: v for k, v in _L0_attn_all.items() if k in ('w_qkv', 'b_qkv', 'w_out', 'b_out')}
    del _L0_attn_all

    def _L0_ffn_setup():
        import jax, jax.numpy as jnp
        import numpy as np
        B, S, D_IN, D_OUT = (4, 512, 512, 512)
        EPS = 1e-10
        key = jax.random.key(seed)
        kx, kw, kb = jax.random.split(key, 3)
        x = jax.random.normal(kx, (B, S, D_IN), dtype=jnp.float32)
        weight = jax.random.normal(kw, (D_OUT, D_IN), dtype=jnp.float32) * 0.02
        bias = jax.random.normal(kb, (D_OUT,), dtype=jnp.float32) * 0.02
        return {'x': x, 'weight': weight, 'bias': bias}
    _L0_ffn_all = _L0_ffn_setup()
    _L0_ffn_in = {k: v for k, v in _L0_ffn_all.items() if k in ('weight', 'bias')}
    del _L0_ffn_all
    return {'x': x, 'txt': txt, 'L0_tok_A': _L0_tok_in['A'], 'L0_tok_B': _L0_tok_in['B'], 'L0_tok_log_dt': _L0_tok_in['log_dt'], 'L0_attn_w_qkv': _L0_attn_in['w_qkv'], 'L0_attn_b_qkv': _L0_attn_in['b_qkv'], 'L0_attn_w_out': _L0_attn_in['w_out'], 'L0_attn_b_out': _L0_attn_in['b_out'], 'L0_ffn_weight': _L0_ffn_in['weight'], 'L0_ffn_bias': _L0_ffn_in['bias']}

def reference(x, txt, L0_tok_A, L0_tok_B, L0_tok_log_dt, L0_attn_w_qkv, L0_attn_b_qkv, L0_attn_w_out, L0_attn_b_out, L0_ffn_weight, L0_ffn_bias):
    import jax
    import jax.numpy as jnp

    def _L0_tok_ref(A, B, C, log_dt, L):
        import jax, jax.numpy as jnp
        import numpy as np
        H, N, CH = (64, 64, 1)

        def _r2c(x):
            return x[..., 0] + 1j * x[..., 1]

        def _bilinear(dt, Ac, Bc):
            n = Ac.shape[-1]
            I = jnp.eye(n, dtype=Ac.dtype)
            half = (dt.astype(Ac.real.dtype) / 2)[:, None]
            A_back = I - half * Ac
            A_fwd = I + half * Ac
            dB = dt.astype(Ac.dtype) * jnp.linalg.solve(A_back, Bc[..., None])[..., 0]
            dA = jnp.linalg.solve(A_back, A_fwd)
            return (dA, dB)

        def _krylov(L, dA, dB):
            x = dB[..., None]
            A_ = dA
            while x.shape[-1] < L:
                x = jnp.concatenate([x, jnp.einsum('hnm,hml->hnl', A_, x)], axis=-1)
                A_ = A_ @ A_
            return x[..., :L]
        Ac, Bc, Cc = (_r2c(A), _r2c(B), _r2c(C))
        dt = jnp.exp(log_dt)
        dA, dB = _bilinear(dt, Ac, Bc)
        x = _krylov(L, dA, dB)
        k = jnp.einsum('chn,hnl->chl', Cc, x).real.astype(jnp.float32)
        return k

    def _L0_attn_ref(x, w_qkv, b_qkv, w_out, b_out):
        import math
        import jax, jax.numpy as jnp
        import numpy as np
        MODEL_DIM = 512
        N_HEADS = 32
        N_GROUPS = 8
        R = N_HEADS // N_GROUPS
        HEAD_DIM = MODEL_DIM // N_HEADS
        KV_DIM = MODEL_DIM // R
        B, S = (1, 512)
        Bx, Sx, _ = x.shape
        fused = x @ w_qkv.T + b_qkv
        q = fused[..., :MODEL_DIM]
        k = fused[..., MODEL_DIM:MODEL_DIM + KV_DIM]
        v = fused[..., MODEL_DIM + KV_DIM:]
        q = q.reshape(Bx, Sx, N_GROUPS, R, HEAD_DIM).transpose(0, 2, 3, 1, 4)
        k = k.reshape(Bx, Sx, N_GROUPS, HEAD_DIM).transpose(0, 2, 1, 3)
        v = v.reshape(Bx, Sx, N_GROUPS, HEAD_DIM).transpose(0, 2, 1, 3)
        sim = jnp.einsum('bgrsd,bgtd->bgrst', q, k) / math.sqrt(HEAD_DIM)
        attn = jax.nn.softmax(sim, axis=-1)
        out = jnp.einsum('bgrst,bgtd->bgrsd', attn, v)
        out = out.transpose(0, 3, 1, 2, 4).reshape(Bx, Sx, MODEL_DIM)
        return out @ w_out.T + b_out

    def _L0_ffn_ref(x, weight, bias):
        import jax, jax.numpy as jnp
        import numpy as np
        B, S, D_IN, D_OUT = (4, 512, 512, 512)
        EPS = 1e-10
        scale = jnp.mean(jnp.abs(weight))
        w_t = jnp.clip(jnp.round(weight / (scale + EPS)), -1.0, 1.0)
        w_ste = weight + jax.lax.stop_gradient(w_t * scale - weight)
        return jnp.einsum('bsi,oi->bso', x, w_ste) + bias
    h = _L0_tok_ref(L0_tok_A, L0_tok_B, x, L0_tok_log_dt, 512)
    h = jnp.concatenate([h, txt], axis=1)
    h = h + _L0_attn_ref(_layernorm(h, axis=-1), L0_attn_w_qkv, L0_attn_b_qkv, L0_attn_w_out, L0_attn_b_out)
    h = h + _L0_ffn_ref(_layernorm(h, axis=-1), L0_ffn_weight, L0_ffn_bias)
    return h

_drawn_inputs = setup_inputs


def setup_inputs(seed=0):
    import zlib

    import numpy as np

    out = dict(_drawn_inputs(seed))
    spreads = {'L0_attn_b_qkv': (0.0, 0.1), 'L0_attn_b_out': (0.0, 0.1)}
    factors = {}
    for name, (base, spread) in spreads.items():
        noise = np.random.default_rng([zlib.crc32(name.encode()), seed]).standard_normal(out[name].shape)
        drawn = base * np.exp(spread * noise) if base else spread * noise
        out[name] = jnp.asarray(drawn.astype(out[name].dtype))
    for name, factor in factors.items():
        out[name] = (out[name] * factor).astype(out[name].dtype)
    return out
```

```python
from contextlib import ExitStack

import concourse.bass as bass
import numpy as np
from concourse import mybir

F32 = mybir.dt.float32
F16 = mybir.dt.float16
I32 = mybir.dt.int32
ALU = mybir.AluOpType
ACT = mybir.ActivationFunctionType
AX = mybir.AxisListType

P = 128
B, TK, TT, D = 64, 64, 77, 512
S = TK + TT
NS, L = 64, 512
G, R, HD = 8, 4, 16
KB = D // P
EPS = 1e-5
LN_SCALE = 1024.0
PAIRS = B // 2
TILE = 94
NT = 2 * S // TILE
REM = S - P
MROWS = 96
NEG = -32768.0
DOUBLINGS = 6
SQUARINGS = 8
HC = 4


def sliding(nc, ctx):
    def sb(name, shape, dt):
        return ctx.enter_context(nc.sbuf_tensor(name, shape, dt))

    def pb(name, shape, dt=F32):
        return ctx.enter_context(nc.psum_tensor(name, shape, dt))

    def sem(name):
        return ctx.enter_context(nc.semaphore(name))

    return sb, pb, sem


def constants_and_weights(nc, T, wq_t, bqk_t, bv_row, wo_t, b_out, wf_t, b_ffn):
    with ExitStack() as ctx:
        sb, pb, sem = sliding(nc, ctx)
        wq = sb("wq_raw", [P, KB, 6 * P], F32)
        wo = sb("wo_raw", [P, R, D], F32)
        wf = sb("wf_raw", [P, KB, D], F32)
        wneg = sb("wf_negative", [P, KB, D], F32)
        bqk = sb("bqk_raw", [P, R + 1], F32)
        bv = sb("bv_raw", [P, P], F32)
        red = sb("w_reduced", [P, 4], F32)
        tot = sb("w_total", [P, 4], F32)
        sc = sb("w_scalars", [P, 16], F32)

        loaded = sem("w_loaded")
        consts = sem("w_consts")
        reduced = sem("w_reduced_ready")
        total = sem("w_total_ready")
        chain = sem("w_scalar_step")
        hi_ready = sem("w_hi_ready")

        with nc.Block() as block:
            @block.sync
            def _(sp):
                sp.dma_start(wq[:], wq_t.rearrange("(m p) c -> p m c", p=P)).then_inc(loaded, 16)
                sp.dma_start(wo[:], wo_t).then_inc(loaded, 16)
                sp.dma_start(wf[:], wf_t.rearrange("(m p) o -> p m o", p=P)).then_inc(loaded, 16)
                sp.dma_start(bqk[:], bqk_t).then_inc(loaded, 16)
                sp.dma_start(bv[:], bv_row.partition_broadcast(P)).then_inc(loaded, 16)
                sp.dma_start(T.bo[:], b_out.partition_broadcast(P)).then_inc(loaded, 16)
                sp.dma_start(T.bf[:], b_ffn.partition_broadcast(P)).then_inc(loaded, 16)
                sp.wait_ge(loaded, 16 * 7)

            @block.gpsimd
            def _(pool):
                n = [0]

                def step(ins):
                    n[0] += 1
                    ins.then_inc(consts, 1)
                    pool.wait_ge(consts, n[0])

                def keep_within(ap, pattern, width):
                    step(pool.affine_select(out=ap, in_=ap, compare_op=ALU.is_ge, fill=0.0, base=0,
                                            pattern=[[-a, c] for a, c in pattern], channel_multiplier=1))
                    step(pool.affine_select(out=ap, in_=ap, compare_op=ALU.is_ge, fill=0.0, base=width - 1,
                                            pattern=pattern, channel_multiplier=-1))

                step(pool.memset(T.rem_mask[:], 1.0))
                keep_within(T.rem_mask[:].rearrange("p (g d) -> p g d", g=G), [[REM, G], [0, HD]], REM)
                step(pool.memset(T.ident[:], 0.0))
                step(pool.affine_select(out=T.ident[:], in_=T.ident[:], compare_op=ALU.not_equal, fill=1.0, base=0,
                                        pattern=[[-1, P]], channel_multiplier=1))
                step(pool.tensor_copy(T.ident16[:], T.ident[:]))
                step(pool.memset(T.group_mask[:], 1.0))
                keep_within(T.group_mask[:], [[HD, G]], HD)
                step(pool.memset(T.rem_select[:], 0.0))
                for piece in range(2):
                    v = T.rem_select[:].rearrange("p (g t) -> p g t", g=G)
                    step(pool.affine_select(out=v, in_=v, compare_op=ALU.not_equal, fill=NEG, base=-G * piece,
                                            pattern=[[-1, G], [0, REM]], channel_multiplier=1))
                for parity in range(2):
                    step(pool.memset(T.ones_half[:, parity], 0.0))
                    step(pool.memset(T.ones_half[:, parity, HD * parity:HD * parity + HD], 1.0))
                step(pool.memset(T.minus_half[:], -0.5))
                step(pool.memset(T.ones128[:], 1.0))
                step(pool.memset(T.sign[0:64], 1.0))
                step(pool.memset(T.sign[64:128], -1.0))
                step(pool.memset(T.unit_block[:], 0.0))
                step(pool.tensor_copy(T.unit_block[0:64, :], T.ident[0:64, 0:64]))
                for par in range(2):
                    step(pool.memset(T.v_pad[par][:], 0.0))
                    step(pool.memset(T.qs[par][64:MROWS], 0.0))
                    step(pool.memset(T.ks_max[par][64:MROWS], 0.0))
                    step(pool.memset(T.ks_exp[par][64:MROWS], 0.0))
                    step(pool.memset(T.ks_exp[par][64:66], NEG))
                pool.wait_ge(reduced, 4)
                pool.partition_all_reduce(tot[:, 0:2], red[:, 0:2], P, bass.bass_isa.ReduceOp.max).then_inc(total, 1)
                pool.partition_all_reduce(tot[:, 2:3], red[:, 2:3], P, bass.bass_isa.ReduceOp.add).then_inc(total, 1)
                pool.partition_all_reduce(tot[:, 3:4], red[:, 3:4], P, bass.bass_isa.ReduceOp.max).then_inc(total, 1)

            @block.vector
            def _(dve):
                n = [0]

                def step(ins):
                    n[0] += 1
                    ins.then_inc(chain, 1)
                    dve.wait_ge(chain, n[0])

                dve.wait_ge(loaded, 16 * 7)
                dve.tensor_reduce(red[:, 0:1], wq[:], AX.XY, ALU.max, apply_absolute_value=True).then_inc(reduced, 1)
                dve.tensor_reduce(red[:, 1:2], wo[:], AX.XY, ALU.max, apply_absolute_value=True).then_inc(reduced, 1)
                dve.tensor_reduce(red[:, 2:3], wf[:], AX.XY, ALU.add, apply_absolute_value=True).then_inc(reduced, 1)
                step(dve.tensor_reduce(sc[:, 0:1], bqk[:], AX.X, ALU.max, apply_absolute_value=True))
                step(dve.tensor_reduce(sc[:, 1:2], bv[:], AX.X, ALU.max, apply_absolute_value=True))
                dve.tensor_reduce(red[:, 3:4], sc[:, 0:2], AX.X, ALU.max).then_inc(reduced, 1)
                dve.wait_ge(total, 3)
                step(dve.tensor_copy(sc[:, 0:2], tot[:, 0:2]))
                step(dve.scalar_tensor_tensor(sc[:, 2:3], tot[:, 0:1], float(D), tot[:, 3:4], ALU.mult, ALU.add))
                step(dve.tensor_scalar(sc[:, 0:3], sc[:, 0:3], 2.0 ** -60, 2.0 ** 60, ALU.max, ALU.min))

                def bits(a, b):
                    return sc[:, a:b].bitcast(I32)

                step(dve.tensor_scalar(bits(4, 7), bits(0, 3), 0x7F800000, None, ALU.bitwise_and))
                step(dve.tensor_scalar(bits(8, 11), bits(4, 7), -1.0, float(254 << 23), ALU.mult, ALU.add))
                step(dve.tensor_scalar(T.c_wq[:], sc[:, 8:9], 2.0 ** 14, None, ALU.mult))
                step(dve.tensor_scalar(T.c_wo[:], sc[:, 9:10], 2.0 ** 14, None, ALU.mult))
                step(dve.tensor_scalar(T.c_b[:], sc[:, 10:11], 2.0 ** 12, None, ALU.mult))
                step(dve.tensor_scalar(sc[:, 12:13], sc[:, 4:5], 2.0 ** -14 / LN_SCALE, None, ALU.mult))
                step(dve.tensor_tensor(T.f_qkv[:], sc[:, 12:13], T.c_b[:], ALU.mult))
                step(dve.tensor_scalar(sc[:, 13:14], sc[:, 5:6], 2.0 ** -14, None, ALU.mult))
                step(dve.tensor_scalar(sc[:, 14:15], sc[:, 6:7], 2.0 ** -12, None, ALU.mult))
                step(dve.tensor_tensor(T.f_out[:], sc[:, 13:14], sc[:, 14:15], ALU.mult))
                step(dve.scalar_tensor_tensor(T.f_exp[:], sc[:, 14:15], HD ** -0.5, sc[:, 14:15], ALU.mult, ALU.mult))
                step(dve.tensor_scalar(T.bq[:], bqk[:], T.c_b[:, 0:1], None, ALU.mult))
                step(dve.tensor_scalar(T.bv[:], bv[:], T.c_b[:, 0:1], None, ALU.mult))
                dve.wait_ge(consts, 3)
                step(dve.tensor_tensor(T.bv_rem[:], T.bv[:], T.rem_mask[:], ALU.mult))
                step(dve.tensor_scalar(sc[:, 15:16], tot[:, 2:3], 1.0 / (D * D), None, ALU.mult))
                step(dve.tensor_scalar(T.f_ffn[:], sc[:, 15:16], 1.0 / LN_SCALE, None, ALU.mult))
                step(dve.tensor_scalar(sc[:, 3:4], sc[:, 15:16], 1e-10, 0.5, ALU.add, ALU.mult))
                step(dve.tensor_scalar(sc[:, 7:8], sc[:, 3:4], -1.0, None, ALU.mult))
                step(dve.tensor_scalar(wneg[:], wf[:], sc[:, 7:8], None, ALU.is_lt))
                flat = "p a b -> p (a b)"
                dve.scalar_tensor_tensor(T.wf[:].rearrange(flat), wf[:].rearrange(flat), sc[:, 3:4], wneg[:].rearrange(flat),
                                         ALU.is_gt, ALU.subtract)
                dve.wait_ge(hi_ready, 2)
                for f in range(KB):
                    dve.scalar_tensor_tensor(T.wq[:, 1, f].rearrange(flat), wq[:, f, :], T.c_wq[:, 0:1], T.wq[:, 0, f].rearrange(flat),
                                             ALU.mult, ALU.subtract)
                dve.scalar_tensor_tensor(T.wo[:, 1].rearrange(flat), wo[:].rearrange(flat), T.c_wo[:, 0:1], T.wo[:, 0].rearrange(flat),
                                         ALU.mult, ALU.subtract)

            @block.scalar
            def _(act):
                act.wait_ge(chain, 9)
                act.activation(T.wq[:, 0].rearrange("p f m c -> p (f m c)"), wq[:].rearrange("p f c -> p (f c)"), ACT.Copy,
                               scale=T.c_wq[:, 0:1]).then_inc(hi_ready, 1)
                act.activation(T.wo[:, 0], wo[:], ACT.Copy, scale=T.c_wo[:, 0:1]).then_inc(hi_ready, 1)


def state_space_kernel(nc, T, hk, c_t, a_t, b_t, log_dt):
    NC_ = 2
    ITERS = NS // (HC * NC_)
    with ExitStack() as ctx:
        sb, pb, sem = sliding(nc, ctx)
        raw = [sb(f"a_raw{c}", [P, 2, HC, NS], F32) for c in range(NC_)]
        craw = [sb(f"c_raw{c}", [P, HC, NS], F32) for c in range(NC_)]
        mh = [sb(f"m_back{c}", [P, HC, P], F32) for c in range(NC_)]
        mt = [sb(f"m_back_t{c}", [P, HC, P], F32) for c in range(NC_)]
        tmp = [sb(f"s_tmp{c}", [P, HC, 64], F32) for c in range(NC_)]
        ry = [sb(f"residual_and_sum{c}", [P, HC, 192], F32) for c in range(NC_)]
        yf = [sb(f"inverse_gram{c}", [P, HC, P], F32) for c in range(NC_)]
        dn = [sb(f"step_pair{c}", [P, HC, 2, P], F32) for c in range(NC_)]
        xs = [sb(f"krylov{c}", [P, HC, L], F32) for c in range(NC_)]
        ct = [sb(f"c_t{c}", [P, HC, NS], F32) for c in range(NC_)]
        sc = [sb(f"s_scal{c}", [P, 4, HC], F32) for c in range(NC_)]
        ko = [sb(f"k_out{c}", [P, HC // 2, L], F32) for c in range(NC_)]
        bcol = sb("b_columns", [P, NS], F32)
        half = sb("half_step", [P, NS], F32)
        hb = sb("half_step_b", [P, NS], F32)
        pa = [pb(f"s_pa{c}", [P, HC, 128]) for c in range(NC_)]
        pq = [pb(f"s_pq{c}", [P, HC, 256]) for c in range(NC_)]
        pk = [pb(f"s_pk{c}", [P, 512]) for c in range(NC_)]

        loaded0 = sem("s_const_loaded")
        const_dve = sem("s_const_dve")
        const_act = sem("s_const_act")
        loaded = [sem(f"s_loaded{c}") for c in range(NC_)]
        stored = [sem(f"s_stored{c}") for c in range(NC_)]
        by_pe = [sem(f"s_by_pe{c}") for c in range(NC_)]
        by_dve = [sem(f"s_by_dve{c}") for c in range(NC_)]
        by_act = [sem(f"s_by_act{c}") for c in range(NC_)]

        K1 = list(range(SQUARINGS + 1))
        PE_EV = (["transposed", "gram", "colsum"] + [f"r{k}" for k in range(DOUBLINGS)] + ["inverse", "x_first"]
                 + [f"step{k}" for k in K1] + [f"out{j}" for j in range(HC // 2)])
        DVE_EV = (["small", "half_a", "m_tl", "m_tr", "m_bl", "m_back", "al_max", "alpha", "g_scaled", "r_left", "r_full", "y_first"]
                  + [f"r{k}" for k in range(DOUBLINGS)] + ["yf_left", "d_left", "d_full", "x_first"]
                  + [f"{e}{k}" for k in range(SQUARINGS) for e in ("square", "step")] + ["x_last", "out0"])
        ACT_EV = (["m_back_t", "abs_gram", "r_top"] + [f"r{k}" for k in range(DOUBLINGS - 1)] + ["yf_full", "d_top"]
                  + [f"step{k}" for k in range(SQUARINGS)] + ["x_last", "c_t", "out1"])

        def value(events, it, event):
            return it * len(events) + (events.index(event) + 1)

        def unit(p0, p1):
            return T.unit_block[p0:p1, :].unsqueeze(1).broadcast_to([p1 - p0, HC, 64])

        def bc(ap):
            return ap.unsqueeze(2).broadcast_to([P, HC, 64])

        with nc.Block() as block:
            @block.sync
            def _(sp):
                sp.dma_start(half[:], log_dt.partition_broadcast(P)).then_inc(loaded0, 16)
                sp.dma_start(bcol[:], b_t).then_inc(loaded0, 16)
                for c in range(NC_):
                    sp.sem_inc(stored[c], 1)

                def load_a(it, c):
                    src = a_t[:, :, bass.ds(it * (HC * NC_) + HC * c, HC), :]
                    sp.dma_start(raw[c][0:64], src).then_inc(loaded[c], 16)
                    sp.dma_start(raw[c][64:128], src).then_inc(loaded[c], 16)

                def load_c(it, c):
                    sp.dma_start(craw[c][:], c_t[:, bass.ds(it * (HC * NC_) + HC * c, HC), :]).then_inc(loaded[c], 16)

                def store(it, c, j):
                    for e in range(2):
                        sp.dma_start(hk[:, bass.ds(it * (HC * NC_) + HC * c + 2 * j + e, 1), :],
                                     ko[c][64 * e:64 * e + 64, j:j + 1, :]).then_inc(stored[c], 16)

                for c in range(NC_):
                    load_a(0, c)
                    load_c(0, c)
                with sp.Fori(0, ITERS - 1) as it:
                    for c in range(NC_):
                        sp.wait_ge(by_dve[c], value(DVE_EV, it, "m_back"))
                        load_a(it + 1, c)
                    for c in range(NC_):
                        sp.wait_ge(by_act[c], value(ACT_EV, it, "c_t"))
                        load_c(it + 1, c)
                    for c in range(NC_):
                        sp.wait_ge(by_dve[c], value(DVE_EV, it, "out0"))
                        store(it, c, 0)
                    for c in range(NC_):
                        sp.wait_ge(by_act[c], value(ACT_EV, it, "out1"))
                        store(it, c, 1)
                for c in range(NC_):
                    sp.wait_ge(by_dve[c], ITERS * len(DVE_EV))
                    store(ITERS - 1, c, 0)
                    sp.wait_ge(by_act[c], ITERS * len(ACT_EV))
                    store(ITERS - 1, c, 1)
                for c in range(NC_):
                    sp.wait_ge(stored[c], 16 * HC * ITERS + 1)

            @block.tensor
            def _(pe):
                with pe.Fori(0, ITERS) as it:
                    def wd(c, e):
                        pe.wait_ge(by_dve[c], value(DVE_EV, it, e))

                    def wa(c, e):
                        pe.wait_ge(by_act[c], value(ACT_EV, it, e))

                    for c in range(NC_):
                        wd(c, "m_back")
                        for h in range(HC):
                            ins = pe.transpose(pa[c][:, h, :], mh[c][:, h, :], T.ident[:])
                        ins.then_inc(by_pe[c], 1)
                        for h in range(HC):
                            ins = pe.matmul(pq[c][:, 0, 64 * h:64 * h + 64], mh[c][:, h, :], mh[c][:, h, 0:64], start=True, stop=True)
                        ins.then_inc(by_pe[c], 1)
                    for c in range(NC_):
                        wa(c, "abs_gram")
                        pe.matmul(pq[c][:, 2, :], T.ones128[:], tmp[c][:].rearrange("p h j -> p (h j)"),
                                  start=True, stop=True).then_inc(by_pe[c], 1)
                    for k in range(DOUBLINGS):
                        for c in range(NC_):
                            if k == 0:
                                wd(c, "y_first")
                                wa(c, "r_top")
                            else:
                                wd(c, f"r{k - 1}")
                                wa(c, f"r{k - 1}")
                            lo, hi = (0, 64) if k == 0 else ((64, 128) if k == DOUBLINGS - 1 else (0, 128))
                            for h in range(HC):
                                ins = pe.matmul(pa[c][:, h, lo:hi], ry[c][:, h, 0:P], ry[c][:, h, 64 + lo:64 + hi], start=True, stop=True)
                            ins.then_inc(by_pe[c], 1)
                    for c in range(NC_):
                        wa(c, "yf_full")
                        for h in range(HC):
                            pe.matmul(pa[c][:, h, 0:64], yf[c][:, h, :], mt[c][:, h, 0:64], start=True, stop=True)
                            ins = pe.matmul(pa[c][:, h, 64:128], mt[c][:, h, :], yf[c][:, h, 0:64], start=True, stop=True)
                        ins.then_inc(by_pe[c], 1)
                    for c in range(NC_):
                        wd(c, "d_full")
                        wa(c, "d_top")
                        for h in range(HC):
                            ins = pe.matmul(pq[c][:, h, 0:1], dn[c][:, h, 1, :], sc[c][:, 1, h:h + 1], start=True, stop=True)
                        ins.then_inc(by_pe[c], 1)
                    for k in K1:
                        n = 1 << k
                        for c in range(NC_):
                            if k == 0:
                                wd(c, "x_first")
                            else:
                                wd(c, f"step{k - 1}")
                                wa(c, f"step{k - 1}")
                            for h in range(HC):
                                if k < SQUARINGS - 1:
                                    pe.matmul(pa[c][:, h, 0:64], dn[c][:, h, 1, :], dn[c][:, h, 0, 0:64], start=True, stop=True)
                                if k < SQUARINGS:
                                    pe.matmul(pa[c][:, h, 64:128], dn[c][:, h, 0, :], dn[c][:, h, 1, 0:64], start=True, stop=True)
                                ins = pe.matmul(pq[c][:, h, 0:n], dn[c][:, h, 1, :], xs[c][:, h, 0:n], start=True, stop=True)
                            ins.then_inc(by_pe[c], 1)
                    for j in range(HC // 2):
                        for c in range(NC_):
                            wa(c, "c_t")
                            if j == 0:
                                wa(c, "x_last")
                                wd(c, "x_last")
                            else:
                                wd(c, "out0")
                            for e in range(2):
                                ins = pe.matmul(pk[c][64 * e:64 * e + 64, :], ct[c][:, 2 * j + e, :], xs[c][:, 2 * j + e, :],
                                                start=True, stop=True)
                            ins.then_inc(by_pe[c], 1)

            @block.vector
            def _(dve):
                dve.wait_ge(const_act, 1)
                dve.tensor_scalar(half[:], half[:], 0.5, None, ALU.mult).then_inc(const_dve, 1)
                dve.wait_ge(const_dve, 1)
                dve.tensor_tensor(hb[:], half[:], bcol[:], ALU.mult).then_inc(const_dve, 1)
                dve.wait_ge(const_dve, 2)
                with dve.Fori(0, ITERS) as it:
                    def wp(c, e):
                        dve.wait_ge(by_pe[c], value(PE_EV, it, e))

                    def wa(c, e):
                        dve.wait_ge(by_act[c], value(ACT_EV, it, e))

                    def wd(c, e):
                        dve.wait_ge(by_dve[c], value(DVE_EV, it, e))

                    for c in range(NC_):
                        h0 = it * (HC * NC_) + HC * c
                        dve.tensor_scalar(sc[c][:, 0, :], half[:, bass.ds(h0, HC)], -1.0, None, ALU.mult)
                        dve.tensor_copy(sc[c][:, 1, :], hb[:, bass.ds(h0, HC)]).then_inc(by_dve[c], 1)
                        dve.wait_ge(loaded[c], it * 48 + 48)
                        wd(c, "small")
                        dve.tensor_tensor(raw[c][:], raw[c][:], sc[c][:, 0, :].unsqueeze(1).unsqueeze(3).broadcast_to([P, 2, HC, NS]),
                                          ALU.mult).then_inc(by_dve[c], 1)
                        wd(c, "half_a")
                        dve.tensor_tensor(mh[c][0:64, :, 0:64], raw[c][0:64, 0],
                                          unit(0, 64), ALU.add).then_inc(by_dve[c], 1)
                        dve.tensor_scalar(mh[c][0:64, :, 64:128], raw[c][0:64, 1], -1.0, None, ALU.mult).then_inc(by_dve[c], 1)
                        dve.tensor_copy(mh[c][64:128, :, 0:64], raw[c][64:128, 1]).then_inc(by_dve[c], 1)
                        wd(c, "m_tl")
                        dve.tensor_copy(mh[c][64:128, :, 64:128], mh[c][0:64, :, 0:64]).then_inc(by_dve[c], 1)
                    for c in range(NC_):
                        wp(c, "colsum")
                        dve.tensor_reduce(sc[c][:, 2, :], pq[c][:, 2, :].rearrange("p (h j) -> p h j", h=HC), AX.X, ALU.max).then_inc(by_dve[c], 1)
                        wd(c, "al_max")
                        dve.reciprocal(sc[c][:, 3, :], sc[c][:, 2, :]).then_inc(by_dve[c], 1)
                        wd(c, "alpha")
                        dve.tensor_tensor(tmp[c][:], pq[c][:, 0, :].rearrange("p (h j) -> p h j", h=HC), bc(sc[c][:, 3, :]), ALU.mult).then_inc(by_dve[c], 1)
                        wd(c, "g_scaled")
                        dve.tensor_tensor(ry[c][:, :, 0:64], unit(0, P), tmp[c][:], ALU.subtract).then_inc(by_dve[c], 1)
                        wd(c, "r_left")
                        dve.tensor_copy(ry[c][64:128, :, 64:128], ry[c][0:64, :, 0:64]).then_inc(by_dve[c], 1)
                        dve.tensor_tensor(ry[c][:, :, 128:192], unit(0, P), ry[c][:, :, 0:64], ALU.add).then_inc(by_dve[c], 1)
                    for k in range(DOUBLINGS):
                        for c in range(NC_):
                            wp(c, f"r{k}")
                            ps = pa[c]
                            if k > 0:
                                wd(c, "y_first" if k == 1 else f"r{k - 1}")
                                ins = dve.tensor_tensor(ry[c][:, :, 128:192], ry[c][:, :, 128:192], ps[:, :, 64:128], ALU.add)
                            if k < DOUBLINGS - 1:
                                ins = dve.tensor_copy(ry[c][:, :, 64:128], ps[:, :, 0:64])
                            ins.then_inc(by_dve[c], 1)
                    for c in range(NC_):
                        wd(c, f"r{DOUBLINGS - 1}")
                        dve.tensor_tensor(yf[c][:, :, 0:64], ry[c][:, :, 128:192], bc(sc[c][:, 3, :]), ALU.mult).then_inc(by_dve[c], 1)
                    for c in range(NC_):
                        wp(c, "inverse")
                        ps = pa[c][:].rearrange("p h (t j) -> p h t j", t=2)
                        for t in range(2):
                            ins = dve.scalar_tensor_tensor(dn[c][:, :, t, 0:64], ps[:, :, t, :], 2.0, unit(0, P), ALU.mult, ALU.subtract)
                        ins.then_inc(by_dve[c], 1)
                        wd(c, "d_left")
                        dve.tensor_copy(dn[c][64:128, :, :, 64:128], dn[c][0:64, :, :, 0:64]).then_inc(by_dve[c], 1)
                    for c in range(NC_):
                        wp(c, "x_first")
                        dve.tensor_tensor(xs[c][:, :, 0:1], sc[c][:, 1, :].unsqueeze(2), pq[c][:, :, 0:1], ALU.add).then_inc(by_dve[c], 1)
                    for k in range(SQUARINGS):
                        for c in range(NC_):
                            wp(c, f"step{k}")
                            t0 = 0 if k < SQUARINGS - 1 else 1
                            ps = pa[c][:].rearrange("p h (t j) -> p h t j", t=2)
                            dve.tensor_copy(dn[c][:, :, t0:2, 0:64], ps[:, :, t0:2, :]).then_inc(by_dve[c], 1)
                            n = 1 << k
                            dve.tensor_copy(xs[c][:, :, n:2 * n], pq[c][:, :, 0:n]).then_inc(by_dve[c], 1)
                    for c in range(NC_):
                        wp(c, f"step{SQUARINGS}")
                        dve.tensor_copy(xs[c][:, 0:HC // 2, L // 2:L], pq[c][:, 0:HC // 2, :]).then_inc(by_dve[c], 1)
                    for c in range(NC_):
                        wp(c, "out0")
                        dve.wait_ge(stored[c], it * (16 * HC) + 1)
                        dve.tensor_copy(ko[c][:, 0, :], pk[c][:]).then_inc(by_dve[c], 1)

            @block.scalar
            def _(act):
                act.wait_ge(loaded0, 32)
                act.activation(half[:], half[:], ACT.Exp).then_inc(const_act, 1)
                with act.Fori(0, ITERS) as it:
                    def wp(c, e):
                        act.wait_ge(by_pe[c], value(PE_EV, it, e))

                    def wd(c, e):
                        act.wait_ge(by_dve[c], value(DVE_EV, it, e))

                    for c in range(NC_):
                        wp(c, "transposed")
                        act.copy(mt[c][:], pa[c][:]).then_inc(by_act[c], 1)
                        wp(c, "gram")
                        act.activation(tmp[c][:].rearrange("p h j -> p (h j)"), pq[c][:, 0, :], ACT.Abs).then_inc(by_act[c], 1)
                    for c in range(NC_):
                        wd(c, "g_scaled")
                        act.copy(ry[c][0:64, :, 64:128], tmp[c][64:128]).then_inc(by_act[c], 1)
                    for k in range(DOUBLINGS - 1):
                        for c in range(NC_):
                            wd(c, f"r{k}")
                            act.copy(ry[c][0:64, :, 0:64], pa[c][64:128, :, 0:64])
                            act.mul(ry[c][64:128, :, 0:64], pa[c][0:64, :, 0:64], -1.0).then_inc(by_act[c], 1)
                    for c in range(NC_):
                        wd(c, "yf_left")
                        act.copy(yf[c][64:128, :, 64:128], yf[c][0:64, :, 0:64])
                        act.mul(yf[c][0:64, :, 64:128], yf[c][64:128, :, 0:64], -1.0).then_inc(by_act[c], 1)
                    for c in range(NC_):
                        wd(c, "d_left")
                        act.mul(dn[c][0:64, :, :, 64:128], pa[c][64:128].rearrange("p h (t j) -> p h t j", t=2), -2.0).then_inc(by_act[c], 1)
                    for k in range(SQUARINGS):
                        for c in range(NC_):
                            wd(c, f"square{k}")
                            t0 = 0 if k < SQUARINGS - 1 else 1
                            ps = pa[c][:].rearrange("p h (t j) -> p h t j", t=2)
                            act.mul(dn[c][0:64, :, t0:2, 64:128], ps[64:128, :, t0:2, :], -1.0)
                            act.copy(dn[c][64:128, :, t0:2, 64:128], ps[0:64, :, t0:2, :]).then_inc(by_act[c], 1)
                    for c in range(NC_):
                        wp(c, f"step{SQUARINGS}")
                        act.copy(xs[c][:, HC // 2:HC, L // 2:L], pq[c][:, HC // 2:HC, :]).then_inc(by_act[c], 1)
                    for c in range(NC_):
                        act.wait_ge(loaded[c], it * 48 + 48)
                        act.activation(ct[c][:], craw[c][:], ACT.Copy, scale=T.sign[:, 0:1]).then_inc(by_act[c], 1)
                    for c in range(NC_):
                        wp(c, "out1")
                        act.wait_ge(stored[c], it * (16 * HC) + 1)
                        act.copy(ko[c][:, 1, :], pk[c][:]).then_inc(by_act[c], 1)


class Pair:

    def __init__(self, turn, off):
        self.turn, self.off, self.par = turn, off, off % 2

    def at(self, a, c=0):
        return a * self.off + c if self.turn is None else self.turn * (2 * a) + (a * self.off + c)

    def half(self, a, c=0):
        return a * (self.off // 2) + c if self.turn is None else self.turn * a + (a * (self.off // 2) + c)

    def plus(self, k):
        return Pair(self.turn, self.off + k)

    def real(self):
        return self.turn is not None or 0 <= self.off < PAIRS

    def first(self):
        return self.turn is None and self.off == 0


S_MAIN = [(r, g) for r in range(R) for g in range(G)]
S_UNITS = [("main", S_MAIN[i:i + 3]) for i in range(0, len(S_MAIN), 3)] + [("rem", list(range(G))[i:i + 3]) for i in range(0, G, 3)]
E_UNITS = [(h, g) for h in range(2) for g in [G] + list(range(G))]
NSU, NEU = len(S_UNITS), len(E_UNITS)
WEIGHT = {"T1": 5, "T2": 5, "QK": 15, "F": 18, "V": 14, "Oa": 13, "O": 13, "PV0a": 11, "PV0b": 11, "PV0": 10, "PV1a": 11, "PV1b": 11, "PV1": 10}


def schedule():
    def parse(text):
        return [(w.split(".")[0], int(w.split(".")[1]) if "." in w else 0) for w in text.split()]

    even = parse("T1.0 PV1a LN1P.2 RELOAD LOAD T1.1 PV1b T1.2 PV1 QK.0 INV1 QK.1 OUT1 QKP.0 LN2Y.0 QK.2 QKP.1 LN2P.0 QK.3 QKP.2 LN2Y.1 QK.4 QKP.3 LN2P.1 "
                 "PV0a QKP.4 QKMOVE LN2Y.2 T2.0 PV0b LN2P.2 T2.1 MP PV0 BF.0 T2.2 INV0 "
                 "BF.1 MT MMOVE OUT0 BF.2 F.0 STORE.0 F.1 STORE.1 F.2 STORE.2")
    odd = parse("PV1a LN1S.0 PV1b V.0 LN1S.1 PV1 BO.0 V.1 INV1 LN1S.2 Oa.0 LN1 OUT1 O.0 BO.1 LN1Y.0 Oa.1 O.1 LN1P.0 LN2S.0 LN1Y.1 PV0a BO.2 PV0b "
                "LN1P.1 MP LN2S.1 PV0 Oa.2 LN1Y.2 INV0 MT MMOVE O.2 LN2S.2 OUT0 LN2")
    out = []
    for rest in (even, odd):
        total = sum(WEIGHT.get(kind, 0) for kind, _ in rest)
        placed, now = [], 0
        for i, step in enumerate(rest):
            now += WEIGHT.get(step[0], 0)
            placed.append((now / total, 1, i, step))
        at_max = next(at for at, _, _, (kind, _) in placed if kind == "MP")
        placed += [(at_max * k / NSU, 0, k, ("S", k)) for k in range(NSU)]
        placed += [(SPAN_E[0] + (SPAN_E[1] - SPAN_E[0]) * k / NEU, 2, k, ("E", k)) for k in range(NEU)]
        out.append([step for *_, step in sorted(placed, key=lambda x: x[:3])])
    return out


SPAN_E = (0.04, 0.97)
STEPS = schedule()
PSUM_USERS = ("T1", "T2", "QK", "F", "V", "O", "MT")
PER_PAIR = {"T1": NT, "T2": NT, "QK": R + 1, "F": NT, "V": 2, "O": NT, "MT": 2}
SHIFT = {"T1": 1, "QK": 1, "V": 1, "O": -1, "T2": -2, "F": -2}
USES = [(kind, k if kind != "MT" else (b + 1) % 2, SHIFT[kind] if kind != "MT" else (b + 1) // 2)
        for b in range(2) for kind, k in STEPS[b] if kind in PSUM_USERS]


def bank_of(kind, k):
    return next(i for i, u in enumerate(USES) if u[0] == kind and u[1] == k) % 2


def bank_before(slot, kind, k):
    at = next(i for i, u in enumerate(USES) if u[0] == kind and u[1] == k)
    for back in range(4):
        uses = [(i, u) for i, u in enumerate(USES) if i % 2 == at % 2 and (back > 0 or i < at)]
        for i, u in reversed(uses):
            pair = slot.plus(u[2] - back)
            if pair.real():
                return u[0], u[1], pair
    return None


def blocks(nc, T, h_text, hk, out):
    scratch = nc.dram_tensor("stack_scratch", (2, P, 2, 2 * R * S + 2 * S), F16).ap()
    QC = 2 * R * S
    with ExitStack() as ctx:
        sb, pb, sem = sliding(nc, ctx)
        hx = sb("h_rows", [TILE, NT, D], F32)
        hr = sb("h_again", [TILE, NT, D], F32)
        h2 = sb("h_after_attention", [TILE, NT, D], F32)
        yn2 = [sb(f"normed2_{i}", [TILE, D], F32) for i in range(2)]
        xp = {w: sb(f"normed_pieces{w}", [TILE, NT, 2, D], F16) for w in (1, 2)}
        xt = {w: sb(f"normed_t{w}", [P, 2, KB, 2 * S], F16) for w in (1, 2)}
        st = {w: sb(f"ln_stats{w}", [TILE, NT, 6], F32) for w in (1, 2)}
        mv = {w: sb(f"ln_mean_var{w}", [TILE, NT, 2], F32) for w in (1, 2)}
        ve = {w: sb(f"ln_var_eps{w}", [TILE, NT], F32) for w in (1, 2)}
        rs = {w: sb(f"ln_rstd{w}", [TILE, NT], F32) for w in (1, 2)}
        yq = [sb(f"qk_f32_{i}", [P, 2 * S], F32) for i in range(2)]
        qn = [sb(f"qk_pieces{i}", [P, 2, QC + 2 * S], F16) for i in range(2)]
        xr = [sb(f"x_rem{i}", [P, 2 * KB, G * REM], F16) for i in range(2)]
        kr = [[sb(f"k_rem{i}_{b}", [P, 2, G, REM], F16) for b in range(2)] for i in range(2)]
        vr = [[sb(f"v_rem{i}_{b}", [P, P], F32) for b in range(2)] for i in range(2)]
        mx = sb("row_max", [P, R + 1, G], F32)
        mp = sb("row_max_pieces", [P, R + 1, 2, G], F16)
        mt = sb("row_max_t", [2 * G, R, S], F16)
        pt = [sb(f"probs_t{i}", [P, G + 1, R * S], F32) for i in range(2)]
        dinv = [sb(f"row_sum_inv{i}", [P, 2 * S], F32) for i in range(2)]
        oy = [sb(f"attn_out_f32_{i}", [P, 2 * S], F32) for i in range(2)]
        ot = [sb(f"attn_out_t{i}", [P, 2, R, 2 * S], F16) for i in range(2)]
        gen = [pb(f"p_gen{i}", [P, 512]) for i in range(2)]
        psc = [pb(f"p_scores{i}", [P, 512]) for i in range(2)]
        pst = [pb(f"p_scores_t{i}", [P, 512]) for i in range(2)]
        pso = pb("p_attn_out", [P, 512])
        psd = pb("p_row_sums", [P, 512])

        h_loaded = sem("h_loaded")
        h_reloaded = sem("h_reloaded")
        out_stored = [sem(f"out_stored{k}") for k in range(NT)]
        ln_ve = {w: sem(f"ln{w}_var_ready") for w in (1, 2)}
        ln_step = {w: sem(f"ln{w}_step") for w in (1, 2)}
        ln_gate = {w: sem(f"ln{w}_stats_seen") for w in (1, 2)}
        ln_rs = {w: sem(f"ln{w}_rstd_ready") for w in (1, 2)}
        yn_ready = {w: sem(f"ln{w}_normed") for w in (1, 2)}
        hi_ready = {w: sem(f"ln{w}_hi_ready") for w in (1, 2)}
        lo_ready = {w: sem(f"ln{w}_lo_ready") for w in (1, 2)}
        bias_added = {w: sem(f"bias{w}_added") for w in (1, 2)}
        done = {k: sem(f"{k.lower()}_computed") for k in PSUM_USERS}
        taken = {k: sem(f"{k.lower()}_evacuated") for k in PSUM_USERS}
        v_rem = sem("v_rem_scaled")
        x_rem_ready = sem("x_rem_ready")
        q_hi = sem("qk_hi_ready")
        q_lo = sem("qk_lo_ready")
        spilled = [sem(f"stack_written{i}") for i in range(2)]
        stacked = [sem(f"stack_loaded{i}") for i in range(2)]
        k_rem_ready = sem("k_rem_ready")
        s_done = sem("scores_computed")
        s_max = sem("scores_maxed")
        mp_step = sem("max_piece_step")
        m_stacked = sem("max_stacked")
        e_done = sem("scores_t_computed")
        e_exp = sem("probs_ready")
        pv_done = sem("attn_out_computed")
        d_inv = sem("row_sum_inverted")
        oy_ready = sem("attn_out_normed")
        o_hi = sem("attn_hi_ready")
        o_lo = sem("attn_lo_ready")

        def normed(w, k, p):
            return hx[:, k, :] if w == 1 else yn2[(k + p.par) % 2][:]

        def gen16(kind, k):
            return gen[bank_of(kind, k)][:].bitcast(F16)

        def slots(eng, emit):
            for i in range(-2, 4):
                emit(Pair(None, i))
            with eng.Fori(2, (PAIRS - 2) // 2) as turn:
                emit(Pair(turn, 0))
                emit(Pair(turn, 1))
            for i in range(PAIRS - 2, PAIRS + 2):
                emit(Pair(None, i))

        def steps(slot):
            for b in range(2):
                for kind, k in STEPS[b]:
                    p = slot
                    bb = b
                    if kind in ("S", "MP", "MT", "MMOVE"):
                        p, bb = slot.plus((b + 1) // 2), (b + 1) % 2
                    elif kind.startswith("PV1") or kind in ("INV1", "OUT1"):
                        p, bb = slot.plus(b - 1), (b + 1) % 2
                    elif kind in ("T1", "QK", "QKP", "QKMOVE", "V"):
                        p = slot.plus(1)
                    elif kind in ("LN1S", "LN1", "LN1Y", "LOAD") or (kind == "LN1P" and b == 1):
                        p = slot.plus(2)
                    elif kind == "LN1P":
                        p = slot.plus(1)
                    elif kind in ("RELOAD", "BO", "Oa", "O", "LN2S", "LN2"):
                        p = slot.plus(-1)
                    elif kind in ("LN2Y", "LN2P", "BF", "T2", "F", "STORE"):
                        p = slot.plus(-2)
                    if p.real():
                        yield kind, k, p, bb

        def h_parts(t, p):
            def at(src, b, t0, n):
                return src[bass.ds(p.at(2, b), 1), t0:t0 + n, :]
            parts = []
            edges = sorted({0, TK, S, S + TK, 2 * S} | {TILE * i for i in range(NT + 1)})
            for a, z in zip(edges, edges[1:]):
                b, tok = a // S, a % S
                src = at(hk, b, tok, z - a) if tok < TK else at(h_text, b, tok - TK, z - a)
                parts.append((t[a % TILE:a % TILE + z - a, a // TILE:a // TILE + 1, :], src.rearrange("a t d -> t a d")))
            return parts

        H_PARTS = 6

        with nc.Block() as block:
            @block.sync
            def _(sp):
                def emit(slot):
                    for kind, k, p, b in steps(slot):
                        if kind == "LOAD":
                            if not p.first():
                                sp.wait_ge(lo_ready[1], p.at(NT))
                            for dst, src in h_parts(hx, p):
                                sp.dma_start(dst, src).then_inc(h_loaded, 16)
                        elif kind == "RELOAD":
                            if not p.first():
                                sp.wait_ge(taken["O"], p.at(NT))
                            for dst, src in h_parts(hr, p):
                                sp.dma_start(dst, src).then_inc(h_reloaded, 16)
                        elif kind == "QKMOVE":
                            sp.wait_ge(q_hi, p.at(R + 1, R + 1))
                            sp.wait_ge(q_lo, p.at(R + 1, R + 1))
                            sp.dma_start(scratch[p.par], qn[p.par][:]).then_inc(spilled[p.par], 16)
                            sp.wait_ge(spilled[p.par], p.half(16, 16))
                            src = scratch[p.par].rearrange("(g d) l c -> l d g c", g=G)
                            for j in range(4):
                                rows = slice(HD * j, HD * j + HD)
                                sp.dma_start(T.qs[p.par][rows, :, :], src[j % 2, :, :, 0:QC]).then_inc(stacked[p.par], 16)
                                sp.dma_start(T.ks_max[p.par][rows, :, :], src[j // 2, :, :, QC:]).then_inc(stacked[p.par], 16)
                                sp.dma_start(T.ks_exp[p.par][rows, :, :], src[j // 2, :, :, QC:]).then_inc(stacked[p.par], 16)
                        elif kind == "MMOVE":
                            sp.wait_ge(taken["MT"], p.at(2, b + 1))
                            for piece in range(2):
                                sp.dma_start(T.qs[p.par][64 + piece:65 + piece, :, R * S * b:R * S * (b + 1)],
                                             mt[G * piece:G * piece + G].rearrange("g r t -> g (r t)")).then_inc(m_stacked, 16)
                        elif kind == "STORE":
                            sp.wait_ge(taken["F"], p.at(NT, k + 1))
                            dst = out.rearrange("(q b) t d -> q (b t) d", b=2)[bass.ds(p.at(1), 1)]
                            sp.dma_start(dst[:, TILE * k:TILE * k + TILE, :].rearrange("q t d -> t q d"), h2[:, k:k + 1, :]).then_inc(out_stored[k], 16)

                slots(sp, emit)
                for k in range(NT):
                    sp.wait_ge(out_stored[k], 16 * PAIRS)

            @block.tensor
            def _(pe):
                def free_bank(slot_pair, kind, k):
                    shift = SHIFT[kind] if kind != "MT" else 1 - k
                    before = bank_before(slot_pair.plus(-shift), kind, k)
                    if before:
                        pe.wait_ge(taken[before[0]], before[2].at(PER_PAIR[before[0]], before[1] + 1))

                def emit(slot):
                    for kind, k, p, b in steps(slot):
                        if kind in ("T1", "T2"):
                            w = int(kind[1])
                            pe.wait_ge(hi_ready[w], p.at(NT, k + 1))
                            pe.wait_ge(lo_ready[w], p.at(NT, k + 1))
                            free_bank(p, kind, k)
                            for j in range(2 * KB):
                                ins = pe.transpose(gen16(kind, k)[:, TILE * j:TILE * j + TILE],
                                                   xp[w][:, k, j // KB, P * (j % KB):P * (j % KB) + P], T.ident16[0:TILE, 0:TILE])
                            ins.then_inc(done[kind], 1)
                        elif kind == "QK":
                            pe.wait_ge(taken["T1"], p.at(NT, NT))
                            free_bank(p, kind, k)
                            n = 0
                            for f in range(KB):
                                for lw, lx in ((0, 0), (0, 1), (1, 0)):
                                    ins = pe.matmul(gen[bank_of(kind, k)][:, 0:2 * S], T.wq[:, lw, f, k, :], xt[1][:, lx, f, :],
                                                    start=(n == 0), stop=(n == 3 * KB - 1))
                                    n += 1
                            ins.then_inc(done[kind], 1)
                        elif kind == "V":
                            pe.wait_ge(taken["T1"], p.at(NT, NT))
                            pe.wait_ge(x_rem_ready, p.at(2, k + 1))
                            free_bank(p, kind, k)
                            bank = gen[bank_of(kind, k)]
                            for part in range(2):
                                n = 0
                                for f in range(KB):
                                    for lx, lw in ((0, 0), (1, 0), (0, 1)):
                                        if part == 0:
                                            dst, lhs = bank[:, 0:P], xt[1][:, lx, f, S * k:S * k + P]
                                        else:
                                            dst = bank[0:G * REM, P:2 * P]
                                            lhs = xr[k][:, KB * lx + f, :]
                                        ins = pe.matmul(dst, lhs, T.wq[:, lw, f, 5, :], start=(n == 0), stop=(n == 3 * KB - 1))
                                        n += 1
                            ins.then_inc(done[kind], 1)
                        elif kind in ("Oa", "O"):
                            if kind == "Oa":
                                pe.wait_ge(o_hi, p.at(4, 4))
                                pe.wait_ge(o_lo, p.at(4, 4))
                                free_bank(p, "O", k)
                            for r in (range(0, R // 2) if kind == "Oa" else range(R // 2, R)):
                                for n, (lo_, lw) in enumerate(((0, 0), (0, 1), (1, 0))):
                                    ins = pe.matmul(gen[bank_of("O", k)][0:TILE, :], ot[p.par][:, lo_, r, TILE * k:TILE * k + TILE],
                                                    T.wo[:, lw, r, :], start=(r == 0 and n == 0), stop=(r == R - 1 and n == 2))
                            if kind == "O":
                                ins.then_inc(done["O"], 1)
                        elif kind == "F":
                            pe.wait_ge(taken["T2"], p.at(NT, k + 1))
                            free_bank(p, kind, k)
                            n = 0
                            for f in range(KB):
                                for lx in range(2):
                                    ins = pe.matmul(gen[bank_of(kind, k)][0:TILE, :], xt[2][:, lx, f, TILE * k:TILE * k + TILE],
                                                    T.wf[:, f, :], start=(n == 0), stop=(n == 2 * KB - 1))
                                    n += 1
                            ins.then_inc(done[kind], 1)
                        elif kind == "S":
                            if k == 0 and b == 0:
                                pe.wait_ge(stacked[p.par], p.half(16 * 12, 16 * 12))
                            if not (p.first() and b == 0 and k < 2):
                                pe.wait_ge(s_max, p.at(2 * NSU, NSU * b + k - 1))
                            what, tiles = S_UNITS[k]
                            ks = T.ks_max[p.par]
                            for j, tile in enumerate(tiles):
                                if what == "main":
                                    r, g = tile
                                    lhs = T.qs[p.par][0:MROWS, g, R * S * b + S * r:R * S * b + S * r + P]
                                    dst = psc[k % 2][:, S * j:S * j + S]
                                else:
                                    g = tile
                                    for r in range(R):
                                        z = R * S * b + S * (r + 1)
                                        ins = pe.matmul(psc[k % 2][32 * r:32 * r + 32, S * j:S * j + S], T.qs[p.par][0:MROWS, g, z - 32:z],
                                                        ks[0:MROWS, g, S * b:S * b + S], start=True, stop=True)
                                    continue
                                ins = pe.matmul(dst, lhs, ks[0:MROWS, g, S * b:S * b + S], start=True, stop=True)
                            ins.then_inc(s_done, 1)
                        elif kind == "MT":
                            pe.wait_ge(mp_step, p.at(4, 2 * b + 2))
                            free_bank(p, kind, b)
                            for r in range(R + 1):
                                ins = pe.transpose(gen16(kind, b)[0:2 * G, P * r:P * r + P], mp[:, r].rearrange("p l g -> p (l g)"), T.ident16[:])
                            ins.then_inc(done[kind], 1)
                        elif kind == "E":
                            h, g = E_UNITS[k]
                            if k == 0:
                                pe.wait_ge(taken["MT"], p.at(2, b + 1))
                                pe.wait_ge(k_rem_ready, p.at(2, b + 1))
                            if k == 1:
                                pe.wait_ge(m_stacked, p.at(64, 32 * b + 32))
                            if not (p.first() and b == 0 and k < 2):
                                pe.wait_ge(e_exp, p.at(2 * NEU, NEU * b + k - 1))
                            c0 = R * S * b + 2 * S * h
                            if g < G:
                                ins = pe.matmul(pst[k % 2][:, 0:2 * S], T.ks_exp[p.par][0:MROWS, g, S * b:S * b + P],
                                                T.qs[p.par][0:MROWS, g, c0:c0 + 2 * S], start=True, stop=True)
                            else:
                                dst = pst[k % 2][0:G * REM, 0:2 * S]
                                for n, (lk, lq) in enumerate(((0, 0), (0, 1), (1, 0), (1, 1))):
                                    pe.matmul(dst, kr[p.par][b][:, lk].rearrange("p g t -> p (g t)"), qn[p.par][:, lq, c0:c0 + 2 * S],
                                              start=(n == 0), stop=False)
                                ins = pe.matmul(dst, T.rem_select[:], mt[:].rearrange("p r t -> p (r t)")[:, 2 * S * h:2 * S * h + 2 * S],
                                                start=False, stop=True)
                            ins.then_inc(e_done, 1)
                        elif kind[0:2] == "PV":
                            h = int(kind[2])
                            if kind.endswith("a"):
                                pe.wait_ge(e_exp, p.at(2 * NEU, NEU * b + (G + 1) * (h + 1)))
                                pe.wait_ge(taken["V"], p.at(2, b + 1))
                                if not (p.first() and b == 0 and h == 0):
                                    pe.wait_ge(oy_ready, p.at(4, 2 * b + h))
                            cols = slice(2 * S * h, 2 * S * h + 2 * S)
                            if kind[3:]:
                                parity = "ab".index(kind[3])
                                for q in range(G // 2):
                                    rows = slice(32 * q, 32 * q + 32)
                                    pe.matmul(pso[rows, 0:2 * S], T.v_pad[p.par][:, b, parity, rows], pt[b][:, 2 * q + parity, cols],
                                              start=(parity == 0), stop=False, skip_group_check=True)
                                for q in range(G // 2):
                                    rows = slice(32 * q, 32 * q + 32)
                                    pe.matmul(psd[rows, 0:2 * S], T.ones_half[:, parity, :], pt[b][:, 2 * q + parity, cols],
                                              start=(parity == 0), stop=False, skip_group_check=True)
                            else:
                                probs = pt[b][0:G * REM, G, cols]
                                pe.matmul(psd[:, 0:2 * S], T.rem_mask[0:G * REM, :], probs, start=False, stop=True,
                                          skip_group_check=True)
                                pe.matmul(pso[:, 0:2 * S], vr[p.par][b][0:G * REM, :], probs, start=False, stop=True,
                                          skip_group_check=True).then_inc(pv_done, 1)

                slots(pe, emit)

            @block.scalar
            def _(act):
                def emit(slot):
                    for kind, k, p, b in steps(slot):
                        if kind == "QK":
                            act.wait_ge(done["QK"], p.at(R + 1, k + 1))
                            if not (p.first() and k < 2):
                                act.wait_ge(q_hi, p.at(R + 1, k - 1))
                                act.wait_ge(q_lo, p.at(R + 1, k - 1))
                            act.activation(yq[k % 2 if p.par == 0 else (k + 1) % 2][:], gen[bank_of(kind, k)][:, 0:2 * S], ACT.Identity,
                                           bias=T.bq[:, k:k + 1], scale=T.f_qkv[:, 0:1]).then_inc(taken["QK"], 1)
                        elif kind == "QKMOVE":
                            act.wait_ge(taken["T1"], p.at(NT, NT))
                            if not p.first():
                                act.wait_ge(done["V"], p.at(2))
                            for bb in range(2):
                                src = xt[1][:, :, :, S * bb + P:S * bb + S].rearrange("p l f t -> p (l f) t").unsqueeze(2)
                                act.copy(xr[bb][:].rearrange("p x (g t) -> p x g t", g=G),
                                         src.broadcast_to([P, 2 * KB, G, REM])).then_inc(x_rem_ready, 1)
                        elif kind == "E":
                            h, g = E_UNITS[k]
                            act.wait_ge(e_done, p.at(2 * NEU, NEU * b + k + 1))
                            if k in (0, G + 1) and not p.first():
                                act.wait_ge(pv_done, p.at(4, 2 * b - 4 + h + 1))
                            rows = P if g < G else G * REM
                            act.activation(pt[b][0:rows, g, 2 * S * h:2 * S * h + 2 * S], pst[k % 2][0:rows, 0:2 * S], ACT.Exp,
                                           scale=T.f_exp[0:rows, 0:1]).then_inc(e_exp, 1)
                        elif kind in ("LN1P", "LN2P"):
                            w = int(kind[2])
                            act.wait_ge(yn_ready[w], p.at(NT, k + 1))
                            if not p.first():
                                act.wait_ge(done[f"T{w}"], p.at(NT, k - NT + 1))
                            act.copy(xp[w][:, k, 0, :], normed(w, k, p)).then_inc(hi_ready[w], 1)
                        elif kind in ("OUT0", "OUT1"):
                            k = int(kind[3])
                            act.wait_ge(oy_ready, p.at(4, 2 * b + k + 1))
                            if not (p.turn is None and p.off < 2) and b == 0 and k == 0:
                                act.wait_ge(done["O"], p.at(NT, -NT))
                            act.copy(ot[p.par][:, 0, 2 * k:2 * k + 2, S * b:S * b + S],
                                     oy[k][:].rearrange("p (r t) -> p r t", r=2)).then_inc(o_hi, 1)

                slots(act, emit)

            @block.gpsimd
            def _(pool):
                def emit(slot):
                    for kind, k, p, b in steps(slot):
                        if kind in ("LN1", "LN2"):
                            w = int(kind[2])
                            pool.wait_ge(ln_ve[w], p.at(1, 1))
                            pool.tensor_tensor(rs[w][:], ve[w][:], T.minus_half[0:TILE, 0:NT], ALU.pow).then_inc(ln_rs[w], 1)
                        elif kind in ("LN1P", "LN2P"):
                            w = int(kind[2])
                            pool.wait_ge(hi_ready[w], p.at(NT, k + 1))
                            pool.tensor_tensor(xp[w][:, k, 1, :], normed(w, k, p), xp[w][:, k, 0, :],
                                               ALU.subtract).then_inc(lo_ready[w], 1)
                        elif kind == "BF":
                            pool.wait_ge(yn_ready[2], p.at(NT, k + 1))
                            pool.tensor_tensor(h2[:, k, :], h2[:, k, :], T.bf[0:TILE], ALU.add).then_inc(bias_added[2], 1)
                        elif kind == "BO":
                            pool.wait_ge(h_reloaded, p.at(16 * H_PARTS, 16 * H_PARTS))
                            pool.tensor_tensor(hr[:, k, :], hr[:, k, :], T.bo[0:TILE], ALU.add).then_inc(bias_added[1], 1)
                        elif kind == "QKP":
                            pool.wait_ge(q_hi, p.at(R + 1, k + 1))
                            y = yq[k % 2 if p.par == 0 else (k + 1) % 2][:]
                            if k < R:
                                view = lambda l: qn[p.par][:, l, 0:QC].rearrange("p (b r t) -> p b r t", b=2, r=R)[:, :, k, :]
                                y = y.rearrange("p (b t) -> p b t", b=2)
                            else:
                                view = lambda l: qn[p.par][:, l, QC:]
                            pool.tensor_tensor(view(1), y, view(0), ALU.subtract).then_inc(q_lo, 1)
                        elif kind == "QKMOVE":
                            pool.wait_ge(q_lo, p.at(R + 1, R + 1))
                            if not (p.turn is None and p.off < 2):
                                pool.wait_ge(e_done, p.at(2 * NEU, -2 * NEU))
                            for bb in range(2):
                                for l in range(2):
                                    src = qn[p.par][:, l, QC + S * bb + P:QC + S * bb + S].unsqueeze(1).broadcast_to([P, G, REM])
                                    ins = pool.tensor_tensor(kr[p.par][bb][:, l], src, T.group_mask[:].unsqueeze(2).broadcast_to([P, G, REM]), ALU.mult)
                                ins.then_inc(k_rem_ready, 1)
                        elif kind in ("OUT0", "OUT1"):
                            k = int(kind[3])
                            pool.wait_ge(o_hi, p.at(4, 2 * b + k + 1))
                            view = lambda l: ot[p.par][:, l, 2 * k:2 * k + 2, S * b:S * b + S]
                            pool.tensor_tensor(view(1), oy[k][:].rearrange("p (r t) -> p r t", r=2), view(0), ALU.subtract).then_inc(o_lo, 1)

                slots(pool, emit)

            @block.vector
            def _(dve):
                def emit(slot):
                    for kind, k, p, b in steps(slot):
                        if kind in ("LN1S", "LN2S"):
                            w = int(kind[2])
                            src = hx if w == 1 else h2
                            if w == 1:
                                dve.wait_ge(h_loaded, p.at(16 * H_PARTS, 16 * H_PARTS))
                            else:
                                dve.wait_ge(taken["O"], p.at(NT, k + 1))
                            ins = dve.bn_stats(st[w][:, k, :], src[:, k, :])
                            if k == NT - 1:
                                ins.then_inc(ln_step[w], 1)
                        elif kind in ("LN1", "LN2"):
                            w = int(kind[2])
                            dve.wait_ge(ln_step[w], p.at(2, 1))
                            dve.sem_inc(ln_gate[w], 1)
                            for t in range(NT):
                                ins = dve.bn_aggr(mv[w][:, t, :], st[w][:, t, :])
                            ins.then_inc(ln_step[w], 1)
                            dve.wait_ge(ln_step[w], p.at(2, 2))
                            dve.tensor_scalar(ve[w][:], mv[w][:, :, 1], EPS, LN_SCALE ** -2, ALU.add, ALU.mult).then_inc(ln_ve[w], 1)
                        elif kind in ("LN1Y", "LN2Y"):
                            w = int(kind[2])
                            src = hx if w == 1 else h2
                            if k == 0:
                                dve.wait_ge(ln_rs[w], p.at(1, 1))
                            if w == 2 and not (p.first() and k < 2):
                                dve.wait_ge(lo_ready[w], p.at(NT, k - 1))
                            dve.tensor_scalar(normed(w, k, p), src[:, k, :], mv[w][:, k, 0:1], rs[w][:, k:k + 1],
                                              ALU.subtract, ALU.mult).then_inc(yn_ready[w], 1)
                        elif kind in ("T1", "T2"):
                            w = int(kind[1])
                            dve.wait_ge(done[kind], p.at(NT, k + 1))
                            if not p.first() and k == 0:
                                if w == 1:
                                    dve.wait_ge(done["V"], p.at(2))
                                else:
                                    dve.wait_ge(done["F"], p.at(NT))
                            dve.tensor_copy(xt[w][:, :, :, TILE * k:TILE * k + TILE],
                                            gen16(kind, k)[:, 0:2 * KB * TILE].rearrange("p (l f t) -> p l f t", l=2, f=KB)).then_inc(taken[kind], 1)
                        elif kind == "QKP":
                            dve.wait_ge(taken["QK"], p.at(R + 1, k + 1))
                            if k == 0 and not (p.turn is None and p.off < 2):
                                dve.wait_ge(spilled[p.par], p.half(16))
                                dve.wait_ge(e_done, p.at(2 * NEU, -2 * NEU))
                                dve.wait_ge(k_rem_ready, p.at(2, -2))
                            y = yq[k % 2 if p.par == 0 else (k + 1) % 2][:]
                            if k < R:
                                dst = qn[p.par][:, 0, 0:QC].rearrange("p (b r t) -> p b r t", b=2, r=R)[:, :, k, :]
                                y = y.rearrange("p (b t) -> p b t", b=2)
                            else:
                                dst = qn[p.par][:, 0, QC:]
                            dve.tensor_copy(dst, y).then_inc(q_hi, 1)
                        elif kind == "V":
                            dve.wait_ge(done["V"], p.at(2, k + 1))
                            if not (p.turn is None and p.off < 2):
                                dve.wait_ge(pv_done, p.at(4, 2 * k - 8 + 2))
                            bank = gen[bank_of(kind, k)]
                            for parity in range(2):
                                view = lambda ap: ap.rearrange("p (q e d) -> p q e d", e=2, d=HD)[:, :, parity, :]
                                dve.scalar_tensor_tensor(view(T.v_pad[p.par][:, k, parity, :]), view(bank[:, 0:P]), T.f_qkv[:, 0:1], view(T.bv[:]),
                                                         ALU.mult, ALU.add)
                            rr = slice(0, G * REM)
                            dve.scalar_tensor_tensor(vr[p.par][k][rr, :], bank[rr, P:2 * P], T.f_qkv[rr, 0:1], T.rem_mask[rr, :],
                                                     ALU.mult, ALU.mult).then_inc(v_rem, 1)
                            dve.wait_ge(v_rem, p.at(2, k + 1))
                            dve.tensor_tensor(vr[p.par][k][rr, :], vr[p.par][k][rr, :], T.bv_rem[rr, :], ALU.add).then_inc(taken["V"], 1)
                        elif kind == "O":
                            dve.wait_ge(done["O"], p.at(NT, k + 1))
                            dve.wait_ge(bias_added[1], p.at(NT, k + 1))
                            if not p.first():
                                dve.wait_ge(out_stored[k], p.at(16))
                            dve.scalar_tensor_tensor(h2[:, k, :], gen[bank_of(kind, k)][0:TILE, :], T.f_out[0:TILE, 0:1], hr[:, k, :],
                                                     ALU.mult, ALU.add).then_inc(taken["O"], 1)
                        elif kind == "F":
                            dve.wait_ge(done["F"], p.at(NT, k + 1))
                            dve.wait_ge(bias_added[2], p.at(NT, k + 1))
                            dve.scalar_tensor_tensor(h2[:, k, :], gen[bank_of(kind, k)][0:TILE, :], T.f_ffn[0:TILE, 0:1], h2[:, k, :],
                                                     ALU.mult, ALU.add).then_inc(taken["F"], 1)
                        elif kind == "S":
                            what, tiles = S_UNITS[k]
                            dve.wait_ge(s_done, p.at(2 * NSU, NSU * b + k + 1))
                            n = len(tiles)
                            j0 = 3 * k if what == "main" else R * G + tiles[0]
                            dve.tensor_reduce(mx[:].rearrange("p r g -> p (r g)")[:, j0:j0 + n],
                                              psc[k % 2][:, 0:S * n].rearrange("p (j t) -> p j t", j=n), AX.X, ALU.max).then_inc(s_max, 1)
                        elif kind == "MP":
                            dve.wait_ge(s_max, p.at(2 * NSU, NSU * (b + 1)))
                            if not (p.first() and b == 0):
                                dve.wait_ge(done["MT"], p.at(2, b))
                            dve.tensor_scalar(mp[:, :, 0, :], mx[:], -1.0 / NEG, None, ALU.mult).then_inc(mp_step, 1)
                            dve.wait_ge(mp_step, p.at(4, 2 * b + 1))
                            dve.scalar_tensor_tensor(mp[:, :, 1, :], mx[:], -1.0 / NEG, mp[:, :, 0, :], ALU.mult, ALU.subtract).then_inc(mp_step, 1)
                        elif kind == "MT":
                            dve.wait_ge(done["MT"], p.at(2, b + 1))
                            if not (p.first() and b == 0):
                                dve.wait_ge(m_stacked, p.at(64, 32 * b))
                                dve.wait_ge(e_done, p.at(2 * NEU, NEU * b - NEU + G + 2))
                            ps = gen16(kind, b)
                            dve.tensor_copy(mt[:, :, 0:P], ps[0:2 * G, 0:P * R].rearrange("p (r t) -> p r t", r=R))
                            dve.tensor_copy(mt[:, :, P:S], ps[0:2 * G, P * R:P * R + P].rearrange("p (r t) -> p r t", r=R)[:, :, 32 - REM:32]).then_inc(taken["MT"], 1)
                        elif kind in ("PV0", "PV1"):
                            k = int(kind[2])
                            dve.wait_ge(pv_done, p.at(4, 2 * b + k + 1))
                            dve.reciprocal(dinv[k][:, 0:S], psd[:, 0:S])
                        elif kind in ("INV0", "INV1"):
                            k = int(kind[3])
                            dve.reciprocal(dinv[k][:, S:2 * S], psd[:, S:2 * S]).then_inc(d_inv, 1)
                            dve.wait_ge(d_inv, p.at(4, 2 * b + k + 1))
                            if not (p.first() and b == 0):
                                dve.wait_ge(o_lo, p.at(4, 2 * b + k - 1))
                            dve.tensor_tensor(oy[k][:], pso[:, 0:2 * S], dinv[k][:], ALU.mult).then_inc(oy_ready, 1)

                slots(dve, emit)


class Tiles:
    pass


def fusion_kernel(nc, c_t, txt, a_t, b_t, log_dt, wq_t, bqk_t, bv_row, wo_t, b_out, wf_t, b_ffn, out):
    hk = nc.dram_tensor("kernel_tokens", (B, TK, D), F32).ap()
    with ExitStack() as ctx:
        sb, _, _ = sliding(nc, ctx)
        T = Tiles()
        T.ident = sb("ident", [P, P], F32)
        T.ident16 = sb("ident16", [P, P], F16)
        T.ones128 = sb("ones128", [P, P], F32)
        T.sign = sb("sign", [P, 1], F32)
        T.unit_block = sb("unit_block", [P, 64], F32)
        T.group_mask = sb("group_mask", [P, G], F32)
        T.rem_mask = sb("rem_mask", [P, P], F32)
        T.rem_select = sb("rem_select", [2 * G, G * REM], F16)
        T.ones_half = sb("ones_half", [P, 2, 32], F32)
        T.minus_half = sb("minus_half", [P, NT], F32)
        T.wq = sb("wq_t", [P, 2, KB, 6, P], F16)
        T.wo = sb("wo_t", [P, 2, R, D], F16)
        T.wf = sb("wf_t", [P, KB, D], F16)
        T.bq = sb("bq", [P, R + 1], F32)
        T.bv = sb("bv", [P, P], F32)
        T.bv_rem = sb("bv_rem", [P, P], F32)
        T.bo = sb("bo", [P, D], F32)
        T.bf = sb("bf", [P, D], F32)
        T.c_wq, T.c_wo, T.c_b = sb("c_wq", [P, 1], F32), sb("c_wo", [P, 1], F32), sb("c_b", [P, 1], F32)
        T.f_qkv, T.f_out = sb("f_qkv", [P, 1], F32), sb("f_out", [P, 1], F32)
        T.f_exp, T.f_ffn = sb("f_exp", [P, 1], F32), sb("f_ffn", [P, 1], F32)
        T.qs = [sb(f"q_stack{i}", [MROWS, G, 2 * R * S], F16) for i in range(2)]
        T.ks_max = [sb(f"k_stack_max{i}", [MROWS, G, 2 * S], F16) for i in range(2)]
        T.ks_exp = [sb(f"k_stack_exp{i}", [MROWS, G, 2 * S], F16) for i in range(2)]
        T.v_pad = [sb(f"v_pad{i}", [P, 2, 2, P], F32) for i in range(2)]
        constants_and_weights(nc, T, wq_t, bqk_t, bv_row, wo_t, b_out, wf_t, b_ffn)
        state_space_kernel(nc, T, hk, c_t, a_t, b_t, log_dt)
        blocks(nc, T, txt, hk, out)


def laid_out(i):
    w, b = i["L0_attn_w_qkv"], i["L0_attn_b_qkv"]
    wq = w[:D].reshape(G, R, HD, D).transpose(3, 1, 0, 2).reshape(D, R * P)
    bq = b[:D].reshape(G, R, HD).transpose(0, 2, 1).reshape(P, R)
    return {
        "c_t": i["x"].transpose(3, 2, 1, 0).reshape(2 * NS, NS, B),
        "txt": i["txt"],
        "a_t": i["L0_tok_A"].transpose(1, 3, 0, 2),
        "b_t": i["L0_tok_B"].transpose(2, 1, 0).reshape(2 * NS, NS),
        "log_dt": i["L0_tok_log_dt"].reshape(NS),
        "wq_t": np.concatenate([wq, w[D:].T], axis=1),
        "bqk_t": np.concatenate([bq, b[D:D + P].reshape(P, 1)], axis=1),
        "bv": b[D + P:],
        "wo_t": i["L0_attn_w_out"].reshape(D, G, R, HD).transpose(1, 3, 2, 0).reshape(P, R, D),
        "b_out": i["L0_attn_b_out"],
        "wf_t": i["L0_ffn_weight"].T,
        "b_ffn": i["L0_ffn_bias"],
    }


def kernel(**inputs):
    import concourse.bacc as _bacc
    from concourse.bass_utils import run_bass_kernel_spmd as _run

    nc = _bacc.Bacc("TRN2", target_bir_lowering=False, num_devices=1)
    arrays, args = {}, []
    for name, a in laid_out({k: np.asarray(v) for k, v in inputs.items()}).items():
        arrays[f"in_{name}"] = np.ascontiguousarray(a)
        args.append(nc.dram_tensor(f"in_{name}", a.shape, mybir.dt.from_np(a.dtype), kind="ExternalInput").ap())
    args.append(nc.dram_tensor("out_h", (B, S, D), F32, kind="ExternalOutput").ap())
    fusion_kernel(nc, *args)
    return _run(nc, [arrays], core_ids=[0]).results[0]["out_h"]
```

```python
from contextlib import ExitStack

import concourse.bass as bass
import numpy as np
from concourse import mybir

F32 = mybir.dt.float32
F16 = mybir.dt.float16
I32 = mybir.dt.int32
ALU = mybir.AluOpType
ACT = mybir.ActivationFunctionType
AX = mybir.AxisListType

P = 128
B, TK, TT, D = 64, 64, 77, 512
S = TK + TT
NS, L = 64, 512
G, R, HD = 8, 4, 16
KB = D // P
EPS = 1e-5
LN_SCALE = 1024.0
PAIRS = B // 2
TILE = 94
NT = 2 * S // TILE
REM = S - P
MROWS = 96
NEG = -32768.0
DOUBLINGS = 6
SQUARINGS = 8
HC = 4


def sliding(nc, ctx):
    def sb(name, shape, dt):
        return ctx.enter_context(nc.sbuf_tensor(name, shape, dt))

    def pb(name, shape, dt=F32):
        return ctx.enter_context(nc.psum_tensor(name, shape, dt))

    def sem(name):
        return ctx.enter_context(nc.semaphore(name))

    return sb, pb, sem


def constants_and_weights(nc, T, wq_t, bqk_t, bv_row, wo_t, b_out, wf_t, b_ffn):
    with ExitStack() as ctx:
        sb, pb, sem = sliding(nc, ctx)
        wq = sb("wq_raw", [P, KB, 6 * P], F32)
        wo = sb("wo_raw", [P, R, D], F32)
        wf = sb("wf_raw", [P, KB, D], F32)
        wneg = sb("wf_negative", [P, KB, D], F32)
        bqk = sb("bqk_raw", [P, R + 1], F32)
        bv = sb("bv_raw", [P, P], F32)
        red = sb("w_reduced", [P, 4], F32)
        tot = sb("w_total", [P, 4], F32)
        sc = sb("w_scalars", [P, 16], F32)

        loaded = sem("w_loaded")
        consts = sem("w_consts")
        reduced = sem("w_reduced_ready")
        total = sem("w_total_ready")
        chain = sem("w_scalar_step")
        hi_ready = sem("w_hi_ready")

        with nc.Block() as block:
            @block.sync
            def _(sp):
                sp.dma_start(wq[:], wq_t.rearrange("(m p) c -> p m c", p=P)).then_inc(loaded, 16)
                sp.dma_start(wo[:], wo_t).then_inc(loaded, 16)
                sp.dma_start(wf[:], wf_t.rearrange("(m p) o -> p m o", p=P)).then_inc(loaded, 16)
                sp.dma_start(bqk[:], bqk_t).then_inc(loaded, 16)
                sp.dma_start(bv[:], bv_row.partition_broadcast(P)).then_inc(loaded, 16)
                sp.dma_start(T.bo[:], b_out.partition_broadcast(P)).then_inc(loaded, 16)
                sp.dma_start(T.bf[:], b_ffn.partition_broadcast(P)).then_inc(loaded, 16)
                sp.wait_ge(loaded, 16 * 7)

            @block.gpsimd
            def _(pool):
                n = [0]

                def step(ins):
                    n[0] += 1
                    ins.then_inc(consts, 1)
                    pool.wait_ge(consts, n[0])

                def keep_within(ap, pattern, width):
                    step(pool.affine_select(out=ap, in_=ap, compare_op=ALU.is_ge, fill=0.0, base=0,
                                            pattern=[[-a, c] for a, c in pattern], channel_multiplier=1))
                    step(pool.affine_select(out=ap, in_=ap, compare_op=ALU.is_ge, fill=0.0, base=width - 1,
                                            pattern=pattern, channel_multiplier=-1))

                step(pool.memset(T.rem_mask[:], 1.0))
                keep_within(T.rem_mask[:].rearrange("p (g d) -> p g d", g=G), [[REM, G], [0, HD]], REM)
                step(pool.memset(T.ident[:], 0.0))
                step(pool.affine_select(out=T.ident[:], in_=T.ident[:], compare_op=ALU.not_equal, fill=1.0, base=0,
                                        pattern=[[-1, P]], channel_multiplier=1))
                step(pool.tensor_copy(T.ident16[:], T.ident[:]))
                step(pool.memset(T.group_mask[:], 1.0))
                keep_within(T.group_mask[:], [[HD, G]], HD)
                step(pool.memset(T.rem_select[:], 0.0))
                for piece in range(2):
                    v = T.rem_select[:].rearrange("p (g t) -> p g t", g=G)
                    step(pool.affine_select(out=v, in_=v, compare_op=ALU.not_equal, fill=NEG, base=-G * piece,
                                            pattern=[[-1, G], [0, REM]], channel_multiplier=1))
                for parity in range(2):
                    step(pool.memset(T.ones_half[:, parity], 0.0))
                    step(pool.memset(T.ones_half[:, parity, HD * parity:HD * parity + HD], 1.0))
                step(pool.memset(T.minus_half[:], -0.5))
                step(pool.memset(T.ones128[:], 1.0))
                step(pool.memset(T.sign[0:64], 1.0))
                step(pool.memset(T.sign[64:128], -1.0))
                step(pool.memset(T.unit_block[:], 0.0))
                step(pool.tensor_copy(T.unit_block[0:64, :], T.ident[0:64, 0:64]))
                for par in range(2):
                    step(pool.memset(T.v_pad[par][:], 0.0))
                    step(pool.memset(T.qs[par][64:MROWS], 0.0))
                    step(pool.memset(T.ks_max[par][64:MROWS], 0.0))
                    step(pool.memset(T.ks_exp[par][64:MROWS], 0.0))
                    step(pool.memset(T.ks_exp[par][64:66], NEG))
                pool.wait_ge(reduced, 4)
                pool.partition_all_reduce(tot[:, 0:2], red[:, 0:2], P, bass.bass_isa.ReduceOp.max).then_inc(total, 1)
                pool.partition_all_reduce(tot[:, 2:3], red[:, 2:3], P, bass.bass_isa.ReduceOp.add).then_inc(total, 1)
                pool.partition_all_reduce(tot[:, 3:4], red[:, 3:4], P, bass.bass_isa.ReduceOp.max).then_inc(total, 1)

            @block.vector
            def _(dve):
                n = [0]

                def step(ins):
                    n[0] += 1
                    ins.then_inc(chain, 1)
                    dve.wait_ge(chain, n[0])

                dve.wait_ge(loaded, 16 * 7)
                dve.tensor_reduce(red[:, 0:1], wq[:], AX.XY, ALU.max, apply_absolute_value=True).then_inc(reduced, 1)
                dve.tensor_reduce(red[:, 1:2], wo[:], AX.XY, ALU.max, apply_absolute_value=True).then_inc(reduced, 1)
                dve.tensor_reduce(red[:, 2:3], wf[:], AX.XY, ALU.add, apply_absolute_value=True).then_inc(reduced, 1)
                step(dve.tensor_reduce(sc[:, 0:1], bqk[:], AX.X, ALU.max, apply_absolute_value=True))
                step(dve.tensor_reduce(sc[:, 1:2], bv[:], AX.X, ALU.max, apply_absolute_value=True))
                dve.tensor_reduce(red[:, 3:4], sc[:, 0:2], AX.X, ALU.max).then_inc(reduced, 1)
                dve.wait_ge(total, 3)
                step(dve.tensor_copy(sc[:, 0:2], tot[:, 0:2]))
                step(dve.scalar_tensor_tensor(sc[:, 2:3], tot[:, 0:1], float(D), tot[:, 3:4], ALU.mult, ALU.add))
                step(dve.tensor_scalar(sc[:, 0:3], sc[:, 0:3], 2.0 ** -60, 2.0 ** 60, ALU.max, ALU.min))

                def bits(a, b):
                    return sc[:, a:b].bitcast(I32)

                step(dve.tensor_scalar(bits(4, 7), bits(0, 3), 0x7F800000, None, ALU.bitwise_and))
                step(dve.tensor_scalar(bits(8, 11), bits(4, 7), -1.0, float(254 << 23), ALU.mult, ALU.add))
                step(dve.tensor_scalar(T.c_wq[:], sc[:, 8:9], 2.0 ** 14, None, ALU.mult))
                step(dve.tensor_scalar(T.c_wo[:], sc[:, 9:10], 2.0 ** 14, None, ALU.mult))
                step(dve.tensor_scalar(T.c_b[:], sc[:, 10:11], 2.0 ** 12, None, ALU.mult))
                step(dve.tensor_scalar(sc[:, 12:13], sc[:, 4:5], 2.0 ** -14 / LN_SCALE, None, ALU.mult))
                step(dve.tensor_tensor(T.f_qkv[:], sc[:, 12:13], T.c_b[:], ALU.mult))
                step(dve.tensor_scalar(sc[:, 13:14], sc[:, 5:6], 2.0 ** -14, None, ALU.mult))
                step(dve.tensor_scalar(sc[:, 14:15], sc[:, 6:7], 2.0 ** -12, None, ALU.mult))
                step(dve.tensor_tensor(T.f_out[:], sc[:, 13:14], sc[:, 14:15], ALU.mult))
                step(dve.scalar_tensor_tensor(T.f_exp[:], sc[:, 14:15], HD ** -0.5, sc[:, 14:15], ALU.mult, ALU.mult))
                step(dve.tensor_scalar(T.bq[:], bqk[:], T.c_b[:, 0:1], None, ALU.mult))
                step(dve.tensor_scalar(T.bv[:], bv[:], T.c_b[:, 0:1], None, ALU.mult))
                dve.wait_ge(consts, 3)
                step(dve.tensor_tensor(T.bv_rem[:], T.bv[:], T.rem_mask[:], ALU.mult))
                step(dve.tensor_scalar(sc[:, 15:16], tot[:, 2:3], 1.0 / (D * D), None, ALU.mult))
                step(dve.tensor_scalar(T.f_ffn[:], sc[:, 15:16], 1.0 / LN_SCALE, None, ALU.mult))
                step(dve.tensor_scalar(sc[:, 3:4], sc[:, 15:16], 1e-10, 0.5, ALU.add, ALU.mult))
                step(dve.tensor_scalar(sc[:, 7:8], sc[:, 3:4], -1.0, None, ALU.mult))
                step(dve.tensor_scalar(wneg[:], wf[:], sc[:, 7:8], None, ALU.is_lt))
                flat = "p a b -> p (a b)"
                dve.scalar_tensor_tensor(T.wf[:].rearrange(flat), wf[:].rearrange(flat), sc[:, 3:4], wneg[:].rearrange(flat),
                                         ALU.is_gt, ALU.subtract)
                dve.wait_ge(hi_ready, 2)
                for f in range(KB):
                    dve.scalar_tensor_tensor(T.wq[:, 1, f].rearrange(flat), wq[:, f, :], T.c_wq[:, 0:1], T.wq[:, 0, f].rearrange(flat),
                                             ALU.mult, ALU.subtract)
                dve.scalar_tensor_tensor(T.wo[:, 1].rearrange(flat), wo[:].rearrange(flat), T.c_wo[:, 0:1], T.wo[:, 0].rearrange(flat),
                                         ALU.mult, ALU.subtract)

            @block.scalar
            def _(act):
                act.wait_ge(chain, 9)
                act.activation(T.wq[:, 0].rearrange("p f m c -> p (f m c)"), wq[:].rearrange("p f c -> p (f c)"), ACT.Copy,
                               scale=T.c_wq[:, 0:1]).then_inc(hi_ready, 1)
                act.activation(T.wo[:, 0], wo[:], ACT.Copy, scale=T.c_wo[:, 0:1]).then_inc(hi_ready, 1)


def state_space_kernel(nc, T, hk, c_t, a_t, b_t, log_dt):
    NC_ = 2
    ITERS = NS // (HC * NC_)
    with ExitStack() as ctx:
        sb, pb, sem = sliding(nc, ctx)
        raw = [sb(f"a_raw{c}", [P, 2, HC, NS], F32) for c in range(NC_)]
        craw = [sb(f"c_raw{c}", [P, HC, NS], F32) for c in range(NC_)]
        mh = [sb(f"m_back{c}", [P, HC, P], F32) for c in range(NC_)]
        mt = [sb(f"m_back_t{c}", [P, HC, P], F32) for c in range(NC_)]
        tmp = [sb(f"abs_gram{c}", [P, HC, 64], F32) for c in range(NC_)]
        rr = [sb(f"residual{c}", [P, HC, P], F32) for c in range(NC_)]
        yy = [sb(f"inverse_sum{c}", [P, HC, P], F32) for c in range(NC_)]
        dt_ = [sb(f"step_t{c}", [P, HC, P], F32) for c in range(NC_)]
        nx = [sb(f"step_krylov{c}", [P, HC, P + L], F32) for c in range(NC_)]
        ct = [sb(f"c_t{c}", [P, HC, NS], F32) for c in range(NC_)]
        small = [sb(f"half_steps{c}", [P, 3, HC], F32) for c in range(NC_)]
        al = [sb(f"alpha{c}", [P, 3, HC], F32) for c in range(NC_)]
        ko = [sb(f"k_out{c}", [P, HC // 2, L], F32) for c in range(NC_)]
        bcol = sb("b_columns", [P, NS], F32)
        half = sb("half_step", [P, NS + HC * NC_], F32)
        hb = sb("half_step_b", [P, NS + HC * NC_], F32)
        pa = [pb(f"s_pa{c}", [P, HC, 128]) for c in range(NC_)]
        pq = [pb(f"s_pq{c}", [P, HC, 256]) for c in range(NC_)]
        pk = [pb(f"s_pk{c}", [P, 512]) for c in range(NC_)]

        loaded0 = sem("s_const_loaded")
        const_dve = sem("s_const_dve")
        const_act = sem("s_const_act")
        loaded = [sem(f"s_loaded{c}") for c in range(NC_)]
        stored = [sem(f"s_stored{c}") for c in range(NC_)]
        by_pe = [sem(f"s_by_pe{c}") for c in range(NC_)]
        by_dve = [sem(f"s_by_dve{c}") for c in range(NC_)]
        by_act = [sem(f"s_by_act{c}") for c in range(NC_)]
        small_ready = [sem(f"s_half_steps_ready{c}") for c in range(NC_)]
        by_pool = [sem(f"s_by_pool{c}") for c in range(NC_)]

        PE_EV = (["transposed", "gram", "colsum"] + [f"r{k}" for k in range(DOUBLINGS)] + ["inverse", "x_first"]
                 + [f"step{k}" for k in range(SQUARINGS + 1)] + [f"out{j}" for j in range(HC // 2)])
        DVE_EV = (["al_max", "alpha", "alpha_neg", "residual", "y_first"] + [f"r{k}" for k in range(1, DOUBLINGS)] + ["y_scaled", "d", "d_t", "x_first"]
                  + [f"step{k}" for k in range(SQUARINGS)] + ["x_last", "out0"])
        ACT_EV = (["m_back_t", "abs_gram"] + [f"r{k}" for k in range(DOUBLINGS - 1)] + ["d_t2"]
                  + [f"step{k}" for k in range(SQUARINGS)] + ["x_last", "c_t", "out1"])
        POOL_EV = ["half_a", "m_back"]

        def value(events, it, event):
            return it * len(events) + (events.index(event) + 1)

        def heads(ap):
            return ap.unsqueeze(1).broadcast_to([P, HC, P])

        with nc.Block() as block:
            @block.sync
            def _(sp):
                sp.dma_start(half[:, 0:NS], log_dt.partition_broadcast(P)).then_inc(loaded0, 16)
                sp.dma_start(bcol[:], b_t).then_inc(loaded0, 16)
                for c in range(NC_):
                    sp.sem_inc(stored[c], 1)

                def load_a(it, c):
                    src = a_t[:, :, bass.ds(it * (HC * NC_) + HC * c, HC), :]
                    sp.dma_start(raw[c][0:64], src).then_inc(loaded[c], 16)
                    for part in range(2):
                        sp.dma_start(raw[c][64:128, part:part + 1], src[:, 1 - part:2 - part]).then_inc(loaded[c], 16)

                def load_c(it, c):
                    sp.dma_start(craw[c][:], c_t[:, bass.ds(it * (HC * NC_) + HC * c, HC), :]).then_inc(loaded[c], 16)

                def store(it, c, j):
                    for e in range(2):
                        sp.dma_start(hk[:, bass.ds(it * (HC * NC_) + HC * c + 2 * j + e, 1), :],
                                     ko[c][64 * e:64 * e + 64, j:j + 1, :]).then_inc(stored[c], 16)

                for c in range(NC_):
                    load_a(0, c)
                    load_c(0, c)
                with sp.Fori(0, ITERS - 1) as it:
                    for c in range(NC_):
                        sp.wait_ge(by_pool[c], value(POOL_EV, it, "m_back"))
                        load_a(it + 1, c)
                    for c in range(NC_):
                        sp.wait_ge(by_act[c], value(ACT_EV, it, "c_t"))
                        load_c(it + 1, c)
                    for c in range(NC_):
                        sp.wait_ge(by_dve[c], value(DVE_EV, it, "out0"))
                        store(it, c, 0)
                    for c in range(NC_):
                        sp.wait_ge(by_act[c], value(ACT_EV, it, "out1"))
                        store(it, c, 1)
                for c in range(NC_):
                    sp.wait_ge(by_dve[c], ITERS * len(DVE_EV))
                    store(ITERS - 1, c, 0)
                    sp.wait_ge(by_act[c], ITERS * len(ACT_EV))
                    store(ITERS - 1, c, 1)
                for c in range(NC_):
                    sp.wait_ge(stored[c], 16 * HC * ITERS + 1)

            @block.gpsimd
            def _(pool):
                with pool.Fori(0, ITERS) as it:
                    for c in range(NC_):
                        pool.wait_ge(loaded[c], it * 64 + 64)
                        pool.wait_ge(small_ready[c], it + 1)
                        pool.tensor_tensor(raw[c][:], raw[c][:], small[c][:, 0:2, :].unsqueeze(3).broadcast_to([P, 2, HC, NS]),
                                           ALU.mult).then_inc(by_pool[c], 1)
                        pool.wait_ge(by_pool[c], value(POOL_EV, it, "half_a"))
                        pool.tensor_tensor(mh[c][:].rearrange("p h (t j) -> p t h j", t=2), raw[c][:],
                                           T.ident[:].rearrange("p (t j) -> p t j", t=2).unsqueeze(2).broadcast_to([P, 2, HC, NS]),
                                           ALU.add).then_inc(by_pool[c], 1)
                        pool.wait_ge(by_pool[c], value(POOL_EV, it, "m_back"))

            @block.tensor
            def _(pe):
                with pe.Fori(0, ITERS) as it:
                    def wd(c, e):
                        pe.wait_ge(by_dve[c], value(DVE_EV, it, e))

                    def wa(c, e):
                        pe.wait_ge(by_act[c], value(ACT_EV, it, e))

                    for c in range(NC_):
                        pe.wait_ge(by_pool[c], value(POOL_EV, it, "m_back"))
                        for h in range(HC):
                            ins = pe.transpose(pa[c][:, h, :], mh[c][:, h, :], T.ident[:])
                        ins.then_inc(by_pe[c], 1)
                        for h in range(HC):
                            ins = pe.matmul(pq[c][:, h // 2, 128 * (h % 2):128 * (h % 2) + 128], mh[c][:, h, :], mh[c][:, h, :], start=True, stop=True)
                        ins.then_inc(by_pe[c], 1)
                    for c in range(NC_):
                        wa(c, "abs_gram")
                        pe.matmul(pq[c][:, 2, :], T.ones128[:], tmp[c][:].rearrange("p h j -> p (h j)"),
                                  start=True, stop=True).then_inc(by_pe[c], 1)
                    for k in range(DOUBLINGS):
                        for c in range(NC_):
                            if k == 0:
                                wd(c, "residual")
                                wa(c, "m_back_t")
                            else:
                                wd(c, "y_first" if k == 1 else f"r{k - 1}")
                                wa(c, f"r{k - 1}")
                            for h in range(HC):
                                if k < DOUBLINGS - 1:
                                    ins = pe.matmul(pa[c][:, h, :], rr[c][:, h, :], rr[c][:, h, :], start=True, stop=True)
                                if k > 0:
                                    ins = pe.matmul(pq[c][:, h // 2, 128 * (h % 2):128 * (h % 2) + 128], rr[c][:, h, :], yy[c][:, h, :],
                                                    start=True, stop=True)
                            ins.then_inc(by_pe[c], 1)
                    for c in range(NC_):
                        wd(c, "y_scaled")
                        for h in range(HC):
                            pe.matmul(pa[c][:, h, :], mt[c][:, h, :], yy[c][:, h, :], start=True, stop=True)
                            ins = pe.matmul(pq[c][:, h // 2, 128 * (h % 2):128 * (h % 2) + 128], yy[c][:, h, :], mt[c][:, h, :], start=True, stop=True)
                        ins.then_inc(by_pe[c], 1)
                    for c in range(NC_):
                        wd(c, "d_t")
                        for h in range(HC):
                            ins = pe.matmul(pq[c][:, h, 0:1], dt_[c][:, h, :], small[c][:, 2, h:h + 1], start=True, stop=True)
                        ins.then_inc(by_pe[c], 1)
                    for k in range(SQUARINGS + 1):
                        n = 1 << k
                        for c in range(NC_):
                            if k == 0:
                                wd(c, "x_first")
                            else:
                                wd(c, f"step{k - 1}")
                                wa(c, f"step{k - 1}")
                            for h in range(HC):
                                if k < SQUARINGS:
                                    pe.matmul(pa[c][:, h, :], nx[c][:, h, 0:P], dt_[c][:, h, :], start=True, stop=True)
                                a = 0 if k < SQUARINGS - 1 else P
                                ins = pe.matmul(pq[c][:, h, 0:P - a + n], dt_[c][:, h, :], nx[c][:, h, a:P + n], start=True, stop=True)
                            ins.then_inc(by_pe[c], 1)
                    for j in range(HC // 2):
                        for c in range(NC_):
                            wa(c, "c_t")
                            if j == 0:
                                wa(c, "x_last")
                                wd(c, "x_last")
                            else:
                                wd(c, "out0")
                            for e in range(2):
                                ins = pe.matmul(pk[c][64 * e:64 * e + 64, :], ct[c][:, 2 * j + e, :], nx[c][:, 2 * j + e, P:P + L],
                                                start=True, stop=True)
                            ins.then_inc(by_pe[c], 1)

            @block.vector
            def _(dve):
                dve.memset(half[:, NS:], 0.0)
                dve.memset(hb[:, NS:], 0.0)
                dve.wait_ge(const_act, 1)
                dve.tensor_scalar(half[:, 0:NS], half[:, 0:NS], 0.5, None, ALU.mult).then_inc(const_dve, 1)
                dve.wait_ge(const_dve, 1)
                dve.tensor_tensor(hb[:, 0:NS], half[:, 0:NS], bcol[:], ALU.mult).then_inc(const_dve, 1)
                dve.wait_ge(const_dve, 2)

                def small_of(it, c):
                    h0 = it * (HC * NC_) + HC * c
                    dve.tensor_scalar(small[c][:, 0, :], half[:, bass.ds(h0, HC)], -1.0, None, ALU.mult)
                    dve.tensor_scalar(small[c][:, 1, :], half[:, bass.ds(h0, HC)], T.sign[:, 0:1], None, ALU.mult)
                    dve.tensor_copy(small[c][:, 2, :], hb[:, bass.ds(h0, HC)]).then_inc(small_ready[c], 1)

                for c in range(NC_):
                    small_of(0, c)
                with dve.Fori(0, ITERS) as it:
                    def wp(c, e):
                        dve.wait_ge(by_pe[c], value(PE_EV, it, e))

                    def wa(c, e):
                        dve.wait_ge(by_act[c], value(ACT_EV, it, e))

                    def wd(c, e):
                        dve.wait_ge(by_dve[c], value(DVE_EV, it, e))

                    def bank(c):
                        return pq[c][:, 0:2, :].rearrange("p a (b j) -> p (a b) j", j=P)

                    for c in range(NC_):
                        wp(c, "colsum")
                        dve.tensor_reduce(al[c][:, 0, :], pq[c][:, 2, :].rearrange("p (h j) -> p h j", h=HC), AX.X, ALU.max).then_inc(by_dve[c], 1)
                        wd(c, "al_max")
                        dve.reciprocal(al[c][:, 1, :], al[c][:, 0, :]).then_inc(by_dve[c], 1)
                        wd(c, "alpha")
                        dve.tensor_scalar(al[c][:, 2, :], al[c][:, 1, :], -1.0, None, ALU.mult).then_inc(by_dve[c], 1)
                        wd(c, "alpha_neg")
                        for h in range(HC):
                            ins = dve.scalar_tensor_tensor(rr[c][:, h, :], bank(c)[:, h, :], al[c][:, 2, h:h + 1], T.ident[:], ALU.mult, ALU.add)
                        ins.then_inc(by_dve[c], 1)
                        wd(c, "residual")
                        dve.tensor_tensor(yy[c][:], rr[c][:], heads(T.ident[:]), ALU.add).then_inc(by_dve[c], 1)
                    for k in range(1, DOUBLINGS):
                        for c in range(NC_):
                            wp(c, f"r{k}")
                            wd(c, "y_first" if k == 1 else f"r{k - 1}")
                            dve.tensor_tensor(yy[c][:], yy[c][:], bank(c), ALU.add).then_inc(by_dve[c], 1)
                            if k == DOUBLINGS - 1:
                                wd(c, f"r{k}")
                                dve.tensor_tensor(yy[c][:], yy[c][:], al[c][:, 1, :].unsqueeze(2).broadcast_to([P, HC, P]),
                                                  ALU.mult).then_inc(by_dve[c], 1)
                    for c in range(NC_):
                        wp(c, "inverse")
                        dve.scalar_tensor_tensor(nx[c][:, :, 0:P], bank(c), 2.0, heads(T.ident[:]), ALU.mult, ALU.subtract).then_inc(by_dve[c], 1)
                        wa(c, "d_t2")
                        dve.tensor_tensor(dt_[c][:], dt_[c][:], heads(T.ident[:]), ALU.subtract).then_inc(by_dve[c], 1)
                    for c in range(NC_):
                        wp(c, "x_first")
                        dve.tensor_tensor(nx[c][:, :, P:P + 1], small[c][:, 2, :].unsqueeze(2), pq[c][:, :, 0:1], ALU.add).then_inc(by_dve[c], 1)
                    for c in range(NC_):
                        wd(c, "x_first")
                        small_of(it + 1, c)
                    for k in range(SQUARINGS):
                        for c in range(NC_):
                            wp(c, f"step{k}")
                            n = 1 << k
                            a = 0
                            if k < SQUARINGS - 1:
                                a = P
                                dve.tensor_copy(nx[c][:, :, 0:P], pq[c][:, :, 0:P])
                            dve.tensor_copy(nx[c][:, :, P + n:P + 2 * n], pq[c][:, :, a:a + n]).then_inc(by_dve[c], 1)
                    for c in range(NC_):
                        wp(c, f"step{SQUARINGS}")
                        dve.tensor_copy(nx[c][:, 0:HC // 2, P + L // 2:P + L], pq[c][:, 0:HC // 2, :]).then_inc(by_dve[c], 1)
                    for c in range(NC_):
                        wp(c, "out0")
                        dve.wait_ge(stored[c], it * (16 * HC) + 1)
                        dve.tensor_copy(ko[c][:, 0, :], pk[c][:]).then_inc(by_dve[c], 1)

            @block.scalar
            def _(act):
                act.wait_ge(loaded0, 32)
                act.activation(half[:, 0:NS], half[:, 0:NS], ACT.Exp).then_inc(const_act, 1)
                with act.Fori(0, ITERS) as it:
                    def wp(c, e):
                        act.wait_ge(by_pe[c], value(PE_EV, it, e))

                    for c in range(NC_):
                        wp(c, "transposed")
                        act.copy(mt[c][:], pa[c][:]).then_inc(by_act[c], 1)
                        wp(c, "gram")
                        gram = pq[c][:, 0:2, :].rearrange("p a (b j) -> p (a b) j", j=P)
                        act.activation(tmp[c][:], gram[:, :, 0:64], ACT.Abs).then_inc(by_act[c], 1)
                    for k in range(DOUBLINGS - 1):
                        for c in range(NC_):
                            wp(c, f"r{k}")
                            if k == 0:
                                act.wait_ge(by_dve[c], value(DVE_EV, it, "y_first"))
                            act.copy(rr[c][:], pa[c][:]).then_inc(by_act[c], 1)
                    for c in range(NC_):
                        wp(c, "inverse")
                        act.mul(dt_[c][:], pa[c][:], 2.0).then_inc(by_act[c], 1)
                    for k in range(SQUARINGS):
                        for c in range(NC_):
                            wp(c, f"step{k}")
                            act.copy(dt_[c][:], pa[c][:]).then_inc(by_act[c], 1)
                    for c in range(NC_):
                        wp(c, f"step{SQUARINGS}")
                        act.copy(nx[c][:, HC // 2:HC, P + L // 2:P + L], pq[c][:, HC // 2:HC, :]).then_inc(by_act[c], 1)
                    for c in range(NC_):
                        act.wait_ge(loaded[c], it * 64 + 64)
                        act.activation(ct[c][:], craw[c][:], ACT.Copy, scale=T.sign[:, 0:1]).then_inc(by_act[c], 1)
                    for c in range(NC_):
                        wp(c, "out1")
                        act.wait_ge(stored[c], it * (16 * HC) + 1)
                        act.copy(ko[c][:, 1, :], pk[c][:]).then_inc(by_act[c], 1)


class Pair:

    def __init__(self, turn, off):
        self.turn, self.off, self.par = turn, off, off % 2

    def at(self, a, c=0):
        return a * self.off + c if self.turn is None else self.turn * (2 * a) + (a * self.off + c)

    def half(self, a, c=0):
        return a * (self.off // 2) + c if self.turn is None else self.turn * a + (a * (self.off // 2) + c)

    def plus(self, k):
        return Pair(self.turn, self.off + k)

    def real(self):
        return self.turn is not None or 0 <= self.off < PAIRS

    def first(self):
        return self.turn is None and self.off == 0


S_MAIN = [(r, g) for r in range(R) for g in range(G)]
S_UNITS = [("main", S_MAIN[i:i + 3]) for i in range(0, len(S_MAIN), 3)] + [("rem", list(range(G))[i:i + 3]) for i in range(0, G, 3)]
E_UNITS = [(h, g) for h in range(2) for g in [G] + list(range(G))]
NSU, NEU = len(S_UNITS), len(E_UNITS)
WEIGHT = {"T1": 5, "T2": 5, "QK": 15, "F": 18, "V": 14, "Oa": 13, "O": 13, "PV0a": 11, "PV0b": 11, "PV0": 10, "PV1a": 11, "PV1b": 11, "PV1": 10}


def schedule():
    def parse(text):
        return [(w.split(".")[0], int(w.split(".")[1]) if "." in w else 0) for w in text.split()]

    even = parse("PV1a T1.0 RELOAD LOAD T1.1 PV1b T1.2 PV1 QK.0 REC1 QK.1 INV1 QKP.0 LN2Y.0 OUT1 QK.2 QKP.1 LN2P.0 QK.3 QKP.2 LN2Y.1 QK.4 QKP.3 LN2P.1 "
                 "PV0a QKP.4 QKMOVE LN2Y.2 T2.0 PV0b LN2P.2 T2.1 MP PV0 BF.0 REC0 T2.2 INV0 "
                 "BF.1 MT MMOVE OUT0 BF.2 F.0 STORE.0 F.1 STORE.1 F.2 STORE.2")
    odd = parse("PV1a LN1S.0 PV1b V.0 LN1S.1 PV1 BO.0 REC1 V.1 INV1 LN1S.2 Oa.0 LN1 OUT1 O.0 BO.1 LN1Y.0 Oa.1 O.1 LN1P.0 LN2S.0 LN1Y.1 PV0a BO.2 PV0b "
                "LN1P.1 MP LN2S.1 PV0 Oa.2 LN1Y.2 REC0 INV0 MT MMOVE O.2 LN1P.2 LN2S.2 OUT0 LN2")
    out = []
    for rest in (even, odd):
        total = sum(WEIGHT.get(kind, 0) for kind, _ in rest)
        placed, now = [], 0
        for i, step in enumerate(rest):
            now += WEIGHT.get(step[0], 0)
            placed.append((now / total, 1, i, step))
        at_max = next(at for at, _, _, (kind, _) in placed if kind == "MP")
        placed += [(at_max * k / NSU, 0, k, ("S", k)) for k in range(NSU)]
        placed += [(SPAN_E[0] + (SPAN_E[1] - SPAN_E[0]) * k / NEU, 2, k, ("E", k)) for k in range(NEU)]
        out.append([step for *_, step in sorted(placed, key=lambda x: x[:3])])
    return out


SPAN_E = (0.04, 0.97)
STEPS = schedule()
PSUM_USERS = ("T1", "T2", "QK", "F", "V", "O", "MT")
PER_PAIR = {"T1": NT, "T2": NT, "QK": R + 1, "F": NT, "V": 2, "O": NT, "MT": 2}
SHIFT = {"T1": 1, "QK": 1, "V": 1, "O": -1, "T2": -2, "F": -2}
USES = [(kind, k if kind != "MT" else (b + 1) % 2, SHIFT[kind] if kind != "MT" else (b + 1) // 2)
        for b in range(2) for kind, k in STEPS[b] if kind in PSUM_USERS]


def bank_of(kind, k):
    return next(i for i, u in enumerate(USES) if u[0] == kind and u[1] == k) % 2


def bank_before(slot, kind, k):
    at = next(i for i, u in enumerate(USES) if u[0] == kind and u[1] == k)
    for back in range(4):
        uses = [(i, u) for i, u in enumerate(USES) if i % 2 == at % 2 and (back > 0 or i < at)]
        for i, u in reversed(uses):
            pair = slot.plus(u[2] - back)
            if pair.real():
                return u[0], u[1], pair
    return None


def blocks(nc, T, h_text, hk, out):
    scratch = nc.dram_tensor("stack_scratch", (2, P, 2, 2 * R * S + 2 * S), F16).ap()
    QC = 2 * R * S
    with ExitStack() as ctx:
        sb, pb, sem = sliding(nc, ctx)
        hx = sb("h_rows", [TILE, NT, D], F32)
        hr = sb("h_again", [TILE, NT, D], F32)
        h2 = sb("h_after_attention", [TILE, NT, D], F32)
        yn2 = [sb(f"normed2_{i}", [TILE, D], F32) for i in range(2)]
        xp = {w: sb(f"normed_pieces{w}", [TILE, NT, 2, D], F16) for w in (1, 2)}
        xt = {w: sb(f"normed_t{w}", [P, 2, KB, 2 * S], F16) for w in (1, 2)}
        st = {w: sb(f"ln_stats{w}", [TILE, NT, 6], F32) for w in (1, 2)}
        mv = {w: sb(f"ln_mean_var{w}", [TILE, NT, 2], F32) for w in (1, 2)}
        ve = {w: sb(f"ln_var_eps{w}", [TILE, NT], F32) for w in (1, 2)}
        rs = {w: sb(f"ln_rstd{w}", [TILE, NT], F32) for w in (1, 2)}
        yq = [sb(f"qk_f32_{i}", [P, 2 * S], F32) for i in range(2)]
        qn = [sb(f"qk_pieces{i}", [P, 2, QC + 2 * S], F16) for i in range(2)]
        xr = [sb(f"x_rem{i}", [P, 2 * KB, G * REM], F16) for i in range(2)]
        kr = [[sb(f"k_rem{i}_{b}", [P, 2, G, REM], F16) for b in range(2)] for i in range(2)]
        vr = [[sb(f"v_rem{i}_{b}", [P, P], F32) for b in range(2)] for i in range(2)]
        mx = sb("row_max", [P, R + 1, G], F32)
        mp = sb("row_max_pieces", [P, R + 1, 2, G], F16)
        mt = sb("row_max_t", [2 * G, R, S], F16)
        pt = [sb(f"probs_t{i}", [P, G + 1, R * S], F32) for i in range(2)]
        dinv = [sb(f"row_sum_inv{i}", [P, 2 * S], F32) for i in range(2)]
        oy = [sb(f"attn_out_f32_{i}", [P, 2 * S], F32) for i in range(2)]
        ot = [sb(f"attn_out_t{i}", [P, 2, R, 2 * S], F16) for i in range(2)]
        gen = [pb(f"p_gen{i}", [P, 512]) for i in range(2)]
        psc = [pb(f"p_scores{i}", [P, 512]) for i in range(2)]
        pst = [pb(f"p_scores_t{i}", [P, 512]) for i in range(2)]
        pso = pb("p_attn_out", [P, 512])
        psd = pb("p_row_sums", [P, 512])

        h_loaded = sem("h_loaded")
        h_reloaded = sem("h_reloaded")
        out_stored = [sem(f"out_stored{k}") for k in range(NT)]
        ln_ve = {w: sem(f"ln{w}_var_ready") for w in (1, 2)}
        ln_step = {w: sem(f"ln{w}_step") for w in (1, 2)}
        ln_gate = {w: sem(f"ln{w}_stats_seen") for w in (1, 2)}
        ln_rs = {w: sem(f"ln{w}_rstd_ready") for w in (1, 2)}
        yn_ready = {w: sem(f"ln{w}_normed") for w in (1, 2)}
        hi_ready = {w: sem(f"ln{w}_hi_ready") for w in (1, 2)}
        lo_ready = {w: sem(f"ln{w}_lo_ready") for w in (1, 2)}
        bias_added = {w: sem(f"bias{w}_added") for w in (1, 2)}
        done = {k: sem(f"{k.lower()}_computed") for k in PSUM_USERS}
        taken = {k: sem(f"{k.lower()}_evacuated") for k in PSUM_USERS}
        v_rem = sem("v_rem_scaled")
        x_rem_ready = sem("x_rem_ready")
        q_hi = sem("qk_hi_ready")
        q_lo = sem("qk_lo_ready")
        spilled = [sem(f"stack_written{i}") for i in range(2)]
        stacked_exp = [sem(f"stack_exp_loaded{i}") for i in range(2)]
        stacked = [sem(f"stack_loaded{i}") for i in range(2)]
        k_rem_ready = sem("k_rem_ready")
        s_done = sem("scores_computed")
        s_max = sem("scores_maxed")
        mp_step = sem("max_piece_step")
        m_stacked = sem("max_stacked")
        e_done = sem("scores_t_computed")
        e_exp = sem("probs_ready")
        pv_done = sem("attn_out_computed")
        d_inv = sem("row_sum_inverted")
        oy_ready = sem("attn_out_normed")
        o_hi = sem("attn_hi_ready")
        o_lo = sem("attn_lo_ready")

        def normed(w, k, p):
            return hx[:, k, :] if w == 1 else yn2[(k + p.par) % 2][:]

        def gen16(kind, k):
            return gen[bank_of(kind, k)][:].bitcast(F16)

        def slots(eng, emit):
            for i in range(-2, 4):
                emit(Pair(None, i))
            with eng.Fori(2, (PAIRS - 2) // 2) as turn:
                emit(Pair(turn, 0))
                emit(Pair(turn, 1))
            for i in range(PAIRS - 2, PAIRS + 2):
                emit(Pair(None, i))

        def steps(slot):
            for b in range(2):
                for kind, k in STEPS[b]:
                    p = slot
                    bb = b
                    if kind in ("S", "MP", "MT", "MMOVE"):
                        p, bb = slot.plus((b + 1) // 2), (b + 1) % 2
                    elif kind.startswith("PV1") or kind in ("REC1", "INV1", "OUT1"):
                        p, bb = slot.plus(b - 1), (b + 1) % 2
                    elif kind in ("T1", "QK", "QKP", "QKMOVE", "V"):
                        p = slot.plus(1)
                    elif kind in ("LN1S", "LN1", "LN1Y", "LOAD") or kind == "LN1P":
                        p = slot.plus(2)
                    elif kind in ("RELOAD", "BO", "Oa", "O", "LN2S", "LN2"):
                        p = slot.plus(-1)
                    elif kind in ("LN2Y", "LN2P", "BF", "T2", "F", "STORE"):
                        p = slot.plus(-2)
                    if p.real():
                        yield kind, k, p, bb

        def h_parts(t, p):
            def at(src, b, t0, n):
                return src[bass.ds(p.at(2, b), 1), t0:t0 + n, :]
            parts = []
            edges = sorted({0, TK, S, S + TK, 2 * S} | {TILE * i for i in range(NT + 1)})
            for a, z in zip(edges, edges[1:]):
                b, tok = a // S, a % S
                src = at(hk, b, tok, z - a) if tok < TK else at(h_text, b, tok - TK, z - a)
                parts.append((t[a % TILE:a % TILE + z - a, a // TILE:a // TILE + 1, :], src.rearrange("a t d -> t a d")))
            return parts

        H_PARTS = 6

        with nc.Block() as block:
            @block.sync
            def _(sp):
                def emit(slot):
                    for kind, k, p, b in steps(slot):
                        if kind == "LOAD":
                            if not p.first():
                                sp.wait_ge(lo_ready[1], p.at(NT))
                            for dst, src in h_parts(hx, p):
                                sp.dma_start(dst, src).then_inc(h_loaded, 16)
                        elif kind == "RELOAD":
                            if not p.first():
                                sp.wait_ge(taken["O"], p.at(NT))
                            for dst, src in h_parts(hr, p):
                                sp.dma_start(dst, src).then_inc(h_reloaded, 16)
                        elif kind == "QKMOVE":
                            sp.wait_ge(q_hi, p.at(R + 1, R + 1))
                            sp.wait_ge(q_lo, p.at(R + 1, R + 1))
                            sp.dma_start(scratch[p.par], qn[p.par][:]).then_inc(spilled[p.par], 16)
                            sp.wait_ge(spilled[p.par], p.half(16, 16))
                            src = scratch[p.par].rearrange("(g d) l c -> l d g c", g=G)
                            for j in range(4):
                                rows = slice(HD * j, HD * j + HD)
                                sp.dma_start(T.qs[p.par][rows, :, :], src[j % 2, :, :, 0:QC]).then_inc(stacked[p.par], 16)
                                sp.dma_start(T.ks_max[p.par][rows, :, :], src[j // 2, :, :, QC:]).then_inc(stacked[p.par], 16)
                            for j in range(4):
                                sp.dma_start(T.ks_exp[p.par][HD * j:HD * j + HD, :, :], src[j // 2, :, :, QC:]).then_inc(stacked_exp[p.par], 16)
                        elif kind == "MMOVE":
                            sp.wait_ge(taken["MT"], p.at(2, b + 1))
                            for piece in range(2):
                                sp.dma_start(T.qs[p.par][64 + piece:65 + piece, :, R * S * b:R * S * (b + 1)],
                                             mt[G * piece:G * piece + G].rearrange("g r t -> g (r t)")).then_inc(m_stacked, 16)
                        elif kind == "STORE":
                            sp.wait_ge(taken["F"], p.at(NT, k + 1))
                            dst = out.rearrange("(q b) t d -> q (b t) d", b=2)[bass.ds(p.at(1), 1)]
                            sp.dma_start(dst[:, TILE * k:TILE * k + TILE, :].rearrange("q t d -> t q d"), h2[:, k:k + 1, :]).then_inc(out_stored[k], 16)

                slots(sp, emit)
                for k in range(NT):
                    sp.wait_ge(out_stored[k], 16 * PAIRS)

            @block.tensor
            def _(pe):
                def free_bank(slot_pair, kind, k):
                    shift = SHIFT[kind] if kind != "MT" else 1 - k
                    before = bank_before(slot_pair.plus(-shift), kind, k)
                    if before:
                        pe.wait_ge(taken[before[0]], before[2].at(PER_PAIR[before[0]], before[1] + 1))

                def emit(slot):
                    for kind, k, p, b in steps(slot):
                        if kind in ("T1", "T2"):
                            w = int(kind[1])
                            pe.wait_ge(hi_ready[w], p.at(NT, k + 1))
                            pe.wait_ge(lo_ready[w], p.at(NT, k + 1))
                            free_bank(p, kind, k)
                            for j in range(2 * KB):
                                ins = pe.transpose(gen16(kind, k)[:, TILE * j:TILE * j + TILE],
                                                   xp[w][:, k, j // KB, P * (j % KB):P * (j % KB) + P], T.ident16[0:TILE, 0:TILE])
                            ins.then_inc(done[kind], 1)
                        elif kind == "QK":
                            pe.wait_ge(taken["T1"], p.at(NT, NT))
                            free_bank(p, kind, k)
                            n = 0
                            for f in range(KB):
                                for lw, lx in ((0, 0), (0, 1), (1, 0)):
                                    ins = pe.matmul(gen[bank_of(kind, k)][:, 0:2 * S], T.wq[:, lw, f, k, :], xt[1][:, lx, f, :],
                                                    start=(n == 0), stop=(n == 3 * KB - 1))
                                    n += 1
                            ins.then_inc(done[kind], 1)
                        elif kind == "V":
                            pe.wait_ge(taken["T1"], p.at(NT, NT))
                            pe.wait_ge(x_rem_ready, p.at(2, k + 1))
                            free_bank(p, kind, k)
                            bank = gen[bank_of(kind, k)]
                            for part in range(2):
                                n = 0
                                for f in range(KB):
                                    for lx, lw in ((0, 0), (1, 0), (0, 1)):
                                        if part == 0:
                                            dst, lhs = bank[:, 0:P], xt[1][:, lx, f, S * k:S * k + P]
                                        else:
                                            dst = bank[0:G * REM, P:2 * P]
                                            lhs = xr[k][:, KB * lx + f, :]
                                        ins = pe.matmul(dst, lhs, T.wq[:, lw, f, 5, :], start=(n == 0), stop=(n == 3 * KB - 1))
                                        n += 1
                            ins.then_inc(done[kind], 1)
                        elif kind in ("Oa", "O"):
                            if kind == "Oa":
                                pe.wait_ge(o_hi, p.at(4, 4))
                                pe.wait_ge(o_lo, p.at(4, 4))
                                free_bank(p, "O", k)
                            for r in (range(0, R // 2) if kind == "Oa" else range(R // 2, R)):
                                for n, (lo_, lw) in enumerate(((0, 0), (0, 1), (1, 0))):
                                    ins = pe.matmul(gen[bank_of("O", k)][0:TILE, :], ot[p.par][:, lo_, r, TILE * k:TILE * k + TILE],
                                                    T.wo[:, lw, r, :], start=(r == 0 and n == 0), stop=(r == R - 1 and n == 2))
                            if kind == "O":
                                ins.then_inc(done["O"], 1)
                        elif kind == "F":
                            pe.wait_ge(taken["T2"], p.at(NT, k + 1))
                            free_bank(p, kind, k)
                            n = 0
                            for f in range(KB):
                                for lx in range(2):
                                    ins = pe.matmul(gen[bank_of(kind, k)][0:TILE, :], xt[2][:, lx, f, TILE * k:TILE * k + TILE],
                                                    T.wf[:, f, :], start=(n == 0), stop=(n == 2 * KB - 1))
                                    n += 1
                            ins.then_inc(done[kind], 1)
                        elif kind == "S":
                            if k == 0 and b == 0:
                                pe.wait_ge(stacked[p.par], p.half(16 * 8, 16 * 8))
                            if not (p.first() and b == 0 and k < 2):
                                pe.wait_ge(s_max, p.at(2 * NSU, NSU * b + k - 1))
                            what, tiles = S_UNITS[k]
                            ks = T.ks_max[p.par]
                            for j, tile in enumerate(tiles):
                                if what == "main":
                                    r, g = tile
                                    lhs = T.qs[p.par][0:MROWS, g, R * S * b + S * r:R * S * b + S * r + P]
                                    dst = psc[k % 2][:, S * j:S * j + S]
                                else:
                                    g = tile
                                    for r in range(R):
                                        z = R * S * b + S * (r + 1)
                                        ins = pe.matmul(psc[k % 2][32 * r:32 * r + 32, S * j:S * j + S], T.qs[p.par][0:MROWS, g, z - 32:z],
                                                        ks[0:MROWS, g, S * b:S * b + S], start=True, stop=True)
                                    continue
                                ins = pe.matmul(dst, lhs, ks[0:MROWS, g, S * b:S * b + S], start=True, stop=True)
                            ins.then_inc(s_done, 1)
                        elif kind == "MT":
                            pe.wait_ge(mp_step, p.at(4, 2 * b + 2))
                            free_bank(p, kind, b)
                            for r in range(R + 1):
                                ins = pe.transpose(gen16(kind, b)[0:2 * G, P * r:P * r + P], mp[:, r].rearrange("p l g -> p (l g)"), T.ident16[:])
                            ins.then_inc(done[kind], 1)
                        elif kind == "E":
                            h, g = E_UNITS[k]
                            if k == 0:
                                pe.wait_ge(taken["MT"], p.at(2, b + 1))
                                pe.wait_ge(k_rem_ready, p.at(2, b + 1))
                            if k == 1 and b == 0:
                                pe.wait_ge(stacked_exp[p.par], p.half(16 * 4, 16 * 4))
                            if k == 1:
                                pe.wait_ge(m_stacked, p.at(64, 32 * b + 32))
                            if not (p.first() and b == 0 and k < 2):
                                pe.wait_ge(e_exp, p.at(2 * NEU, NEU * b + k - 1))
                            c0 = R * S * b + 2 * S * h
                            if g < G:
                                ins = pe.matmul(pst[k % 2][:, 0:2 * S], T.ks_exp[p.par][0:MROWS, g, S * b:S * b + P],
                                                T.qs[p.par][0:MROWS, g, c0:c0 + 2 * S], start=True, stop=True)
                            else:
                                dst = pst[k % 2][0:G * REM, 0:2 * S]
                                for n, (lk, lq) in enumerate(((0, 0), (0, 1), (1, 0), (1, 1))):
                                    pe.matmul(dst, kr[p.par][b][:, lk].rearrange("p g t -> p (g t)"), qn[p.par][:, lq, c0:c0 + 2 * S],
                                              start=(n == 0), stop=False)
                                ins = pe.matmul(dst, T.rem_select[:], mt[:].rearrange("p r t -> p (r t)")[:, 2 * S * h:2 * S * h + 2 * S],
                                                start=False, stop=True)
                            ins.then_inc(e_done, 1)
                        elif kind[0:2] == "PV":
                            h = int(kind[2])
                            if kind.endswith("a"):
                                pe.wait_ge(e_exp, p.at(2 * NEU, NEU * b + (G + 1) * (h + 1)))
                                pe.wait_ge(taken["V"], p.at(2, b + 1))
                                if not (p.first() and b == 0 and h == 0):
                                    pe.wait_ge(oy_ready, p.at(4, 2 * b + h))
                            cols = slice(2 * S * h, 2 * S * h + 2 * S)
                            if kind[3:]:
                                parity = "ab".index(kind[3])
                                for q in range(G // 2):
                                    rows = slice(32 * q, 32 * q + 32)
                                    pe.matmul(pso[rows, 0:2 * S], T.v_pad[p.par][:, b, parity, rows], pt[b][:, 2 * q + parity, cols],
                                              start=(parity == 0), stop=False, skip_group_check=True)
                                for q in range(G // 2):
                                    rows = slice(32 * q, 32 * q + 32)
                                    pe.matmul(psd[rows, 0:2 * S], T.ones_half[:, parity, :], pt[b][:, 2 * q + parity, cols],
                                              start=(parity == 0), stop=False, skip_group_check=True)
                            else:
                                probs = pt[b][0:G * REM, G, cols]
                                pe.matmul(psd[:, 0:2 * S], T.rem_mask[0:G * REM, :], probs, start=False, stop=True,
                                          skip_group_check=True)
                                pe.matmul(pso[:, 0:2 * S], vr[p.par][b][0:G * REM, :], probs, start=False, stop=True,
                                          skip_group_check=True).then_inc(pv_done, 1)

                slots(pe, emit)

            @block.scalar
            def _(act):
                def emit(slot):
                    for kind, k, p, b in steps(slot):
                        if kind == "QK":
                            act.wait_ge(done["QK"], p.at(R + 1, k + 1))
                            if not (p.first() and k < 2):
                                act.wait_ge(q_hi, p.at(R + 1, k - 1))
                                act.wait_ge(q_lo, p.at(R + 1, k - 1))
                            act.activation(yq[k % 2 if p.par == 0 else (k + 1) % 2][:], gen[bank_of(kind, k)][:, 0:2 * S], ACT.Identity,
                                           bias=T.bq[:, k:k + 1], scale=T.f_qkv[:, 0:1]).then_inc(taken["QK"], 1)
                        elif kind == "QKMOVE":
                            act.wait_ge(taken["T1"], p.at(NT, NT))
                            if not p.first():
                                act.wait_ge(done["V"], p.at(2))
                            for bb in range(2):
                                src = xt[1][:, :, :, S * bb + P:S * bb + S].rearrange("p l f t -> p (l f) t").unsqueeze(2)
                                act.copy(xr[bb][:].rearrange("p x (g t) -> p x g t", g=G),
                                         src.broadcast_to([P, 2 * KB, G, REM])).then_inc(x_rem_ready, 1)
                        elif kind == "E":
                            h, g = E_UNITS[k]
                            act.wait_ge(e_done, p.at(2 * NEU, NEU * b + k + 1))
                            if k in (0, G + 1) and not p.first():
                                act.wait_ge(pv_done, p.at(4, 2 * b - 4 + h + 1))
                            rows = P if g < G else G * REM
                            act.activation(pt[b][0:rows, g, 2 * S * h:2 * S * h + 2 * S], pst[k % 2][0:rows, 0:2 * S], ACT.Exp,
                                           scale=T.f_exp[0:rows, 0:1]).then_inc(e_exp, 1)
                        elif kind in ("LN1P", "LN2P"):
                            w = int(kind[2])
                            act.wait_ge(yn_ready[w], p.at(NT, k + 1))
                            if not p.first():
                                act.wait_ge(done[f"T{w}"], p.at(NT, k - NT + 1))
                            act.copy(xp[w][:, k, 0, :], normed(w, k, p)).then_inc(hi_ready[w], 1)
                        elif kind in ("OUT0", "OUT1"):
                            k = int(kind[3])
                            act.wait_ge(oy_ready, p.at(4, 2 * b + k + 1))
                            if not (p.turn is None and p.off < 2) and b == 0 and k == 0:
                                act.wait_ge(done["O"], p.at(NT, -NT))
                            act.copy(ot[p.par][:, 0, 2 * k:2 * k + 2, S * b:S * b + S],
                                     oy[k][:].rearrange("p (r t) -> p r t", r=2)).then_inc(o_hi, 1)

                slots(act, emit)

            @block.gpsimd
            def _(pool):
                def emit(slot):
                    for kind, k, p, b in steps(slot):
                        if kind in ("LN1", "LN2"):
                            w = int(kind[2])
                            pool.wait_ge(ln_ve[w], p.at(1, 1))
                            pool.tensor_tensor(rs[w][:], ve[w][:], T.minus_half[0:TILE, 0:NT], ALU.pow).then_inc(ln_rs[w], 1)
                        elif kind in ("LN1P", "LN2P"):
                            w = int(kind[2])
                            pool.wait_ge(hi_ready[w], p.at(NT, k + 1))
                            pool.tensor_tensor(xp[w][:, k, 1, :], normed(w, k, p), xp[w][:, k, 0, :],
                                               ALU.subtract).then_inc(lo_ready[w], 1)
                        elif kind == "BF":
                            pool.wait_ge(yn_ready[2], p.at(NT, k + 1))
                            pool.tensor_tensor(h2[:, k, :], h2[:, k, :], T.bf[0:TILE], ALU.add).then_inc(bias_added[2], 1)
                        elif kind == "BO":
                            pool.wait_ge(h_reloaded, p.at(16 * H_PARTS, 16 * H_PARTS))
                            pool.tensor_tensor(hr[:, k, :], hr[:, k, :], T.bo[0:TILE], ALU.add).then_inc(bias_added[1], 1)
                        elif kind == "QKP":
                            pool.wait_ge(q_hi, p.at(R + 1, k + 1))
                            y = yq[k % 2 if p.par == 0 else (k + 1) % 2][:]
                            if k < R:
                                view = lambda l: qn[p.par][:, l, 0:QC].rearrange("p (b r t) -> p b r t", b=2, r=R)[:, :, k, :]
                                y = y.rearrange("p (b t) -> p b t", b=2)
                            else:
                                view = lambda l: qn[p.par][:, l, QC:]
                            pool.tensor_tensor(view(1), y, view(0), ALU.subtract).then_inc(q_lo, 1)
                        elif kind == "QKMOVE":
                            pool.wait_ge(q_lo, p.at(R + 1, R + 1))
                            if not (p.turn is None and p.off < 2):
                                pool.wait_ge(e_done, p.at(2 * NEU, -2 * NEU))
                            for bb in range(2):
                                for l in range(2):
                                    src = qn[p.par][:, l, QC + S * bb + P:QC + S * bb + S].unsqueeze(1).broadcast_to([P, G, REM])
                                    ins = pool.tensor_tensor(kr[p.par][bb][:, l], src, T.group_mask[:].unsqueeze(2).broadcast_to([P, G, REM]), ALU.mult)
                                ins.then_inc(k_rem_ready, 1)
                        elif kind in ("OUT0", "OUT1"):
                            k = int(kind[3])
                            pool.wait_ge(o_hi, p.at(4, 2 * b + k + 1))
                            view = lambda l: ot[p.par][:, l, 2 * k:2 * k + 2, S * b:S * b + S]
                            pool.tensor_tensor(view(1), oy[k][:].rearrange("p (r t) -> p r t", r=2), view(0), ALU.subtract).then_inc(o_lo, 1)

                slots(pool, emit)

            @block.vector
            def _(dve):
                def emit(slot):
                    for kind, k, p, b in steps(slot):
                        if kind in ("LN1S", "LN2S"):
                            w = int(kind[2])
                            src = hx if w == 1 else h2
                            if w == 1:
                                dve.wait_ge(h_loaded, p.at(16 * H_PARTS, 16 * H_PARTS))
                            else:
                                dve.wait_ge(taken["O"], p.at(NT, k + 1))
                            ins = dve.bn_stats(st[w][:, k, :], src[:, k, :])
                            if k == NT - 1:
                                ins.then_inc(ln_step[w], 1)
                        elif kind in ("LN1", "LN2"):
                            w = int(kind[2])
                            dve.wait_ge(ln_step[w], p.at(2, 1))
                            dve.sem_inc(ln_gate[w], 1)
                            for t in range(NT):
                                ins = dve.bn_aggr(mv[w][:, t, :], st[w][:, t, :])
                            ins.then_inc(ln_step[w], 1)
                            dve.wait_ge(ln_step[w], p.at(2, 2))
                            dve.tensor_scalar(ve[w][:], mv[w][:, :, 1], EPS, LN_SCALE ** -2, ALU.add, ALU.mult).then_inc(ln_ve[w], 1)
                        elif kind in ("LN1Y", "LN2Y"):
                            w = int(kind[2])
                            src = hx if w == 1 else h2
                            if k == 0:
                                dve.wait_ge(ln_rs[w], p.at(1, 1))
                            if w == 2 and not (p.first() and k < 2):
                                dve.wait_ge(lo_ready[w], p.at(NT, k - 1))
                            dve.tensor_scalar(normed(w, k, p), src[:, k, :], mv[w][:, k, 0:1], rs[w][:, k:k + 1],
                                              ALU.subtract, ALU.mult).then_inc(yn_ready[w], 1)
                        elif kind in ("T1", "T2"):
                            w = int(kind[1])
                            dve.wait_ge(done[kind], p.at(NT, k + 1))
                            if not p.first() and k == 0:
                                if w == 1:
                                    dve.wait_ge(done["V"], p.at(2))
                                else:
                                    dve.wait_ge(done["F"], p.at(NT))
                            dve.tensor_copy(xt[w][:, :, :, TILE * k:TILE * k + TILE],
                                            gen16(kind, k)[:, 0:2 * KB * TILE].rearrange("p (l f t) -> p l f t", l=2, f=KB)).then_inc(taken[kind], 1)
                        elif kind == "QKP":
                            dve.wait_ge(taken["QK"], p.at(R + 1, k + 1))
                            if k == 0 and not (p.turn is None and p.off < 2):
                                dve.wait_ge(spilled[p.par], p.half(16))
                                dve.wait_ge(e_done, p.at(2 * NEU, -2 * NEU))
                                dve.wait_ge(k_rem_ready, p.at(2, -2))
                            y = yq[k % 2 if p.par == 0 else (k + 1) % 2][:]
                            if k < R:
                                dst = qn[p.par][:, 0, 0:QC].rearrange("p (b r t) -> p b r t", b=2, r=R)[:, :, k, :]
                                y = y.rearrange("p (b t) -> p b t", b=2)
                            else:
                                dst = qn[p.par][:, 0, QC:]
                            dve.tensor_copy(dst, y).then_inc(q_hi, 1)
                        elif kind == "V":
                            dve.wait_ge(done["V"], p.at(2, k + 1))
                            if not (p.turn is None and p.off < 2):
                                dve.wait_ge(pv_done, p.at(4, 2 * k - 8 + 2))
                            bank = gen[bank_of(kind, k)]
                            for parity in range(2):
                                view = lambda ap: ap.rearrange("p (q e d) -> p q e d", e=2, d=HD)[:, :, parity, :]
                                dve.scalar_tensor_tensor(view(T.v_pad[p.par][:, k, parity, :]), view(bank[:, 0:P]), T.f_qkv[:, 0:1], view(T.bv[:]),
                                                         ALU.mult, ALU.add)
                            rr = slice(0, G * REM)
                            dve.scalar_tensor_tensor(vr[p.par][k][rr, :], bank[rr, P:2 * P], T.f_qkv[rr, 0:1], T.rem_mask[rr, :],
                                                     ALU.mult, ALU.mult).then_inc(v_rem, 1)
                            dve.wait_ge(v_rem, p.at(2, k + 1))
                            dve.tensor_tensor(vr[p.par][k][rr, :], vr[p.par][k][rr, :], T.bv_rem[rr, :], ALU.add).then_inc(taken["V"], 1)
                        elif kind == "O":
                            dve.wait_ge(done["O"], p.at(NT, k + 1))
                            dve.wait_ge(bias_added[1], p.at(NT, k + 1))
                            if not p.first():
                                dve.wait_ge(out_stored[k], p.at(16))
                            dve.scalar_tensor_tensor(h2[:, k, :], gen[bank_of(kind, k)][0:TILE, :], T.f_out[0:TILE, 0:1], hr[:, k, :],
                                                     ALU.mult, ALU.add).then_inc(taken["O"], 1)
                        elif kind == "F":
                            dve.wait_ge(done["F"], p.at(NT, k + 1))
                            dve.wait_ge(bias_added[2], p.at(NT, k + 1))
                            dve.scalar_tensor_tensor(h2[:, k, :], gen[bank_of(kind, k)][0:TILE, :], T.f_ffn[0:TILE, 0:1], h2[:, k, :],
                                                     ALU.mult, ALU.add).then_inc(taken["F"], 1)
                        elif kind == "S":
                            what, tiles = S_UNITS[k]
                            dve.wait_ge(s_done, p.at(2 * NSU, NSU * b + k + 1))
                            n = len(tiles)
                            j0 = 3 * k if what == "main" else R * G + tiles[0]
                            dve.tensor_reduce(mx[:].rearrange("p r g -> p (r g)")[:, j0:j0 + n],
                                              psc[k % 2][:, 0:S * n].rearrange("p (j t) -> p j t", j=n), AX.X, ALU.max).then_inc(s_max, 1)
                        elif kind == "MP":
                            dve.wait_ge(s_max, p.at(2 * NSU, NSU * (b + 1)))
                            if not (p.first() and b == 0):
                                dve.wait_ge(done["MT"], p.at(2, b))
                            dve.tensor_scalar(mp[:, :, 0, :], mx[:], -1.0 / NEG, None, ALU.mult).then_inc(mp_step, 1)
                            dve.wait_ge(mp_step, p.at(4, 2 * b + 1))
                            dve.scalar_tensor_tensor(mp[:, :, 1, :], mx[:], -1.0 / NEG, mp[:, :, 0, :], ALU.mult, ALU.subtract).then_inc(mp_step, 1)
                        elif kind == "MT":
                            dve.wait_ge(done["MT"], p.at(2, b + 1))
                            if not (p.first() and b == 0):
                                dve.wait_ge(m_stacked, p.at(64, 32 * b))
                                dve.wait_ge(e_done, p.at(2 * NEU, NEU * b - NEU + G + 2))
                            ps = gen16(kind, b)
                            dve.tensor_copy(mt[:, :, 0:P], ps[0:2 * G, 0:P * R].rearrange("p (r t) -> p r t", r=R))
                            dve.tensor_copy(mt[:, :, P:S], ps[0:2 * G, P * R:P * R + P].rearrange("p (r t) -> p r t", r=R)[:, :, 32 - REM:32]).then_inc(taken["MT"], 1)
                        elif kind in ("PV0", "PV1"):
                            k = int(kind[2])
                            dve.wait_ge(pv_done, p.at(4, 2 * b + k + 1))
                            dve.reciprocal(dinv[k][:, 0:TILE], psd[:, 0:TILE])
                        elif kind in ("REC0", "REC1"):
                            k = int(kind[3])
                            dve.reciprocal(dinv[k][:, TILE:2 * TILE], psd[:, TILE:2 * TILE])
                        elif kind in ("INV0", "INV1"):
                            k = int(kind[3])
                            dve.reciprocal(dinv[k][:, 2 * TILE:2 * S], psd[:, 2 * TILE:2 * S]).then_inc(d_inv, 1)
                            dve.wait_ge(d_inv, p.at(4, 2 * b + k + 1))
                            if not (p.first() and b == 0):
                                dve.wait_ge(o_lo, p.at(4, 2 * b + k - 1))
                            dve.tensor_tensor(oy[k][:], pso[:, 0:2 * S], dinv[k][:], ALU.mult).then_inc(oy_ready, 1)

                slots(dve, emit)


class Tiles:
    pass


def fusion_kernel(nc, c_t, txt, a_t, b_t, log_dt, wq_t, bqk_t, bv_row, wo_t, b_out, wf_t, b_ffn, out):
    hk = nc.dram_tensor("kernel_tokens", (B, TK, D), F32).ap()
    with ExitStack() as ctx:
        sb, _, _ = sliding(nc, ctx)
        T = Tiles()
        T.ident = sb("ident", [P, P], F32)
        T.ident16 = sb("ident16", [P, P], F16)
        T.ones128 = sb("ones128", [P, P], F32)
        T.sign = sb("sign", [P, 1], F32)
        T.unit_block = sb("unit_block", [P, 64], F32)
        T.group_mask = sb("group_mask", [P, G], F32)
        T.rem_mask = sb("rem_mask", [P, P], F32)
        T.rem_select = sb("rem_select", [2 * G, G * REM], F16)
        T.ones_half = sb("ones_half", [P, 2, 32], F32)
        T.minus_half = sb("minus_half", [P, NT], F32)
        T.wq = sb("wq_t", [P, 2, KB, 6, P], F16)
        T.wo = sb("wo_t", [P, 2, R, D], F16)
        T.wf = sb("wf_t", [P, KB, D], F16)
        T.bq = sb("bq", [P, R + 1], F32)
        T.bv = sb("bv", [P, P], F32)
        T.bv_rem = sb("bv_rem", [P, P], F32)
        T.bo = sb("bo", [P, D], F32)
        T.bf = sb("bf", [P, D], F32)
        T.c_wq, T.c_wo, T.c_b = sb("c_wq", [P, 1], F32), sb("c_wo", [P, 1], F32), sb("c_b", [P, 1], F32)
        T.f_qkv, T.f_out = sb("f_qkv", [P, 1], F32), sb("f_out", [P, 1], F32)
        T.f_exp, T.f_ffn = sb("f_exp", [P, 1], F32), sb("f_ffn", [P, 1], F32)
        T.qs = [sb(f"q_stack{i}", [MROWS, G, 2 * R * S], F16) for i in range(2)]
        T.ks_max = [sb(f"k_stack_max{i}", [MROWS, G, 2 * S], F16) for i in range(2)]
        T.ks_exp = [sb(f"k_stack_exp{i}", [MROWS, G, 2 * S], F16) for i in range(2)]
        T.v_pad = [sb(f"v_pad{i}", [P, 2, 2, P], F32) for i in range(2)]
        constants_and_weights(nc, T, wq_t, bqk_t, bv_row, wo_t, b_out, wf_t, b_ffn)
        state_space_kernel(nc, T, hk, c_t, a_t, b_t, log_dt)
        blocks(nc, T, txt, hk, out)


def laid_out(i):
    w, b = i["L0_attn_w_qkv"], i["L0_attn_b_qkv"]
    wq = w[:D].reshape(G, R, HD, D).transpose(3, 1, 0, 2).reshape(D, R * P)
    bq = b[:D].reshape(G, R, HD).transpose(0, 2, 1).reshape(P, R)
    return {
        "c_t": i["x"].transpose(3, 2, 1, 0).reshape(2 * NS, NS, B),
        "txt": i["txt"],
        "a_t": i["L0_tok_A"].transpose(1, 3, 0, 2),
        "b_t": i["L0_tok_B"].transpose(2, 1, 0).reshape(2 * NS, NS),
        "log_dt": i["L0_tok_log_dt"].reshape(NS),
        "wq_t": np.concatenate([wq, w[D:].T], axis=1),
        "bqk_t": np.concatenate([bq, b[D:D + P].reshape(P, 1)], axis=1),
        "bv": b[D + P:],
        "wo_t": i["L0_attn_w_out"].reshape(D, G, R, HD).transpose(1, 3, 2, 0).reshape(P, R, D),
        "b_out": i["L0_attn_b_out"],
        "wf_t": i["L0_ffn_weight"].T,
        "b_ffn": i["L0_ffn_bias"],
    }


def kernel(**inputs):
    import concourse.bacc as _bacc
    from concourse.bass_utils import run_bass_kernel_spmd as _run

    nc = _bacc.Bacc("TRN2", target_bir_lowering=False, num_devices=1)
    arrays, args = {}, []
    for name, a in laid_out({k: np.asarray(v) for k, v in inputs.items()}).items():
        arrays[f"in_{name}"] = np.ascontiguousarray(a)
        args.append(nc.dram_tensor(f"in_{name}", a.shape, mybir.dt.from_np(a.dtype), kind="ExternalInput").ap())
    args.append(nc.dram_tensor("out_h", (B, S, D), F32, kind="ExternalOutput").ap())
    fusion_kernel(nc, *args)
    return _run(nc, [arrays], core_ids=[0]).results[0]["out_h"]
```

```python
from contextlib import ExitStack

import concourse.bass as bass
import numpy as np
from concourse import mybir

F32 = mybir.dt.float32
F16 = mybir.dt.float16
I32 = mybir.dt.int32
ALU = mybir.AluOpType
ACT = mybir.ActivationFunctionType
AX = mybir.AxisListType

P = 128
B, TK, TT, D = 64, 64, 77, 512
S = TK + TT
NS, L = 64, 512
G, R, HD = 8, 4, 16
KB = D // P
EPS = 1e-5
LN_SCALE = 1024.0
PAIRS = B // 2
TILE = 94
NT = 2 * S // TILE
REM = S - P
MROWS = 96
NEG = -32768.0
DOUBLINGS = 6
SQUARINGS = 8
HC = 4


def sliding(nc, ctx):
    def sb(name, shape, dt):
        return ctx.enter_context(nc.sbuf_tensor(name, shape, dt))

    def pb(name, shape, dt=F32):
        return ctx.enter_context(nc.psum_tensor(name, shape, dt))

    def sem(name):
        return ctx.enter_context(nc.semaphore(name))

    return sb, pb, sem


def state_space_kernel(nc, T, hk, c_t, a_t, b_t, log_dt, wq_t, bqk_t, bv_row, wo_t, b_out, wf_t, b_ffn):
    NC_ = 2
    ITERS = NS // (HC * NC_)
    with ExitStack() as ctx:
        sb, pb, sem = sliding(nc, ctx)
        raw = [sb(f"a_raw{c}", [P, 2, HC, NS], F32) for c in range(NC_)]
        craw = [sb(f"c_raw{c}", [P, HC, NS], F32) for c in range(NC_)]
        mh = [sb(f"m_back{c}", [P, HC, P], F32) for c in range(NC_)]
        mt = [sb(f"m_back_t{c}", [P, HC, P], F32) for c in range(NC_)]
        tmp = [sb(f"abs_gram{c}", [P, HC, 64], F32) for c in range(NC_)]
        rr = [sb(f"residual{c}", [P, HC, P], F32) for c in range(NC_)]
        yy = [sb(f"inverse_sum{c}", [P, HC, P], F32) for c in range(NC_)]
        dt_ = [sb(f"step_t{c}", [P, HC, P], F32) for c in range(NC_)]
        nx = [sb(f"step_krylov{c}", [P, HC, P + L], F32) for c in range(NC_)]
        ct = [sb(f"c_t{c}", [P, HC, NS], F32) for c in range(NC_)]
        small = [sb(f"half_steps{c}", [P, 3, HC], F32) for c in range(NC_)]
        al = [sb(f"alpha{c}", [P, 3, HC], F32) for c in range(NC_)]
        ko = [sb(f"k_out{c}", [P, HC // 2, L], F32) for c in range(NC_)]
        wq = sb("wq_raw", [P, KB, 6 * P], F32)
        wo = sb("wo_raw", [P, R, D], F32)
        wf = sb("wf_raw", [P, KB, D], F32)
        wneg = sb("wf_negative", [P, KB, D], F32)
        bqk = sb("bqk_raw", [P, R + 1], F32)
        bv = sb("bv_raw", [P, P], F32)
        parts = sb("w_reduced_parts", [P, 3, KB], F32)
        red = sb("w_reduced", [P, 4], F32)
        tot = sb("w_total", [P, 4], F32)
        wsc = sb("w_scalars", [P, 16], F32)
        bcol = sb("b_columns", [P, NS], F32)
        half = sb("half_step", [P, NS], F32)
        hb = sb("half_step_b", [P, NS], F32)
        pa = [pb(f"s_pa{c}", [P, HC, 128]) for c in range(NC_)]
        pq = [pb(f"s_pq{c}", [P, HC, 256]) for c in range(NC_)]
        pk = [pb(f"s_pk{c}", [P, 512]) for c in range(NC_)]

        w_loaded = sem("w_loaded")
        consts = sem("w_consts")
        w_parts = sem("w_parts_reduced")
        reduced = sem("w_reduced_ready")
        total = sem("w_total_ready")
        chain = sem("w_scalar_step")
        hi_ready = sem("w_hi_ready")
        loaded0 = sem("s_const_loaded")
        const_dve = sem("s_const_dve")
        const_act = sem("s_const_act")
        a_loaded = [sem(f"s_a_loaded{c}") for c in range(NC_)]
        c_loaded = [sem(f"s_c_loaded{c}") for c in range(NC_)]
        out_by_pe = [sem(f"s_out_by_pe{c}") for c in range(NC_)]
        out_by_act = [sem(f"s_out_by_act{c}") for c in range(NC_)]
        stored = [sem(f"s_stored{c}") for c in range(NC_)]
        by_pe = [sem(f"s_by_pe{c}") for c in range(NC_)]
        by_dve = [sem(f"s_by_dve{c}") for c in range(NC_)]
        by_act = [sem(f"s_by_act{c}") for c in range(NC_)]
        small_ready = [sem(f"s_half_steps_ready{c}") for c in range(NC_)]
        by_pool = [sem(f"s_by_pool{c}") for c in range(NC_)]

        PE_EV = (["transposed", "gram", "colsum"] + [f"r{k}" for k in range(DOUBLINGS)] + ["inverse", "x_first"]
                 + [f"step{k}" for k in range(SQUARINGS + 1)])
        DVE_EV = (["al_max", "alpha", "alpha_neg", "residual", "y_first"] + [f"r{k}" for k in range(1, DOUBLINGS)] + ["y_scaled", "d", "d_t", "x_first"]
                  + [f"step{k}" for k in range(SQUARINGS)] + ["x_last"])
        ACT_EV = (["m_back_t", "abs_gram"] + [f"r{k}" for k in range(DOUBLINGS - 1)] + ["d_t2"]
                  + ["c_t"] + [f"step{k}" for k in range(SQUARINGS)] + ["x_last"])
        POOL_EV = ["half_a", "m_back"]

        def value(events, it, event):
            return it * len(events) + (events.index(event) + 1)

        def heads(ap):
            return ap.unsqueeze(1).broadcast_to([P, HC, P])

        with nc.Block() as block:
            @block.sync
            def _(sp):
                sp.dma_start(half[:, 0:NS], log_dt.partition_broadcast(P)).then_inc(loaded0, 16)
                sp.dma_start(bcol[:], b_t).then_inc(loaded0, 16)
                for c in range(NC_):
                    sp.sem_inc(stored[c], 1)

                def load_a(it, c):
                    src = a_t[:, :, bass.ds(it * (HC * NC_) + HC * c, HC), :]
                    sp.dma_start(raw[c][0:64], src).then_inc(a_loaded[c], 16)
                    for part in range(2):
                        sp.dma_start(raw[c][64:128, part:part + 1], src[:, 1 - part:2 - part]).then_inc(a_loaded[c], 16)

                def load_c(it, c):
                    sp.dma_start(craw[c][:], c_t[:, bass.ds(it * (HC * NC_) + HC * c, HC), :]).then_inc(c_loaded[c], 16)

                def store(it, c, j):
                    for e in range(2):
                        sp.dma_start(hk[:, bass.ds(it * (HC * NC_) + HC * c + 2 * j + e, 1), :],
                                     ko[c][64 * e:64 * e + 64, j:j + 1, :]).then_inc(stored[c], 16)

                for c in range(NC_):
                    load_a(0, c)
                    load_c(0, c)
                sp.dma_start(wq[:], wq_t.rearrange("(m p) c -> p m c", p=P)).then_inc(w_loaded, 16)
                sp.dma_start(wo[:], wo_t).then_inc(w_loaded, 16)
                sp.dma_start(wf[:], wf_t.rearrange("(m p) o -> p m o", p=P)).then_inc(w_loaded, 16)
                sp.dma_start(bqk[:], bqk_t).then_inc(w_loaded, 16)
                sp.dma_start(bv[:], bv_row.partition_broadcast(P)).then_inc(w_loaded, 16)
                sp.dma_start(T.bo[:], b_out.partition_broadcast(P)).then_inc(w_loaded, 16)
                sp.dma_start(T.bf[:], b_ffn.partition_broadcast(P)).then_inc(w_loaded, 16)
                with sp.Fori(0, ITERS - 1) as it:
                    for c in range(NC_):
                        sp.wait_ge(by_pool[c], value(POOL_EV, it, "m_back"))
                        load_a(it + 1, c)
                    for c in range(NC_):
                        sp.wait_ge(by_act[c], value(ACT_EV, it, "c_t"))
                        load_c(it + 1, c)
                    for j in range(HC // 2):
                        for c in range(NC_):
                            sp.wait_ge(out_by_act[c], it * (HC // 2) + j + 1)
                            store(it, c, j)
                for j in range(HC // 2):
                    for c in range(NC_):
                        sp.wait_ge(out_by_act[c], (ITERS - 1) * (HC // 2) + j + 1)
                        store(ITERS - 1, c, j)
                for c in range(NC_):
                    sp.wait_ge(stored[c], 16 * HC * ITERS + 1)

            @block.gpsimd
            def _(pool):
                n = [0]

                def step(ins):
                    n[0] += 1
                    ins.then_inc(consts, 1)
                    pool.wait_ge(consts, n[0])

                def keep_within(ap, pattern, width):
                    step(pool.affine_select(out=ap, in_=ap, compare_op=ALU.is_ge, fill=0.0, base=0,
                                            pattern=[[-a, c] for a, c in pattern], channel_multiplier=1))
                    step(pool.affine_select(out=ap, in_=ap, compare_op=ALU.is_ge, fill=0.0, base=width - 1,
                                            pattern=pattern, channel_multiplier=-1))

                def build(it):
                    for c in range(NC_):
                        pool.wait_ge(a_loaded[c], it * 48 + 48)
                        pool.wait_ge(small_ready[c], it + 1)
                        pool.tensor_tensor(raw[c][:], raw[c][:], small[c][:, 0:2, :].unsqueeze(3).broadcast_to([P, 2, HC, NS]),
                                           ALU.mult).then_inc(by_pool[c], 1)
                        pool.wait_ge(by_pool[c], value(POOL_EV, it, "half_a"))
                        pool.tensor_tensor(mh[c][:].rearrange("p h (t j) -> p t h j", t=2), raw[c][:],
                                           T.ident[:].rearrange("p (t j) -> p t j", t=2).unsqueeze(2).broadcast_to([P, 2, HC, NS]),
                                           ALU.add).then_inc(by_pool[c], 1)
                        pool.wait_ge(by_pool[c], value(POOL_EV, it, "m_back"))

                step(pool.memset(T.sign[0:64], 1.0))
                step(pool.memset(T.sign[64:128], -1.0))
                step(pool.memset(T.ident[:], 0.0))
                step(pool.affine_select(out=T.ident[:], in_=T.ident[:], compare_op=ALU.not_equal, fill=1.0, base=0,
                                        pattern=[[-1, P]], channel_multiplier=1))
                step(pool.memset(T.ones128[:], 1.0))
                build(0)
                step(pool.memset(T.rem_mask[:], 1.0))
                keep_within(T.rem_mask[:].rearrange("p (g d) -> p g d", g=G), [[REM, G], [0, HD]], REM)
                step(pool.tensor_copy(T.ident16[:], T.ident[:]))
                step(pool.memset(T.group_mask[:], 1.0))
                keep_within(T.group_mask[:], [[HD, G]], HD)
                step(pool.memset(T.rem_select[:], 0.0))
                for piece in range(2):
                    v = T.rem_select[:].rearrange("p (g t) -> p g t", g=G)
                    step(pool.affine_select(out=v, in_=v, compare_op=ALU.not_equal, fill=NEG, base=-G * piece,
                                            pattern=[[-1, G], [0, REM]], channel_multiplier=1))
                for parity in range(2):
                    step(pool.memset(T.ones_half[:, parity], 0.0))
                    step(pool.memset(T.ones_half[:, parity, HD * parity:HD * parity + HD], 1.0))
                step(pool.memset(T.minus_half[:], -0.5))
                for par in range(2):
                    step(pool.memset(T.v_pad[par][:], 0.0))
                    step(pool.memset(T.qs[par][64:MROWS], 0.0))
                    step(pool.memset(T.ks_max[par][64:MROWS], 0.0))
                    step(pool.memset(T.ks_exp[par][64:MROWS], 0.0))
                    step(pool.memset(T.ks_exp[par][64:66], NEG))
                with pool.Fori(1, ITERS) as it:
                    build(it)
                pool.wait_ge(reduced, 4)
                pool.partition_all_reduce(tot[:, 0:2], red[:, 0:2], P, bass.bass_isa.ReduceOp.max).then_inc(total, 1)
                pool.partition_all_reduce(tot[:, 2:3], red[:, 2:3], P, bass.bass_isa.ReduceOp.add).then_inc(total, 1)
                pool.partition_all_reduce(tot[:, 3:4], red[:, 3:4], P, bass.bass_isa.ReduceOp.max).then_inc(total, 1)

            @block.tensor
            def _(pe):
                def out(it, j):
                    for c in range(NC_):
                        if j == 0:
                            pe.wait_ge(by_act[c], value(ACT_EV, it, "x_last"))
                            pe.wait_ge(by_dve[c], value(DVE_EV, it, "x_last"))
                        else:
                            pe.wait_ge(out_by_act[c], it * (HC // 2) + j)
                        for e in range(2):
                            ins = pe.matmul(pk[c][64 * e:64 * e + 64, :], ct[c][:, 2 * j + e, :], nx[c][:, 2 * j + e, P:P + L],
                                            start=True, stop=True)
                        ins.then_inc(out_by_pe[c], 1)

                def iteration(it, first):
                    def wd(c, e):
                        pe.wait_ge(by_dve[c], value(DVE_EV, it, e))

                    def wa(c, e):
                        pe.wait_ge(by_act[c], value(ACT_EV, it, e))

                    for c in range(NC_):
                        pe.wait_ge(by_pool[c], value(POOL_EV, it, "m_back"))
                        for h in range(HC):
                            ins = pe.transpose(pa[c][:, h, :], mh[c][:, h, :], T.ident[:])
                        ins.then_inc(by_pe[c], 1)
                        if not first:
                            pe.wait_ge(by_act[c], value(ACT_EV, it - 1, "x_last"))
                            pe.wait_ge(by_dve[c], value(DVE_EV, it - 1, "x_last"))
                        for h in range(HC):
                            ins = pe.matmul(pq[c][:, h // 2, 128 * (h % 2):128 * (h % 2) + 128], mh[c][:, h, :], mh[c][:, h, :], start=True, stop=True)
                        ins.then_inc(by_pe[c], 1)
                    if not first:
                        out(it - 1, 0)
                    for c in range(NC_):
                        wa(c, "abs_gram")
                        pe.matmul(pq[c][:, 2, :], T.ones128[:], tmp[c][:].rearrange("p h j -> p (h j)"),
                                  start=True, stop=True).then_inc(by_pe[c], 1)
                    if not first:
                        out(it - 1, 1)
                    for k in range(DOUBLINGS):
                        for c in range(NC_):
                            if k == 0:
                                wd(c, "residual")
                                wa(c, "m_back_t")
                            else:
                                wd(c, "y_first" if k == 1 else f"r{k - 1}")
                                wa(c, f"r{k - 1}")
                            for h in range(HC):
                                if k < DOUBLINGS - 1:
                                    ins = pe.matmul(pa[c][:, h, :], rr[c][:, h, :], rr[c][:, h, :], start=True, stop=True)
                                if k > 0:
                                    ins = pe.matmul(pq[c][:, h // 2, 128 * (h % 2):128 * (h % 2) + 128], rr[c][:, h, :], yy[c][:, h, :],
                                                    start=True, stop=True)
                            ins.then_inc(by_pe[c], 1)
                    for c in range(NC_):
                        wd(c, "y_scaled")
                        for h in range(HC):
                            pe.matmul(pa[c][:, h, :], mt[c][:, h, :], yy[c][:, h, :], start=True, stop=True)
                            ins = pe.matmul(pq[c][:, h // 2, 128 * (h % 2):128 * (h % 2) + 128], yy[c][:, h, :], mt[c][:, h, :], start=True, stop=True)
                        ins.then_inc(by_pe[c], 1)
                    for c in range(NC_):
                        wd(c, "d_t")
                        for h in range(HC):
                            ins = pe.matmul(pq[c][:, h, 0:1], dt_[c][:, h, :], small[c][:, 2, h:h + 1], start=True, stop=True)
                        ins.then_inc(by_pe[c], 1)
                    for k in range(SQUARINGS + 1):
                        n = 1 << k
                        for c in range(NC_):
                            if k == 0:
                                wd(c, "x_first")
                            else:
                                wd(c, f"step{k - 1}")
                                wa(c, f"step{k - 1}")
                            for h in range(HC):
                                if k < SQUARINGS:
                                    pe.matmul(pa[c][:, h, :], nx[c][:, h, 0:P], dt_[c][:, h, :], start=True, stop=True)
                                a = 0 if k < SQUARINGS - 1 else P
                                ins = pe.matmul(pq[c][:, h, 0:P - a + n], dt_[c][:, h, :], nx[c][:, h, a:P + n], start=True, stop=True)
                            ins.then_inc(by_pe[c], 1)

                iteration(0, True)
                with pe.Fori(1, ITERS) as it:
                    iteration(it, False)
                for j in range(HC // 2):
                    out(ITERS - 1, j)

            @block.vector
            def _(dve):
                dve.wait_ge(const_act, 1)
                dve.tensor_scalar(half[:, 0:NS], half[:, 0:NS], 0.5, None, ALU.mult).then_inc(const_dve, 1)
                dve.wait_ge(const_dve, 1)
                dve.tensor_tensor(hb[:, 0:NS], half[:, 0:NS], bcol[:], ALU.mult).then_inc(const_dve, 1)
                dve.wait_ge(const_dve, 2)

                def small_of(it, c):
                    h0 = it * (HC * NC_) + HC * c
                    dve.tensor_scalar(small[c][:, 0, :], half[:, bass.ds(h0, HC)], -1.0, None, ALU.mult)
                    dve.tensor_scalar(small[c][:, 1, :], half[:, bass.ds(h0, HC)], T.sign[:, 0:1], None, ALU.mult)
                    dve.tensor_copy(small[c][:, 2, :], hb[:, bass.ds(h0, HC)]).then_inc(small_ready[c], 1)

                dve.wait_ge(consts, 2)
                for c in range(NC_):
                    small_of(0, c)

                n = [0]

                def step(ins):
                    n[0] += 1
                    ins.then_inc(chain, 1)
                    dve.wait_ge(chain, n[0])

                def reductions():
                    dve.wait_ge(w_loaded, 16 * 7)
                    for i, w in enumerate((wq, wo, wf)):
                        for f in range(KB):
                            dve.tensor_reduce(parts[:, i, f:f + 1], w[:, f, :], AX.X, ALU.add if w is wf else ALU.max,
                                              apply_absolute_value=True).then_inc(w_parts, 1)
                            yield
                    step(dve.tensor_reduce(wsc[:, 0:1], bqk[:], AX.X, ALU.max, apply_absolute_value=True))
                    step(dve.tensor_reduce(wsc[:, 1:2], bv[:], AX.X, ALU.max, apply_absolute_value=True))
                    yield
                    dve.wait_ge(w_parts, 3 * KB)
                    dve.tensor_reduce(red[:, 0:2], parts[:, 0:2, :], AX.X, ALU.max).then_inc(reduced, 2)
                    dve.tensor_reduce(red[:, 2:3], parts[:, 2, :], AX.X, ALU.add).then_inc(reduced, 1)
                    dve.tensor_reduce(red[:, 3:4], wsc[:, 0:2], AX.X, ALU.max).then_inc(reduced, 1)
                    yield

                def scales_and_pieces():
                    dve.wait_ge(total, 3)
                    step(dve.tensor_copy(wsc[:, 0:2], tot[:, 0:2]))
                    step(dve.scalar_tensor_tensor(wsc[:, 2:3], tot[:, 0:1], float(D), tot[:, 3:4], ALU.mult, ALU.add))
                    step(dve.tensor_scalar(wsc[:, 0:3], wsc[:, 0:3], 2.0 ** -60, 2.0 ** 60, ALU.max, ALU.min))
                    yield

                    def bits(a, b):
                        return wsc[:, a:b].bitcast(I32)

                    step(dve.tensor_scalar(bits(4, 7), bits(0, 3), 0x7F800000, None, ALU.bitwise_and))
                    step(dve.tensor_scalar(bits(8, 11), bits(4, 7), -1.0, float(254 << 23), ALU.mult, ALU.add))
                    step(dve.tensor_scalar(T.c_wq[:], wsc[:, 8:9], 2.0 ** 14, None, ALU.mult))
                    step(dve.tensor_scalar(T.c_wo[:], wsc[:, 9:10], 2.0 ** 14, None, ALU.mult))
                    yield
                    step(dve.tensor_scalar(T.c_b[:], wsc[:, 10:11], 2.0 ** 12, None, ALU.mult))
                    step(dve.tensor_scalar(wsc[:, 12:13], wsc[:, 4:5], 2.0 ** -14 / LN_SCALE, None, ALU.mult))
                    step(dve.tensor_tensor(T.f_qkv[:], wsc[:, 12:13], T.c_b[:], ALU.mult))
                    yield
                    step(dve.tensor_scalar(wsc[:, 13:14], wsc[:, 5:6], 2.0 ** -14, None, ALU.mult))
                    step(dve.tensor_scalar(wsc[:, 14:15], wsc[:, 6:7], 2.0 ** -12, None, ALU.mult))
                    step(dve.tensor_tensor(T.f_out[:], wsc[:, 13:14], wsc[:, 14:15], ALU.mult))
                    yield
                    step(dve.scalar_tensor_tensor(T.f_exp[:], wsc[:, 14:15], HD ** -0.5, wsc[:, 14:15], ALU.mult, ALU.mult))
                    step(dve.tensor_scalar(T.bq[:], bqk[:], T.c_b[:, 0:1], None, ALU.mult))
                    step(dve.tensor_scalar(T.bv[:], bv[:], T.c_b[:, 0:1], None, ALU.mult))
                    yield
                    dve.wait_ge(consts, 8)
                    step(dve.tensor_tensor(T.bv_rem[:], T.bv[:], T.rem_mask[:], ALU.mult))
                    step(dve.tensor_scalar(wsc[:, 15:16], tot[:, 2:3], 1.0 / (D * D), None, ALU.mult))
                    step(dve.tensor_scalar(T.f_ffn[:], wsc[:, 15:16], 1.0 / LN_SCALE, None, ALU.mult))
                    yield
                    step(dve.tensor_scalar(wsc[:, 3:4], wsc[:, 15:16], 1e-10, 0.5, ALU.add, ALU.mult))
                    step(dve.tensor_scalar(wsc[:, 7:8], wsc[:, 3:4], -1.0, None, ALU.mult))
                    yield
                    for f in range(KB):
                        step(dve.tensor_scalar(wneg[:, f, :], wf[:, f, :], wsc[:, 7:8], None, ALU.is_lt))
                        dve.scalar_tensor_tensor(T.wf[:, f, :], wf[:, f, :], wsc[:, 3:4], wneg[:, f, :], ALU.is_gt, ALU.subtract)
                        yield
                    for f in range(KB):
                        dve.wait_ge(hi_ready, 2 * f + 1)
                        dve.scalar_tensor_tensor(T.wq[:, 1, f].rearrange("p m c -> p (m c)"), wq[:, f, :], T.c_wq[:, 0:1],
                                                 T.wq[:, 0, f].rearrange("p m c -> p (m c)"), ALU.mult, ALU.subtract)
                        yield
                        dve.wait_ge(hi_ready, 2 * f + 2)
                        dve.scalar_tensor_tensor(T.wo[:, 1, f, :], wo[:, f, :], T.c_wo[:, 0:1], T.wo[:, 0, f, :], ALU.mult, ALU.subtract)
                        yield

                def iteration(it, between, last):
                    def wp(c, e):
                        dve.wait_ge(by_pe[c], value(PE_EV, it, e))

                    def wa(c, e):
                        dve.wait_ge(by_act[c], value(ACT_EV, it, e))

                    def wd(c, e):
                        dve.wait_ge(by_dve[c], value(DVE_EV, it, e))

                    def bank(c):
                        return pq[c][:, 0:2, :].rearrange("p a (b j) -> p (a b) j", j=P)

                    for c in range(NC_):
                        wp(c, "colsum")
                        dve.tensor_reduce(al[c][:, 0, :], pq[c][:, 2, :].rearrange("p (h j) -> p h j", h=HC), AX.X, ALU.max).then_inc(by_dve[c], 1)
                        wd(c, "al_max")
                        dve.reciprocal(al[c][:, 1, :], al[c][:, 0, :]).then_inc(by_dve[c], 1)
                        wd(c, "alpha")
                        dve.tensor_scalar(al[c][:, 2, :], al[c][:, 1, :], -1.0, None, ALU.mult).then_inc(by_dve[c], 1)
                        wd(c, "alpha_neg")
                        for h in range(HC):
                            ins = dve.scalar_tensor_tensor(rr[c][:, h, :], bank(c)[:, h, :], al[c][:, 2, h:h + 1], T.ident[:], ALU.mult, ALU.add)
                        ins.then_inc(by_dve[c], 1)
                        wd(c, "residual")
                        dve.tensor_tensor(yy[c][:], rr[c][:], heads(T.ident[:]), ALU.add).then_inc(by_dve[c], 1)
                    for k in range(1, DOUBLINGS):
                        for c in range(NC_):
                            wp(c, f"r{k}")
                            wd(c, "y_first" if k == 1 else f"r{k - 1}")
                            dve.tensor_tensor(yy[c][:], yy[c][:], bank(c), ALU.add).then_inc(by_dve[c], 1)
                            next(between, None)
                            if k == DOUBLINGS - 1:
                                wd(c, f"r{k}")
                                dve.tensor_tensor(yy[c][:], yy[c][:], al[c][:, 1, :].unsqueeze(2).broadcast_to([P, HC, P]),
                                                  ALU.mult).then_inc(by_dve[c], 1)
                    for c in range(NC_):
                        wp(c, "inverse")
                        dve.scalar_tensor_tensor(nx[c][:, :, 0:P], bank(c), 2.0, heads(T.ident[:]), ALU.mult, ALU.subtract).then_inc(by_dve[c], 1)
                        wa(c, "d_t2")
                        dve.tensor_tensor(dt_[c][:], dt_[c][:], heads(T.ident[:]), ALU.subtract).then_inc(by_dve[c], 1)
                    for c in range(NC_):
                        wp(c, "x_first")
                        dve.tensor_tensor(nx[c][:, :, P:P + 1], small[c][:, 2, :].unsqueeze(2), pq[c][:, :, 0:1], ALU.add).then_inc(by_dve[c], 1)
                    for c in range(0 if last else NC_):
                        wd(c, "x_first")
                        small_of(it + 1, c)
                    for k in range(SQUARINGS):
                        for c in range(NC_):
                            wp(c, f"step{k}")
                            n = 1 << k
                            a = 0
                            if k < SQUARINGS - 1:
                                a = P
                                dve.tensor_copy(nx[c][:, :, 0:P], pq[c][:, :, 0:P])
                            dve.tensor_copy(nx[c][:, :, P + n:P + 2 * n], pq[c][:, :, a:a + n]).then_inc(by_dve[c], 1)
                            next(between, None)
                    for c in range(NC_):
                        wp(c, f"step{SQUARINGS}")
                        dve.tensor_copy(nx[c][:, 0:HC // 2, P + L // 2:P + L], pq[c][:, 0:HC // 2, :]).then_inc(by_dve[c], 1)
                    for _ in between:
                        pass

                iteration(0, reductions(), False)
                with dve.Fori(1, ITERS - 1) as it:
                    iteration(it, iter(()), False)
                iteration(ITERS - 1, scales_and_pieces(), True)

            @block.scalar
            def _(act):
                act.wait_ge(loaded0, 32)
                act.activation(half[:, 0:NS], half[:, 0:NS], ACT.Exp).then_inc(const_act, 1)

                def out(it):
                    for j in range(HC // 2):
                        for c in range(NC_):
                            act.wait_ge(out_by_pe[c], it * (HC // 2) + j + 1)
                            act.wait_ge(stored[c], it * (16 * HC) + 1)
                            act.copy(ko[c][:, j, :], pk[c][:]).then_inc(out_by_act[c], 1)

                def high_pieces():
                    for f in range(KB):
                        if f == 0:
                            act.wait_ge(chain, 9)
                        act.activation(T.wq[:, 0, f].rearrange("p m c -> p (m c)"), wq[:, f, :], ACT.Copy,
                                       scale=T.c_wq[:, 0:1]).then_inc(hi_ready, 1)
                        yield
                        act.activation(T.wo[:, 0, f, :], wo[:, f, :], ACT.Copy, scale=T.c_wo[:, 0:1]).then_inc(hi_ready, 1)
                        yield

                def iteration(it, first, between):
                    def wp(c, e):
                        act.wait_ge(by_pe[c], value(PE_EV, it, e))

                    for c in range(NC_):
                        wp(c, "transposed")
                        act.copy(mt[c][:], pa[c][:]).then_inc(by_act[c], 1)
                        wp(c, "gram")
                        gram = pq[c][:, 0:2, :].rearrange("p a (b j) -> p (a b) j", j=P)
                        act.activation(tmp[c][:], gram[:, :, 0:64], ACT.Abs).then_inc(by_act[c], 1)
                    if not first:
                        out(it - 1)
                    for k in range(DOUBLINGS - 1):
                        for c in range(NC_):
                            wp(c, f"r{k}")
                            if k == 0:
                                act.wait_ge(by_dve[c], value(DVE_EV, it, "y_first"))
                            act.copy(rr[c][:], pa[c][:]).then_inc(by_act[c], 1)
                    for c in range(NC_):
                        wp(c, "inverse")
                        act.mul(dt_[c][:], pa[c][:], 2.0).then_inc(by_act[c], 1)
                    for c in range(NC_):
                        act.wait_ge(c_loaded[c], it * 16 + 16)
                        act.activation(ct[c][:], craw[c][:], ACT.Copy, scale=T.sign[:, 0:1]).then_inc(by_act[c], 1)
                    for k in range(SQUARINGS):
                        for c in range(NC_):
                            wp(c, f"step{k}")
                            act.copy(dt_[c][:], pa[c][:]).then_inc(by_act[c], 1)
                            next(between, None)
                    for c in range(NC_):
                        wp(c, f"step{SQUARINGS}")
                        act.copy(nx[c][:, HC // 2:HC, P + L // 2:P + L], pq[c][:, HC // 2:HC, :]).then_inc(by_act[c], 1)

                iteration(0, True, iter(()))
                with act.Fori(1, ITERS - 1) as it:
                    iteration(it, False, iter(()))
                iteration(ITERS - 1, False, high_pieces())
                out(ITERS - 1)


class Pair:

    def __init__(self, turn, off):
        self.turn, self.off, self.par = turn, off, off % 2

    def at(self, a, c=0):
        return a * self.off + c if self.turn is None else self.turn * (2 * a) + (a * self.off + c)

    def half(self, a, c=0):
        return a * (self.off // 2) + c if self.turn is None else self.turn * a + (a * (self.off // 2) + c)

    def plus(self, k):
        return Pair(self.turn, self.off + k)

    def real(self):
        return self.turn is not None or 0 <= self.off < PAIRS

    def first(self):
        return self.turn is None and self.off == 0


S_MAIN = [(r, g) for r in range(R) for g in range(G)]
S_UNITS = [("main", S_MAIN[i:i + 3]) for i in range(0, len(S_MAIN), 3)] + [("rem", list(range(G))[i:i + 3]) for i in range(0, G, 3)]
E_UNITS = [(h, g) for h in range(2) for g in [G] + list(range(G))]
NSU, NEU = len(S_UNITS), len(E_UNITS)
WEIGHT = {"T1": 5, "T2": 5, "QK": 15, "F": 18, "V": 14, "Oa": 13, "O": 13, "PV0a": 11, "PV0b": 11, "PV0": 10, "PV1a": 11, "PV1b": 11, "PV1": 10}


def schedule():
    def parse(text):
        return [(w.split(".")[0], int(w.split(".")[1]) if "." in w else 0) for w in text.split()]

    even = parse("PV1a T1.0 RELOAD LOAD T1.1 PV1b T1.2 PV1 QK.0 REC1 LN2Y.0 QK.1 INV1 QKP.0 LN2P.0 OUT1 QK.2 LN2Y.1 QKP.1 QK.3 QKP.2 LN2P.1 QK.4 LN2Y.2 QKP.3 "
                 "PV0a QKP.4 QKMOVE LN2P.2 PV0b T2.0 MP T2.1 PV0 BF.0 T2.2 MT MMOVE REC0 BF.1 INV0 "
                 "BF.2 F.0 OUT0 STORE.0 F.1 STORE.1 F.2 STORE.2")
    odd = parse("PV1a LN1S.0 PV1b V.0 LN1S.1 PV1 BO.0 REC1 V.1 INV1 LN1S.2 Oa.0 LN1 OUT1 O.0 BO.1 LN1Y.0 Oa.1 O.1 LN1P.0 LN2S.0 LN1Y.1 PV0a BO.2 PV0b "
                "LN1P.1 MP LN2S.1 PV0 Oa.2 LN1Y.2 REC0 INV0 MT MMOVE O.2 LN1P.2 LN2S.2 OUT0 LN2")
    out = []
    for rest in (even, odd):
        total = sum(WEIGHT.get(kind, 0) for kind, _ in rest)
        placed, now = [], 0
        for i, step in enumerate(rest):
            now += WEIGHT.get(step[0], 0)
            placed.append((now / total, 1, i, step))
        at_max = next(at for at, _, _, (kind, _) in placed if kind == "MP")
        placed += [(0.02 + (at_max - 0.02) * k / NSU, 0, k, ("S", k)) for k in range(NSU)]
        placed += [(SPAN_E[0] + (SPAN_E[1] - SPAN_E[0]) * k / NEU, 2, k, ("E", k)) for k in range(NEU)]
        out.append([step for *_, step in sorted(placed, key=lambda x: x[:3])])
    return out


SPAN_E = (0.08, 0.98)
STEPS = schedule()
PSUM_USERS = ("T1", "T2", "QK", "F", "V", "O", "MT")
PER_PAIR = {"T1": NT, "T2": NT, "QK": R + 1, "F": NT, "V": 2, "O": NT, "MT": 2}
SHIFT = {"T1": 1, "QK": 1, "V": 1, "O": -1, "T2": -2, "F": -2}
USES = [(kind, k if kind != "MT" else (b + 1) % 2, SHIFT[kind] if kind != "MT" else (b + 1) // 2)
        for b in range(2) for kind, k in STEPS[b] if kind in PSUM_USERS]


def bank_of(kind, k):
    return next(i for i, u in enumerate(USES) if u[0] == kind and u[1] == k) % 2


def bank_before(slot, kind, k):
    at = next(i for i, u in enumerate(USES) if u[0] == kind and u[1] == k)
    for back in range(4):
        uses = [(i, u) for i, u in enumerate(USES) if i % 2 == at % 2 and (back > 0 or i < at)]
        for i, u in reversed(uses):
            pair = slot.plus(u[2] - back)
            if pair.real():
                return u[0], u[1], pair
    return None


def blocks(nc, T, h_text, hk, out):
    scratch = nc.dram_tensor("stack_scratch", (2, P, 2, 2 * R * S + 2 * S), F16).ap()
    QC = 2 * R * S
    with ExitStack() as ctx:
        sb, pb, sem = sliding(nc, ctx)
        hx = sb("h_rows", [TILE, NT, D], F32)
        hr = sb("h_again", [TILE, NT, D], F32)
        h2 = sb("h_after_attention", [TILE, NT, D], F32)
        yn2 = [sb(f"normed2_{i}", [TILE, D], F32) for i in range(2)]
        xp = {w: sb(f"normed_pieces{w}", [TILE, NT, 2, D], F16) for w in (1, 2)}
        xt = {w: sb(f"normed_t{w}", [P, 2, KB, 2 * S], F16) for w in (1, 2)}
        st = {w: sb(f"ln_stats{w}", [TILE, NT, 6], F32) for w in (1, 2)}
        mv = {w: sb(f"ln_mean_var{w}", [TILE, NT, 2], F32) for w in (1, 2)}
        ve = {w: sb(f"ln_var_eps{w}", [TILE, NT], F32) for w in (1, 2)}
        rs = {w: sb(f"ln_rstd{w}", [TILE, NT], F32) for w in (1, 2)}
        yq = [sb(f"qk_f32_{i}", [P, 2 * S], F32) for i in range(2)]
        qn = [sb(f"qk_pieces{i}", [P, 2, QC + 2 * S], F16) for i in range(2)]
        xr = [sb(f"x_rem{i}", [P, 2 * KB, G * REM], F16) for i in range(2)]
        kr = [[sb(f"k_rem{i}_{b}", [P, 2, G, REM], F16) for b in range(2)] for i in range(2)]
        vr = [[sb(f"v_rem{i}_{b}", [P, P], F32) for b in range(2)] for i in range(2)]
        mx = sb("row_max", [P, R + 1, G], F32)
        mp = sb("row_max_pieces", [P, R + 1, 2, G], F16)
        mt = sb("row_max_t", [2 * G, R, S], F16)
        pt = [sb(f"probs_t{i}", [P, G + 1, R * S], F32) for i in range(2)]
        dinv = [sb(f"row_sum_inv{i}", [P, 2 * S], F32) for i in range(2)]
        oy = [sb(f"attn_out_f32_{i}", [P, 2 * S], F32) for i in range(2)]
        ot = [sb(f"attn_out_t{i}", [P, 2, R, 2 * S], F16) for i in range(2)]
        gen = [pb(f"p_gen{i}", [P, 512]) for i in range(2)]
        psc = [pb(f"p_scores{i}", [P, 512]) for i in range(2)]
        pst = [pb(f"p_scores_t{i}", [P, 512]) for i in range(2)]
        pso = pb("p_attn_out", [P, 512])
        psd = pb("p_row_sums", [P, 512])

        h_loaded = sem("h_loaded")
        h_reloaded = sem("h_reloaded")
        out_stored = [sem(f"out_stored{k}") for k in range(NT)]
        ln_ve = {w: sem(f"ln{w}_var_ready") for w in (1, 2)}
        ln_step = {w: sem(f"ln{w}_step") for w in (1, 2)}
        ln_gate = {w: sem(f"ln{w}_stats_seen") for w in (1, 2)}
        ln_rs = {w: sem(f"ln{w}_rstd_ready") for w in (1, 2)}
        yn_ready = {w: sem(f"ln{w}_normed") for w in (1, 2)}
        hi_ready = {w: sem(f"ln{w}_hi_ready") for w in (1, 2)}
        lo_ready = {w: sem(f"ln{w}_lo_ready") for w in (1, 2)}
        bias_added = {w: sem(f"bias{w}_added") for w in (1, 2)}
        done = {k: sem(f"{k.lower()}_computed") for k in PSUM_USERS}
        taken = {k: sem(f"{k.lower()}_evacuated") for k in PSUM_USERS}
        v_rem = sem("v_rem_scaled")
        x_rem_ready = sem("x_rem_ready")
        q_hi = sem("qk_hi_ready")
        q_lo = sem("qk_lo_ready")
        spilled = [sem(f"stack_written{i}") for i in range(2)]
        stacked_exp = [sem(f"stack_exp_loaded{i}") for i in range(2)]
        stacked = [sem(f"stack_loaded{i}") for i in range(2)]
        k_rem_ready = sem("k_rem_ready")
        s_done = sem("scores_computed")
        s_max = sem("scores_maxed")
        mp_step = sem("max_piece_step")
        m_stacked = sem("max_stacked")
        e_done = sem("scores_t_computed")
        e_exp = sem("probs_ready")
        pv_done = sem("attn_out_computed")
        d_inv = sem("row_sum_inverted")
        oy_ready = sem("attn_out_normed")
        o_hi = sem("attn_hi_ready")
        o_lo = sem("attn_lo_ready")

        def normed(w, k, p):
            return hx[:, k, :] if w == 1 else yn2[(k + p.par) % 2][:]

        def gen16(kind, k):
            return gen[bank_of(kind, k)][:].bitcast(F16)

        def slots(eng, emit):
            for i in range(-2, 4):
                emit(Pair(None, i))
            with eng.Fori(2, (PAIRS - 2) // 2) as turn:
                emit(Pair(turn, 0))
                emit(Pair(turn, 1))
            for i in range(PAIRS - 2, PAIRS + 2):
                emit(Pair(None, i))

        def steps(slot):
            for b in range(2):
                for kind, k in STEPS[b]:
                    p = slot
                    bb = b
                    if kind in ("S", "MP", "MT", "MMOVE"):
                        p, bb = slot.plus((b + 1) // 2), (b + 1) % 2
                    elif kind.startswith("PV1") or kind in ("REC1", "INV1", "OUT1"):
                        p, bb = slot.plus(b - 1), (b + 1) % 2
                    elif kind in ("T1", "QK", "QKP", "QKMOVE", "V"):
                        p = slot.plus(1)
                    elif kind in ("LN1S", "LN1", "LN1Y", "LN1P", "LOAD"):
                        p = slot.plus(2)
                    elif kind in ("RELOAD", "BO", "Oa", "O", "LN2S", "LN2"):
                        p = slot.plus(-1)
                    elif kind in ("LN2Y", "LN2P", "BF", "T2", "F", "STORE"):
                        p = slot.plus(-2)
                    if p.real():
                        yield kind, k, p, bb

        def h_parts(t, p):
            def at(src, b, t0, n):
                return src[bass.ds(p.at(2, b), 1), t0:t0 + n, :]
            parts = []
            edges = sorted({0, TK, S, S + TK, 2 * S} | {TILE * i for i in range(NT + 1)})
            for a, z in zip(edges, edges[1:]):
                b, tok = a // S, a % S
                src = at(hk, b, tok, z - a) if tok < TK else at(h_text, b, tok - TK, z - a)
                parts.append((t[a % TILE:a % TILE + z - a, a // TILE:a // TILE + 1, :], src.rearrange("a t d -> t a d")))
            return parts

        H_PARTS = 6

        with nc.Block() as block:
            @block.sync
            def _(sp):
                def emit(slot):
                    for kind, k, p, b in steps(slot):
                        if kind == "LOAD":
                            if not p.first():
                                sp.wait_ge(lo_ready[1], p.at(NT))
                            for dst, src in h_parts(hx, p):
                                sp.dma_start(dst, src).then_inc(h_loaded, 16)
                        elif kind == "RELOAD":
                            if not p.first():
                                sp.wait_ge(taken["O"], p.at(NT))
                            for dst, src in h_parts(hr, p):
                                sp.dma_start(dst, src).then_inc(h_reloaded, 16)
                        elif kind == "QKMOVE":
                            sp.wait_ge(q_hi, p.at(R + 1, R + 1))
                            sp.wait_ge(q_lo, p.at(R + 1, R + 1))
                            sp.dma_start(scratch[p.par], qn[p.par][:]).then_inc(spilled[p.par], 16)
                            sp.wait_ge(spilled[p.par], p.half(16, 16))
                            src = scratch[p.par].rearrange("(g d) l c -> l d g c", g=G)
                            for j in range(4):
                                rows = slice(HD * j, HD * j + HD)
                                sp.dma_start(T.qs[p.par][rows, :, :], src[j % 2, :, :, 0:QC]).then_inc(stacked[p.par], 16)
                                sp.dma_start(T.ks_max[p.par][rows, :, :], src[j // 2, :, :, QC:]).then_inc(stacked[p.par], 16)
                            for j in range(4):
                                sp.dma_start(T.ks_exp[p.par][HD * j:HD * j + HD, :, :], src[j // 2, :, :, QC:]).then_inc(stacked_exp[p.par], 16)
                        elif kind == "MMOVE":
                            sp.wait_ge(taken["MT"], p.at(2, b + 1))
                            for piece in range(2):
                                sp.dma_start(T.qs[p.par][64 + piece:65 + piece, :, R * S * b:R * S * (b + 1)],
                                             mt[G * piece:G * piece + G].rearrange("g r t -> g (r t)")).then_inc(m_stacked, 16)
                        elif kind == "STORE":
                            sp.wait_ge(taken["F"], p.at(NT, k + 1))
                            dst = out.rearrange("(q b) t d -> q (b t) d", b=2)[bass.ds(p.at(1), 1)]
                            sp.dma_start(dst[:, TILE * k:TILE * k + TILE, :].rearrange("q t d -> t q d"), h2[:, k:k + 1, :]).then_inc(out_stored[k], 16)

                slots(sp, emit)
                for k in range(NT):
                    sp.wait_ge(out_stored[k], 16 * PAIRS)

            @block.tensor
            def _(pe):
                def free_bank(slot_pair, kind, k):
                    shift = SHIFT[kind] if kind != "MT" else 1 - k
                    before = bank_before(slot_pair.plus(-shift), kind, k)
                    if before:
                        pe.wait_ge(taken[before[0]], before[2].at(PER_PAIR[before[0]], before[1] + 1))

                def emit(slot):
                    for kind, k, p, b in steps(slot):
                        if kind in ("T1", "T2"):
                            w = int(kind[1])
                            pe.wait_ge(hi_ready[w], p.at(NT, k + 1))
                            pe.wait_ge(lo_ready[w], p.at(NT, k + 1))
                            free_bank(p, kind, k)
                            for j in range(2 * KB):
                                ins = pe.transpose(gen16(kind, k)[:, TILE * j:TILE * j + TILE],
                                                   xp[w][:, k, j // KB, P * (j % KB):P * (j % KB) + P], T.ident16[0:TILE, 0:TILE])
                            ins.then_inc(done[kind], 1)
                        elif kind == "QK":
                            pe.wait_ge(taken["T1"], p.at(NT, NT))
                            free_bank(p, kind, k)
                            n = 0
                            for f in range(KB):
                                for lw, lx in ((0, 0), (0, 1), (1, 0)):
                                    ins = pe.matmul(gen[bank_of(kind, k)][:, 0:2 * S], T.wq[:, lw, f, k, :], xt[1][:, lx, f, :],
                                                    start=(n == 0), stop=(n == 3 * KB - 1))
                                    n += 1
                            ins.then_inc(done[kind], 1)
                        elif kind == "V":
                            pe.wait_ge(taken["T1"], p.at(NT, NT))
                            pe.wait_ge(x_rem_ready, p.at(2, k + 1))
                            free_bank(p, kind, k)
                            bank = gen[bank_of(kind, k)]
                            for part in range(2):
                                n = 0
                                for f in range(KB):
                                    for lx, lw in ((0, 0), (1, 0), (0, 1)):
                                        if part == 0:
                                            dst, lhs = bank[:, 0:P], xt[1][:, lx, f, S * k:S * k + P]
                                        else:
                                            dst = bank[0:G * REM, P:2 * P]
                                            lhs = xr[k][:, KB * lx + f, :]
                                        ins = pe.matmul(dst, lhs, T.wq[:, lw, f, 5, :], start=(n == 0), stop=(n == 3 * KB - 1))
                                        n += 1
                            ins.then_inc(done[kind], 1)
                        elif kind in ("Oa", "O"):
                            if kind == "Oa":
                                pe.wait_ge(o_hi, p.at(4, 4))
                                pe.wait_ge(o_lo, p.at(4, 4))
                                free_bank(p, "O", k)
                            for r in (range(0, R // 2) if kind == "Oa" else range(R // 2, R)):
                                for n, (lo_, lw) in enumerate(((0, 0), (0, 1), (1, 0))):
                                    ins = pe.matmul(gen[bank_of("O", k)][0:TILE, :], ot[p.par][:, lo_, r, TILE * k:TILE * k + TILE],
                                                    T.wo[:, lw, r, :], start=(r == 0 and n == 0), stop=(r == R - 1 and n == 2))
                            if kind == "O":
                                ins.then_inc(done["O"], 1)
                        elif kind == "F":
                            pe.wait_ge(taken["T2"], p.at(NT, k + 1))
                            free_bank(p, kind, k)
                            n = 0
                            for f in range(KB):
                                for lx in range(2):
                                    ins = pe.matmul(gen[bank_of(kind, k)][0:TILE, :], xt[2][:, lx, f, TILE * k:TILE * k + TILE],
                                                    T.wf[:, f, :], start=(n == 0), stop=(n == 2 * KB - 1))
                                    n += 1
                            ins.then_inc(done[kind], 1)
                        elif kind == "S":
                            if k == 0 and b == 0:
                                pe.wait_ge(stacked[p.par], p.half(16 * 8, 16 * 8))
                            if not (p.first() and b == 0 and k < 2):
                                pe.wait_ge(s_max, p.at(2 * NSU, NSU * b + k - 1))
                            what, tiles = S_UNITS[k]
                            ks = T.ks_max[p.par]
                            for j, tile in enumerate(tiles):
                                if what == "main":
                                    r, g = tile
                                    lhs = T.qs[p.par][0:MROWS, g, R * S * b + S * r:R * S * b + S * r + P]
                                    dst = psc[k % 2][:, S * j:S * j + S]
                                else:
                                    g = tile
                                    for r in range(R):
                                        z = R * S * b + S * (r + 1)
                                        ins = pe.matmul(psc[k % 2][32 * r:32 * r + 32, S * j:S * j + S], T.qs[p.par][0:MROWS, g, z - 32:z],
                                                        ks[0:MROWS, g, S * b:S * b + S], start=True, stop=True)
                                    continue
                                ins = pe.matmul(dst, lhs, ks[0:MROWS, g, S * b:S * b + S], start=True, stop=True)
                            ins.then_inc(s_done, 1)
                        elif kind == "MT":
                            pe.wait_ge(mp_step, p.at(4, 2 * b + 2))
                            free_bank(p, kind, b)
                            for r in range(R + 1):
                                ins = pe.transpose(gen16(kind, b)[0:2 * G, P * r:P * r + P], mp[:, r].rearrange("p l g -> p (l g)"), T.ident16[:])
                            ins.then_inc(done[kind], 1)
                        elif kind == "E":
                            h, g = E_UNITS[k]
                            if k == 0:
                                pe.wait_ge(taken["MT"], p.at(2, b + 1))
                                pe.wait_ge(k_rem_ready, p.at(2, b + 1))
                            if k == 1 and b == 0:
                                pe.wait_ge(stacked_exp[p.par], p.half(16 * 4, 16 * 4))
                            if k == 1:
                                pe.wait_ge(m_stacked, p.at(64, 32 * b + 32))
                            if not (p.first() and b == 0 and k < 2):
                                pe.wait_ge(e_exp, p.at(2 * NEU, NEU * b + k - 1))
                            c0 = R * S * b + 2 * S * h
                            if g < G:
                                ins = pe.matmul(pst[k % 2][:, 0:2 * S], T.ks_exp[p.par][0:MROWS, g, S * b:S * b + P],
                                                T.qs[p.par][0:MROWS, g, c0:c0 + 2 * S], start=True, stop=True)
                            else:
                                dst = pst[k % 2][0:G * REM, 0:2 * S]
                                for n, (lk, lq) in enumerate(((0, 0), (0, 1), (1, 0), (1, 1))):
                                    pe.matmul(dst, kr[p.par][b][:, lk].rearrange("p g t -> p (g t)"), qn[p.par][:, lq, c0:c0 + 2 * S],
                                              start=(n == 0), stop=False)
                                ins = pe.matmul(dst, T.rem_select[:], mt[:].rearrange("p r t -> p (r t)")[:, 2 * S * h:2 * S * h + 2 * S],
                                                start=False, stop=True)
                            ins.then_inc(e_done, 1)
                        elif kind[0:2] == "PV":
                            h = int(kind[2])
                            if kind.endswith("a"):
                                pe.wait_ge(e_exp, p.at(2 * NEU, NEU * b + (G + 1) * (h + 1)))
                                pe.wait_ge(taken["V"], p.at(2, b + 1))
                                if not (p.first() and b == 0 and h == 0):
                                    pe.wait_ge(oy_ready, p.at(4, 2 * b + h))
                            cols = slice(2 * S * h, 2 * S * h + 2 * S)
                            if kind[3:]:
                                parity = "ab".index(kind[3])
                                for q in range(G // 2):
                                    rows = slice(32 * q, 32 * q + 32)
                                    pe.matmul(pso[rows, 0:2 * S], T.v_pad[p.par][:, b, parity, rows], pt[b][:, 2 * q + parity, cols],
                                              start=(parity == 0), stop=False, skip_group_check=True)
                                for q in range(G // 2):
                                    rows = slice(32 * q, 32 * q + 32)
                                    pe.matmul(psd[rows, 0:2 * S], T.ones_half[:, parity, :], pt[b][:, 2 * q + parity, cols],
                                              start=(parity == 0), stop=False, skip_group_check=True)
                            else:
                                probs = pt[b][0:G * REM, G, cols]
                                pe.matmul(psd[:, 0:2 * S], T.rem_mask[0:G * REM, :], probs, start=False, stop=True,
                                          skip_group_check=True)
                                pe.matmul(pso[:, 0:2 * S], vr[p.par][b][0:G * REM, :], probs, start=False, stop=True,
                                          skip_group_check=True).then_inc(pv_done, 1)

                slots(pe, emit)

            @block.scalar
            def _(act):
                def emit(slot):
                    for kind, k, p, b in steps(slot):
                        if kind == "QK":
                            act.wait_ge(done["QK"], p.at(R + 1, k + 1))
                            if not (p.first() and k < 2):
                                act.wait_ge(q_hi, p.at(R + 1, k - 1))
                                act.wait_ge(q_lo, p.at(R + 1, k - 1))
                            act.activation(yq[k % 2 if p.par == 0 else (k + 1) % 2][:], gen[bank_of(kind, k)][:, 0:2 * S], ACT.Identity,
                                           bias=T.bq[:, k:k + 1], scale=T.f_qkv[:, 0:1]).then_inc(taken["QK"], 1)
                        elif kind == "QKMOVE":
                            act.wait_ge(taken["T1"], p.at(NT, NT))
                            if not p.first():
                                act.wait_ge(done["V"], p.at(2))
                            for bb in range(2):
                                src = xt[1][:, :, :, S * bb + P:S * bb + S].rearrange("p l f t -> p (l f) t").unsqueeze(2)
                                act.copy(xr[bb][:].rearrange("p x (g t) -> p x g t", g=G),
                                         src.broadcast_to([P, 2 * KB, G, REM])).then_inc(x_rem_ready, 1)
                        elif kind == "E":
                            h, g = E_UNITS[k]
                            act.wait_ge(e_done, p.at(2 * NEU, NEU * b + k + 1))
                            if k in (0, G + 1) and not p.first():
                                act.wait_ge(pv_done, p.at(4, 2 * b - 4 + h + 1))
                            rows = P if g < G else G * REM
                            act.activation(pt[b][0:rows, g, 2 * S * h:2 * S * h + 2 * S], pst[k % 2][0:rows, 0:2 * S], ACT.Exp,
                                           scale=T.f_exp[0:rows, 0:1]).then_inc(e_exp, 1)
                        elif kind in ("LN1P", "LN2P"):
                            w = int(kind[2])
                            act.wait_ge(yn_ready[w], p.at(NT, k + 1))
                            if not p.first():
                                act.wait_ge(done[f"T{w}"], p.at(NT, k - NT + 1))
                            act.copy(xp[w][:, k, 0, :], normed(w, k, p)).then_inc(hi_ready[w], 1)
                        elif kind in ("OUT0", "OUT1"):
                            k = int(kind[3])
                            act.wait_ge(oy_ready, p.at(4, 2 * b + k + 1))
                            if not (p.turn is None and p.off < 2) and b == 0 and k == 0:
                                act.wait_ge(done["O"], p.at(NT, -NT))
                            act.copy(ot[p.par][:, 0, 2 * k:2 * k + 2, S * b:S * b + S],
                                     oy[k][:].rearrange("p (r t) -> p r t", r=2)).then_inc(o_hi, 1)

                slots(act, emit)

            @block.gpsimd
            def _(pool):
                def emit(slot):
                    for kind, k, p, b in steps(slot):
                        if kind in ("LN1", "LN2"):
                            w = int(kind[2])
                            pool.wait_ge(ln_ve[w], p.at(1, 1))
                            pool.tensor_tensor(rs[w][:], ve[w][:], T.minus_half[0:TILE, 0:NT], ALU.pow).then_inc(ln_rs[w], 1)
                        elif kind in ("LN1P", "LN2P"):
                            w = int(kind[2])
                            pool.wait_ge(hi_ready[w], p.at(NT, k + 1))
                            pool.tensor_tensor(xp[w][:, k, 1, :], normed(w, k, p), xp[w][:, k, 0, :],
                                               ALU.subtract).then_inc(lo_ready[w], 1)
                        elif kind == "BF":
                            pool.wait_ge(yn_ready[2], p.at(NT, k + 1))
                            pool.tensor_tensor(h2[:, k, :], h2[:, k, :], T.bf[0:TILE], ALU.add).then_inc(bias_added[2], 1)
                        elif kind == "BO":
                            pool.wait_ge(h_reloaded, p.at(16 * H_PARTS, 16 * H_PARTS))
                            pool.tensor_tensor(hr[:, k, :], hr[:, k, :], T.bo[0:TILE], ALU.add).then_inc(bias_added[1], 1)
                        elif kind == "QKP":
                            pool.wait_ge(q_hi, p.at(R + 1, k + 1))
                            y = yq[k % 2 if p.par == 0 else (k + 1) % 2][:]
                            if k < R:
                                view = lambda l: qn[p.par][:, l, 0:QC].rearrange("p (b r t) -> p b r t", b=2, r=R)[:, :, k, :]
                                y = y.rearrange("p (b t) -> p b t", b=2)
                            else:
                                view = lambda l: qn[p.par][:, l, QC:]
                            pool.tensor_tensor(view(1), y, view(0), ALU.subtract).then_inc(q_lo, 1)
                        elif kind == "QKMOVE":
                            pool.wait_ge(q_lo, p.at(R + 1, R + 1))
                            if not (p.turn is None and p.off < 2):
                                pool.wait_ge(e_done, p.at(2 * NEU, -2 * NEU))
                            for bb in range(2):
                                for l in range(2):
                                    src = qn[p.par][:, l, QC + S * bb + P:QC + S * bb + S].unsqueeze(1).broadcast_to([P, G, REM])
                                    ins = pool.tensor_tensor(kr[p.par][bb][:, l], src, T.group_mask[:].unsqueeze(2).broadcast_to([P, G, REM]), ALU.mult)
                                ins.then_inc(k_rem_ready, 1)
                        elif kind in ("OUT0", "OUT1"):
                            k = int(kind[3])
                            pool.wait_ge(o_hi, p.at(4, 2 * b + k + 1))
                            view = lambda l: ot[p.par][:, l, 2 * k:2 * k + 2, S * b:S * b + S]
                            pool.tensor_tensor(view(1), oy[k][:].rearrange("p (r t) -> p r t", r=2), view(0), ALU.subtract).then_inc(o_lo, 1)

                slots(pool, emit)

            @block.vector
            def _(dve):
                def emit(slot):
                    for kind, k, p, b in steps(slot):
                        if kind in ("LN1S", "LN2S"):
                            w = int(kind[2])
                            src = hx if w == 1 else h2
                            if w == 1:
                                dve.wait_ge(h_loaded, p.at(16 * H_PARTS, 16 * H_PARTS))
                            else:
                                dve.wait_ge(taken["O"], p.at(NT, k + 1))
                            ins = dve.bn_stats(st[w][:, k, :], src[:, k, :])
                            if k == NT - 1:
                                ins.then_inc(ln_step[w], 1)
                        elif kind in ("LN1", "LN2"):
                            w = int(kind[2])
                            dve.wait_ge(ln_step[w], p.at(2, 1))
                            dve.sem_inc(ln_gate[w], 1)
                            for t in range(NT):
                                ins = dve.bn_aggr(mv[w][:, t, :], st[w][:, t, :])
                            ins.then_inc(ln_step[w], 1)
                            dve.wait_ge(ln_step[w], p.at(2, 2))
                            dve.tensor_scalar(ve[w][:], mv[w][:, :, 1], EPS, LN_SCALE ** -2, ALU.add, ALU.mult).then_inc(ln_ve[w], 1)
                        elif kind in ("LN1Y", "LN2Y"):
                            w = int(kind[2])
                            src = hx if w == 1 else h2
                            if k == 0:
                                dve.wait_ge(ln_rs[w], p.at(1, 1))
                            if w == 2 and not (p.first() and k < 2):
                                dve.wait_ge(lo_ready[w], p.at(NT, k - 1))
                            dve.tensor_scalar(normed(w, k, p), src[:, k, :], mv[w][:, k, 0:1], rs[w][:, k:k + 1],
                                              ALU.subtract, ALU.mult).then_inc(yn_ready[w], 1)
                        elif kind in ("T1", "T2"):
                            w = int(kind[1])
                            dve.wait_ge(done[kind], p.at(NT, k + 1))
                            if not p.first() and k == 0:
                                if w == 1:
                                    dve.wait_ge(done["V"], p.at(2))
                                else:
                                    dve.wait_ge(done["F"], p.at(NT))
                            dve.tensor_copy(xt[w][:, :, :, TILE * k:TILE * k + TILE],
                                            gen16(kind, k)[:, 0:2 * KB * TILE].rearrange("p (l f t) -> p l f t", l=2, f=KB)).then_inc(taken[kind], 1)
                        elif kind == "QKP":
                            dve.wait_ge(taken["QK"], p.at(R + 1, k + 1))
                            if k == 0 and not (p.turn is None and p.off < 2):
                                dve.wait_ge(spilled[p.par], p.half(16))
                                dve.wait_ge(e_done, p.at(2 * NEU, -2 * NEU))
                                dve.wait_ge(k_rem_ready, p.at(2, -2))
                            y = yq[k % 2 if p.par == 0 else (k + 1) % 2][:]
                            if k < R:
                                dst = qn[p.par][:, 0, 0:QC].rearrange("p (b r t) -> p b r t", b=2, r=R)[:, :, k, :]
                                y = y.rearrange("p (b t) -> p b t", b=2)
                            else:
                                dst = qn[p.par][:, 0, QC:]
                            dve.tensor_copy(dst, y).then_inc(q_hi, 1)
                        elif kind == "V":
                            dve.wait_ge(done["V"], p.at(2, k + 1))
                            if not (p.turn is None and p.off < 2):
                                dve.wait_ge(pv_done, p.at(4, 2 * k - 8 + 2))
                            bank = gen[bank_of(kind, k)]
                            for parity in range(2):
                                view = lambda ap: ap.rearrange("p (q e d) -> p q e d", e=2, d=HD)[:, :, parity, :]
                                dve.scalar_tensor_tensor(view(T.v_pad[p.par][:, k, parity, :]), view(bank[:, 0:P]), T.f_qkv[:, 0:1], view(T.bv[:]),
                                                         ALU.mult, ALU.add)
                            rr = slice(0, G * REM)
                            dve.scalar_tensor_tensor(vr[p.par][k][rr, :], bank[rr, P:2 * P], T.f_qkv[rr, 0:1], T.rem_mask[rr, :],
                                                     ALU.mult, ALU.mult).then_inc(v_rem, 1)
                            dve.wait_ge(v_rem, p.at(2, k + 1))
                            dve.tensor_tensor(vr[p.par][k][rr, :], vr[p.par][k][rr, :], T.bv_rem[rr, :], ALU.add).then_inc(taken["V"], 1)
                        elif kind == "O":
                            dve.wait_ge(done["O"], p.at(NT, k + 1))
                            dve.wait_ge(bias_added[1], p.at(NT, k + 1))
                            if not p.first():
                                dve.wait_ge(out_stored[k], p.at(16))
                            dve.scalar_tensor_tensor(h2[:, k, :], gen[bank_of(kind, k)][0:TILE, :], T.f_out[0:TILE, 0:1], hr[:, k, :],
                                                     ALU.mult, ALU.add).then_inc(taken["O"], 1)
                        elif kind == "F":
                            dve.wait_ge(done["F"], p.at(NT, k + 1))
                            dve.wait_ge(bias_added[2], p.at(NT, k + 1))
                            dve.scalar_tensor_tensor(h2[:, k, :], gen[bank_of(kind, k)][0:TILE, :], T.f_ffn[0:TILE, 0:1], h2[:, k, :],
                                                     ALU.mult, ALU.add).then_inc(taken["F"], 1)
                        elif kind == "S":
                            what, tiles = S_UNITS[k]
                            dve.wait_ge(s_done, p.at(2 * NSU, NSU * b + k + 1))
                            n = len(tiles)
                            j0 = 3 * k if what == "main" else R * G + tiles[0]
                            dve.tensor_reduce(mx[:].rearrange("p r g -> p (r g)")[:, j0:j0 + n],
                                              psc[k % 2][:, 0:S * n].rearrange("p (j t) -> p j t", j=n), AX.X, ALU.max).then_inc(s_max, 1)
                        elif kind == "MP":
                            dve.wait_ge(s_max, p.at(2 * NSU, NSU * (b + 1)))
                            if not (p.first() and b == 0):
                                dve.wait_ge(done["MT"], p.at(2, b))
                            dve.tensor_scalar(mp[:, :, 0, :], mx[:], -1.0 / NEG, None, ALU.mult).then_inc(mp_step, 1)
                            dve.wait_ge(mp_step, p.at(4, 2 * b + 1))
                            dve.scalar_tensor_tensor(mp[:, :, 1, :], mx[:], -1.0 / NEG, mp[:, :, 0, :], ALU.mult, ALU.subtract).then_inc(mp_step, 1)
                        elif kind == "MT":
                            dve.wait_ge(done["MT"], p.at(2, b + 1))
                            if not (p.first() and b == 0):
                                dve.wait_ge(m_stacked, p.at(64, 32 * b))
                                dve.wait_ge(e_done, p.at(2 * NEU, NEU * b - NEU + G + 2))
                            ps = gen16(kind, b)
                            dve.tensor_copy(mt[:, :, 0:P], ps[0:2 * G, 0:P * R].rearrange("p (r t) -> p r t", r=R))
                            dve.tensor_copy(mt[:, :, P:S], ps[0:2 * G, P * R:P * R + P].rearrange("p (r t) -> p r t", r=R)[:, :, 32 - REM:32]).then_inc(taken["MT"], 1)
                        elif kind in ("PV0", "PV1"):
                            k = int(kind[2])
                            dve.wait_ge(pv_done, p.at(4, 2 * b + k + 1))
                            dve.reciprocal(dinv[k][:, 0:TILE], psd[:, 0:TILE])
                        elif kind in ("REC0", "REC1"):
                            k = int(kind[3])
                            dve.reciprocal(dinv[k][:, TILE:2 * TILE], psd[:, TILE:2 * TILE])
                        elif kind in ("INV0", "INV1"):
                            k = int(kind[3])
                            dve.reciprocal(dinv[k][:, 2 * TILE:2 * S], psd[:, 2 * TILE:2 * S]).then_inc(d_inv, 1)
                            dve.wait_ge(d_inv, p.at(4, 2 * b + k + 1))
                            if not (p.first() and b == 0):
                                dve.wait_ge(o_lo, p.at(4, 2 * b + k - 1))
                            dve.tensor_tensor(oy[k][:], pso[:, 0:2 * S], dinv[k][:], ALU.mult).then_inc(oy_ready, 1)

                slots(dve, emit)


class Tiles:
    pass


def fusion_kernel(nc, c_t, txt, a_t, b_t, log_dt, wq_t, bqk_t, bv_row, wo_t, b_out, wf_t, b_ffn, out):
    hk = nc.dram_tensor("kernel_tokens", (B, TK, D), F32).ap()
    with ExitStack() as ctx:
        sb, _, _ = sliding(nc, ctx)
        T = Tiles()
        T.ident = sb("ident", [P, P], F32)
        T.ident16 = sb("ident16", [P, P], F16)
        T.ones128 = sb("ones128", [P, P], F32)
        T.sign = sb("sign", [P, 1], F32)
        T.group_mask = sb("group_mask", [P, G], F32)
        T.rem_mask = sb("rem_mask", [P, P], F32)
        T.rem_select = sb("rem_select", [2 * G, G * REM], F16)
        T.ones_half = sb("ones_half", [P, 2, 32], F32)
        T.minus_half = sb("minus_half", [P, NT], F32)
        T.wq = sb("wq_t", [P, 2, KB, 6, P], F16)
        T.wo = sb("wo_t", [P, 2, R, D], F16)
        T.wf = sb("wf_t", [P, KB, D], F16)
        T.bq = sb("bq", [P, R + 1], F32)
        T.bv = sb("bv", [P, P], F32)
        T.bv_rem = sb("bv_rem", [P, P], F32)
        T.bo = sb("bo", [P, D], F32)
        T.bf = sb("bf", [P, D], F32)
        T.c_wq, T.c_wo, T.c_b = sb("c_wq", [P, 1], F32), sb("c_wo", [P, 1], F32), sb("c_b", [P, 1], F32)
        T.f_qkv, T.f_out = sb("f_qkv", [P, 1], F32), sb("f_out", [P, 1], F32)
        T.f_exp, T.f_ffn = sb("f_exp", [P, 1], F32), sb("f_ffn", [P, 1], F32)
        T.qs = [sb(f"q_stack{i}", [MROWS, G, 2 * R * S], F16) for i in range(2)]
        T.ks_max = [sb(f"k_stack_max{i}", [MROWS, G, 2 * S], F16) for i in range(2)]
        T.ks_exp = [sb(f"k_stack_exp{i}", [MROWS, G, 2 * S], F16) for i in range(2)]
        T.v_pad = [sb(f"v_pad{i}", [P, 2, 2, P], F32) for i in range(2)]
        state_space_kernel(nc, T, hk, c_t, a_t, b_t, log_dt, wq_t, bqk_t, bv_row, wo_t, b_out, wf_t, b_ffn)
        blocks(nc, T, txt, hk, out)


def laid_out(i):
    w, b = i["L0_attn_w_qkv"], i["L0_attn_b_qkv"]
    wq = w[:D].reshape(G, R, HD, D).transpose(3, 1, 0, 2).reshape(D, R * P)
    bq = b[:D].reshape(G, R, HD).transpose(0, 2, 1).reshape(P, R)
    return {
        "c_t": i["x"].transpose(3, 2, 1, 0).reshape(2 * NS, NS, B),
        "txt": i["txt"],
        "a_t": i["L0_tok_A"].transpose(1, 3, 0, 2),
        "b_t": i["L0_tok_B"].transpose(2, 1, 0).reshape(2 * NS, NS),
        "log_dt": i["L0_tok_log_dt"].reshape(NS),
        "wq_t": np.concatenate([wq, w[D:].T], axis=1),
        "bqk_t": np.concatenate([bq, b[D:D + P].reshape(P, 1)], axis=1),
        "bv": b[D + P:],
        "wo_t": i["L0_attn_w_out"].reshape(D, G, R, HD).transpose(1, 3, 2, 0).reshape(P, R, D),
        "b_out": i["L0_attn_b_out"],
        "wf_t": i["L0_ffn_weight"].T,
        "b_ffn": i["L0_ffn_bias"],
    }


def kernel(**inputs):
    import concourse.bacc as _bacc
    from concourse.bass_utils import run_bass_kernel_spmd as _run

    nc = _bacc.Bacc("TRN2", target_bir_lowering=False, num_devices=1)
    arrays, args = {}, []
    for name, a in laid_out({k: np.asarray(v) for k, v in inputs.items()}).items():
        arrays[f"in_{name}"] = np.ascontiguousarray(a)
        args.append(nc.dram_tensor(f"in_{name}", a.shape, mybir.dt.from_np(a.dtype), kind="ExternalInput").ap())
    args.append(nc.dram_tensor("out_h", (B, S, D), F32, kind="ExternalOutput").ap())
    fusion_kernel(nc, *args)
    return _run(nc, [arrays], core_ids=[0]).results[0]["out_h"]
```
